# Optimizing a Trainium2 kernel written in Bass

```python
import numpy as np
import jax
import jax.numpy as jnp

def _softmax(x, axis=-1):
    return jax.nn.softmax(x, axis=axis)

def _gelu(x):
    return jax.nn.gelu(x, approximate=True)

def _silu(x):
    return jax.nn.silu(x)

def _sigmoid(x):
    return jax.nn.sigmoid(x)

def _layernorm(x, axis=-1, eps=1e-05):
    m = jnp.mean(x, axis=axis, keepdims=True)
    v = jnp.var(x, axis=axis, keepdims=True)
    return (x - m) / jnp.sqrt(v + eps)

def _scatter_add(tgt, idx, src, axis=0):
    return tgt.at[idx].add(src)

def _segment_sum(src, seg, n):
    return jax.ops.segment_sum(src, seg, n)
kernel_name = 'mk_early_fusion_embed_d1_tok_img256_r4_ad0d34'

def setup_inputs(seed: int=0):
    np.random.seed(seed)
    _w = jnp.asarray

    def _rec_inputs():
        import jax
        import jax.numpy as jnp
        _rk = jax.random.key(seed)
        x = -0.000125008 + 0.999885 * jax.random.normal(jax.random.fold_in(_rk, 1), (8, 64, 128, 128), jnp.float32)
        x_txt = jax.random.randint(jax.random.fold_in(_rk, 51), (8, 77), 0, 3, jnp.int32)
        itok_BS_0_4999 = jax.random.randint(jax.random.fold_in(_rk, 71), (8, 77), 0, 1250, jnp.int32)
        fside_BS_outcomes = jax.random.uniform(jax.random.fold_in(_rk, 72), (8, 77), jnp.float32, 0.0, 0.999996)
        fside_BS_delta_ts = jax.random.uniform(jax.random.fold_in(_rk, 73), (8, 77), jnp.float32, 0.0, 0.999995)
        return (x, x_txt, itok_BS_0_4999, fside_BS_outcomes, fside_BS_delta_ts)
    x, x_txt, itok_BS_0_4999, fside_BS_outcomes, fside_BS_delta_ts = _rec_inputs()

    def _L0_tok_setup():
        import jax, jax.numpy as jnp
        import numpy as np
        D_MODEL = 64
        NHEAD = 8
        DS = 4
        OFFSET_SCALE = 4.0

        def bilinear_sample(fm, pts):
            B, C, H, W = fm.shape
            x = (pts[..., 0] + 1.0) * 0.5 * (W - 1)
            y = (pts[..., 1] + 1.0) * 0.5 * (H - 1)
            x0 = jnp.clip(jnp.floor(x), 0.0, W - 2)
            y0 = jnp.clip(jnp.floor(y), 0.0, H - 2)
            wx = jnp.clip(x - x0, 0.0, 1.0)
            wy = jnp.clip(y - y0, 0.0, 1.0)
            x0i = x0.astype(jnp.int32)
            y0i = y0.astype(jnp.int32)
            fm2 = fm.reshape(B, C, H * W)
            N, P = (pts.shape[1], pts.shape[2])

            def gather(yi, xi):
                idx = (yi * W + xi).reshape(B, N * P)
                g = jnp.take_along_axis(fm2, idx[:, None, :], axis=2)
                return g.reshape(B, C, N, P)
            v00 = gather(y0i, x0i)
            v01 = gather(y0i, x0i + 1)
            v10 = gather(y0i + 1, x0i)
            v11 = gather(y0i + 1, x0i + 1)
            wx_ = wx[:, None]
            wy_ = wy[:, None]
            out = v00 * (1 - wx_) * (1 - wy_) + v01 * wx_ * (1 - wy_) + v10 * (1 - wx_) * wy_ + v11 * wx_ * wy_
            return jnp.moveaxis(out, 1, -1)

        def layer_norm(x, g, b, eps=1e-05):
            mu = jnp.mean(x, axis=-1, keepdims=True)
            var = jnp.var(x, axis=-1, keepdims=True)
            return (x - mu) * jax.lax.rsqrt(var + eps) * g + b

        def reference_points(B, H, W):
            yc = jnp.linspace(-1.0, 1.0, H // DS)
            xc = jnp.linspace(-1.0, 1.0, W // DS)
            yg, xg = jnp.meshgrid(yc, xc, indexing='ij')
            ref = jnp.stack([xg.reshape(-1), yg.reshape(-1)], axis=-1)
            return jnp.broadcast_to(ref[None], (B,) + ref.shape)
        key = jax.random.key(seed)
        ks = jax.random.split(key, 6)
        B, C, H, W = (8, D_MODEL, 128, 128)
        s = 0.05
        return {'feature_map': jax.random.normal(ks[0], (B, C, H, W), jnp.float32), 'W_q': jax.random.normal(ks[1], (C, C), jnp.float32) * s, 'W_k': jax.random.normal(ks[2], (C, C), jnp.float32) * s, 'W_v': jax.random.normal(ks[3], (C, C), jnp.float32) * s, 'W_o1': jax.random.normal(ks[4], (C, C // DS), jnp.float32) * s, 'b_o1': jnp.zeros((C // DS,), jnp.float32), 'ln_g': jnp.ones((C // DS,), jnp.float32), 'ln_b': jnp.zeros((C // DS,), jnp.float32), 'W_o2': jax.random.normal(ks[5], (C // DS, NHEAD * 2), jnp.float32) * s, 'b_o2': jnp.zeros((NHEAD * 2,), jnp.float32)}
    _L0_tok_all = _L0_tok_setup()
    _L0_tok_in = {k: v for k, v in _L0_tok_all.items() if k in ('W_q', 'W_k', 'W_v', 'W_o1', 'b_o1', 'ln_g', 'ln_b', 'W_o2', 'b_o2')}
    del _L0_tok_all

    def _L0_txt_setup():
        import jax, jax.numpy as jnp
        import numpy as np
        LN_EPS = 1e-05
        key = jax.random.key(seed)
        ks = jax.random.split(key, 10)
        B, L, d, d_type = (64, 512, 64, 16)
        inp = {'event_types': jax.random.randint(ks[0], (B, L), 0, 3), 'entity_indices': jax.random.randint(ks[1], (B, L), 0, 1250), 'outcomes': jax.random.uniform(ks[2], (B, L), dtype=jnp.float32), 'delta_ts': jax.random.uniform(ks[3], (B, L), dtype=jnp.float32), 'h_qa': jax.random.normal(ks[4], (5000, d), dtype=jnp.float32), 'h_v': jax.random.normal(ks[5], (2000, d), dtype=jnp.float32), 'h_r': jax.random.normal(ks[6], (1250, d), dtype=jnp.float32), 'E_type_w': jax.random.normal(ks[7], (3, d_type), dtype=jnp.float32), 'W_o': jnp.ones((1,), jnp.float32), 'W_delta': jnp.ones((1,), jnp.float32), 'W_proj_w': jax.random.normal(ks[8], (d, d + d_type + 2), dtype=jnp.float32) * (1.0 / np.sqrt(d + d_type + 2)), 'W_proj_b': jnp.zeros((d,), jnp.float32), 'ln_gamma': jnp.ones((d,), jnp.float32), 'ln_beta': jnp.zeros((d,), jnp.float32)}
        return inp
    _L0_txt_all = _L0_txt_setup()
    _L0_txt_in = {k: v for k, v in _L0_txt_all.items() if k in ('h_qa', 'h_v', 'h_r', 'E_type_w', 'W_o', 'W_delta', 'W_proj_w', 'W_proj_b', 'ln_gamma', 'ln_beta')}
    del _L0_txt_all

    def _L0_attn_setup():
        import jax, jax.numpy as jnp
        import numpy as np
        D = 64
        L = 2
        B, S = (8, 1024)
        LR = 0.001
        WD = 0.01
        MAX_ALR = 0.1
        EPS = 1e-08

        def _lmm(Ws, bs, x):
            for i in range(L):
                x = x + jax.nn.silu(x @ Ws[i] + bs[i])
            return x

        def _reference_tuple_inner(x, Wk, Wq, Wv, Wlr, blr, Ws, bs):
            keys = x @ Wk
            queries = x @ Wq
            values = x @ Wv
            alr = (jax.nn.sigmoid(x @ Wlr + blr) * MAX_ALR).reshape(-1)

            def loss_fn(params):
                Ws_, bs_ = params
                preds = _lmm(Ws_, bs_, keys).reshape(-1, D)
                tgt = values.reshape(-1, D)
                per_tok = jnp.mean((preds - tgt) ** 2, axis=-1)
                return jnp.sum(per_tok * alr)
            gWs, gbs = jax.grad(loss_fn)((Ws, bs))

            def adamw_step(p, g):
                return p * (1.0 - LR * WD) - LR * g / (jnp.sqrt(g * g) + EPS)
            nWs = adamw_step(Ws, gWs)
            nbs = adamw_step(bs, gbs)
            retrieved = _lmm(nWs, nbs, queries)
            return (retrieved, -gWs, -gbs)
        key = jax.random.key(seed)
        ks = jax.random.split(key, 9)
        scale = 0.05
        return {'x': jax.random.normal(ks[0], (B, S, D), dtype=jnp.float32), 'Wk': jax.random.normal(ks[1], (D, D), dtype=jnp.float32) * scale, 'Wq': jax.random.normal(ks[2], (D, D), dtype=jnp.float32) * scale, 'Wv': jax.random.normal(ks[3], (D, D), dtype=jnp.float32) * scale, 'Wlr': jax.random.normal(ks[4], (D, 1), dtype=jnp.float32) * scale, 'blr': jnp.zeros((1,), dtype=jnp.float32), 'Ws': jax.random.normal(ks[5], (L, D, D), dtype=jnp.float32) * scale, 'bs': jnp.zeros((L, D), dtype=jnp.float32)}
    _L0_attn_all = _L0_attn_setup()
    _L0_attn_in = {k: v for k, v in _L0_attn_all.items() if k in ('Wk', 'Wq', 'Wv', 'Wlr', 'blr', 'Ws', 'bs')}
    del _L0_attn_all

    def _L0_ffn_setup():
        import jax, jax.numpy as jnp
        import numpy as np
        E, D, H, TOP_K = (6, 64, 64, 2)
        ROUTER_H = D // 2
        key = jax.random.key(seed)
        ks = jax.random.split(key, 12)
        s = 1.0 / np.sqrt(D)
        sh = 1.0 / np.sqrt(H)
        sr = 1.0 / np.sqrt(ROUTER_H)
        return {'features': jax.random.normal(ks[0], (8, 1024, D), dtype=jnp.float32), 'router_w1': jax.random.uniform(ks[1], (D, ROUTER_H), jnp.float32, -s, s), 'router_b1': jnp.zeros((ROUTER_H,), jnp.float32), 'router_w2': jax.random.uniform(ks[2], (ROUTER_H, E), jnp.float32, -sr, sr), 'router_b2': jnp.zeros((E,), jnp.float32), 'expert_w1': jax.random.uniform(ks[3], (E, D, H), jnp.float32, -s, s), 'expert_b1': jnp.zeros((E, H), jnp.float32), 'expert_w2': jax.random.uniform(ks[4], (E, H, H), jnp.float32, -sh, sh), 'expert_b2': jnp.zeros((E, H), jnp.float32), 'expert_w3': jax.random.uniform(ks[5], (E, H, D), jnp.float32, -sh, sh), 'expert_b3': jnp.zeros((E, D), jnp.float32)}
    _L0_ffn_all = _L0_ffn_setup()
    _L0_ffn_in = {k: v for k, v in _L0_ffn_all.items() if k in ('router_w1', 'router_b1', 'router_w2', 'router_b2', 'expert_w1', 'expert_b1', 'expert_w2', 'expert_b2', 'expert_w3', 'expert_b3')}
    del _L0_ffn_all
    return {'x': x, 'x_txt': x_txt, 'itok_BS_0_4999': itok_BS_0_4999, 'fside_BS_outcomes': fside_BS_outcomes, 'fside_BS_delta_ts': fside_BS_delta_ts, 'L0_tok_W_q': _L0_tok_in['W_q'], 'L0_tok_W_k': _L0_tok_in['W_k'], 'L0_tok_W_v': _L0_tok_in['W_v'], 'L0_tok_W_o1': _L0_tok_in['W_o1'], 'L0_tok_b_o1': _L0_tok_in['b_o1'], 'L0_tok_ln_g': _L0_tok_in['ln_g'], 'L0_tok_ln_b': _L0_tok_in['ln_b'], 'L0_tok_W_o2': _L0_tok_in['W_o2'], 'L0_tok_b_o2': _L0_tok_in['b_o2'], 'L0_txt_h_qa': _L0_txt_in['h_qa'], 'L0_txt_h_v': _L0_txt_in['h_v'], 'L0_txt_h_r': _L0_txt_in['h_r'], 'L0_txt_E_type_w': _L0_txt_in['E_type_w'], 'L0_txt_W_o': _L0_txt_in['W_o'], 'L0_txt_W_delta': _L0_txt_in['W_delta'], 'L0_txt_W_proj_w': _L0_txt_in['W_proj_w'], 'L0_txt_W_proj_b': _L0_txt_in['W_proj_b'], 'L0_txt_ln_gamma': _L0_txt_in['ln_gamma'], 'L0_txt_ln_beta': _L0_txt_in['ln_beta'], 'L0_attn_Wk': _L0_attn_in['Wk'], 'L0_attn_Wq': _L0_attn_in['Wq'], 'L0_attn_Wv': _L0_attn_in['Wv'], 'L0_attn_Wlr': _L0_attn_in['Wlr'], 'L0_attn_blr': _L0_attn_in['blr'], 'L0_attn_Ws': _L0_attn_in['Ws'], 'L0_attn_bs': _L0_attn_in['bs'], 'L0_ffn_router_w1': _L0_ffn_in['router_w1'], 'L0_ffn_router_b1': _L0_ffn_in['router_b1'], 'L0_ffn_router_w2': _L0_ffn_in['router_w2'], 'L0_ffn_router_b2': _L0_ffn_in['router_b2'], 'L0_ffn_expert_w1': _L0_ffn_in['expert_w1'], 'L0_ffn_expert_b1': _L0_ffn_in['expert_b1'], 'L0_ffn_expert_w2': _L0_ffn_in['expert_w2'], 'L0_ffn_expert_b2': _L0_ffn_in['expert_b2'], 'L0_ffn_expert_w3': _L0_ffn_in['expert_w3'], 'L0_ffn_expert_b3': _L0_ffn_in['expert_b3']}

def reference(x, x_txt, itok_BS_0_4999, fside_BS_outcomes, fside_BS_delta_ts, L0_tok_W_q, L0_tok_W_k, L0_tok_W_v, L0_tok_W_o1, L0_tok_b_o1, L0_tok_ln_g, L0_tok_ln_b, L0_tok_W_o2, L0_tok_b_o2, L0_txt_h_qa, L0_txt_h_v, L0_txt_h_r, L0_txt_E_type_w, L0_txt_W_o, L0_txt_W_delta, L0_txt_W_proj_w, L0_txt_W_proj_b, L0_txt_ln_gamma, L0_txt_ln_beta, L0_attn_Wk, L0_attn_Wq, L0_attn_Wv, L0_attn_Wlr, L0_attn_blr, L0_attn_Ws, L0_attn_bs, L0_ffn_router_w1, L0_ffn_router_b1, L0_ffn_router_w2, L0_ffn_router_b2, L0_ffn_expert_w1, L0_ffn_expert_b1, L0_ffn_expert_w2, L0_ffn_expert_b2, L0_ffn_expert_w3, L0_ffn_expert_b3):
    import jax
    import jax.numpy as jnp

    def _L0_tok_ref(feature_map, W_q, W_k, W_v, W_o1, b_o1, ln_g, ln_b, W_o2, b_o2):
        import jax, jax.numpy as jnp
        import numpy as np
        D_MODEL = 64
        NHEAD = 8
        DS = 4
        OFFSET_SCALE = 4.0

        def bilinear_sample(fm, pts):
            B, C, H, W = fm.shape
            x = (pts[..., 0] + 1.0) * 0.5 * (W - 1)
            y = (pts[..., 1] + 1.0) * 0.5 * (H - 1)
            x0 = jnp.clip(jnp.floor(x), 0.0, W - 2)
            y0 = jnp.clip(jnp.floor(y), 0.0, H - 2)
            wx = jnp.clip(x - x0, 0.0, 1.0)
            wy = jnp.clip(y - y0, 0.0, 1.0)
            x0i = x0.astype(jnp.int32)
            y0i = y0.astype(jnp.int32)
            fm2 = fm.reshape(B, C, H * W)
            N, P = (pts.shape[1], pts.shape[2])

            def gather(yi, xi):
                idx = (yi * W + xi).reshape(B, N * P)
                g = jnp.take_along_axis(fm2, idx[:, None, :], axis=2)
                return g.reshape(B, C, N, P)
            v00 = gather(y0i, x0i)
            v01 = gather(y0i, x0i + 1)
            v10 = gather(y0i + 1, x0i)
            v11 = gather(y0i + 1, x0i + 1)
            wx_ = wx[:, None]
            wy_ = wy[:, None]
            out = v00 * (1 - wx_) * (1 - wy_) + v01 * wx_ * (1 - wy_) + v10 * (1 - wx_) * wy_ + v11 * wx_ * wy_
            return jnp.moveaxis(out, 1, -1)

        def layer_norm(x, g, b, eps=1e-05):
            mu = jnp.mean(x, axis=-1, keepdims=True)
            var = jnp.var(x, axis=-1, keepdims=True)
            return (x - mu) * jax.lax.rsqrt(var + eps) * g + b

        def reference_points(B, H, W):
            yc = jnp.linspace(-1.0, 1.0, H // DS)
            xc = jnp.linspace(-1.0, 1.0, W // DS)
            yg, xg = jnp.meshgrid(yc, xc, indexing='ij')
            ref = jnp.stack([xg.reshape(-1), yg.reshape(-1)], axis=-1)
            return jnp.broadcast_to(ref[None], (B,) + ref.shape)
        B, C, H, W = feature_map.shape
        dh = C // NHEAD
        ref = reference_points(B, H, W)
        Nq = ref.shape[1]
        q_feat = bilinear_sample(feature_map, ref[:, :, None, :])[:, :, 0]
        queries = q_feat @ W_q.T
        h = jax.nn.gelu(layer_norm(q_feat @ W_o1 + b_o1, ln_g, ln_b))
        off = (h @ W_o2 + b_o2).reshape(B, Nq, NHEAD, 2) * OFFSET_SCALE
        scale = jnp.array([2.0 / (W - 1), 2.0 / (H - 1)], jnp.float32)
        sampling_points = ref[:, :, None, :] + off * scale
        sampled = bilinear_sample(feature_map, sampling_points)
        keys = jnp.einsum('bnpc,dc->bnpd', sampled, W_k)
        values = jnp.einsum('bnpc,dc->bnpd', sampled, W_v)
        q = queries.reshape(B, Nq, NHEAD, dh)
        k = keys.reshape(B, Nq, NHEAD, NHEAD, dh)
        v = values.reshape(B, Nq, NHEAD, NHEAD, dh)
        scores = jnp.einsum('bnhd,bnphd->bnhp', q, k) / jnp.sqrt(jnp.float32(dh))
        attn = jax.nn.softmax(scores, axis=-1)
        out = jnp.einsum('bnhp,bnphd->bnhd', attn, v).reshape(B, Nq, C)
        return out

    def _L0_txt_ref(event_types, entity_indices, outcomes, delta_ts, h_qa, h_v, h_r, E_type_w, W_o, W_delta, W_proj_w, W_proj_b, ln_gamma, ln_beta):
        import jax, jax.numpy as jnp
        import numpy as np
        LN_EPS = 1e-05
        d = h_qa.shape[1]
        max_e = max(h_qa.shape[0], h_v.shape[0], h_r.shape[0])
        pad = lambda h: jnp.pad(h, ((0, max_e - h.shape[0]), (0, 0)))
        entity_table = jnp.stack([pad(h_qa), pad(h_v), pad(h_r)], axis=0)
        emb = entity_table[event_types, entity_indices]
        type_emb = E_type_w[event_types]
        outcome_feat = (W_o * outcomes)[..., None]
        delta_feat = (W_delta * delta_ts)[..., None]
        concat = jnp.concatenate([emb, type_emb, outcome_feat, delta_feat], axis=-1)
        proj = jnp.einsum('bli,oi->blo', concat, W_proj_w) + W_proj_b
        mu = jnp.mean(proj, axis=-1, keepdims=True)
        var = jnp.var(proj, axis=-1, keepdims=True)
        return (proj - mu) * jax.lax.rsqrt(var + LN_EPS) * ln_gamma + ln_beta

    def _L0_attn_ref(x, Wk, Wq, Wv, Wlr, blr, Ws, bs):
        import jax, jax.numpy as jnp
        import numpy as np
        D = 64
        L = 2
        B, S = (8, 1024)
        LR = 0.001
        WD = 0.01
        MAX_ALR = 0.1
        EPS = 1e-08

        def _lmm(Ws, bs, x):
            for i in range(L):
                x = x + jax.nn.silu(x @ Ws[i] + bs[i])
            return x

        def _reference_tuple_inner(x, Wk, Wq, Wv, Wlr, blr, Ws, bs):
            keys = x @ Wk
            queries = x @ Wq
            values = x @ Wv
            alr = (jax.nn.sigmoid(x @ Wlr + blr) * MAX_ALR).reshape(-1)

            def loss_fn(params):
                Ws_, bs_ = params
                preds = _lmm(Ws_, bs_, keys).reshape(-1, D)
                tgt = values.reshape(-1, D)
                per_tok = jnp.mean((preds - tgt) ** 2, axis=-1)
                return jnp.sum(per_tok * alr)
            gWs, gbs = jax.grad(loss_fn)((Ws, bs))

            def adamw_step(p, g):
                return p * (1.0 - LR * WD) - LR * g / (jnp.sqrt(g * g) + EPS)
            nWs = adamw_step(Ws, gWs)
            nbs = adamw_step(bs, gbs)
            retrieved = _lmm(nWs, nbs, queries)
            return (retrieved, -gWs, -gbs)
        return _reference_tuple_inner(x, Wk, Wq, Wv, Wlr, blr, Ws, bs)[0]

    def _L0_ffn_ref(features, router_w1, router_b1, router_w2, router_b2, expert_w1, expert_b1, expert_w2, expert_b2, expert_w3, expert_b3):
        import jax, jax.numpy as jnp
        import numpy as np
        E, D, H, TOP_K = (6, 64, 64, 2)
        ROUTER_H = D // 2
        rh = jax.nn.relu(features @ router_w1 + router_b1)
        expert_logits = jax.nn.softmax(rh @ router_w2 + router_b2, axis=-1)
        top_w, top_i = jax.lax.top_k(expert_logits, TOP_K)
        routing_weights = jax.nn.softmax(top_w, axis=-1)
        h1 = jax.nn.relu(jnp.einsum('bsd,edh->bseh', features, expert_w1) + expert_b1)
        h2 = jax.nn.relu(jnp.einsum('bseh,ehf->bsef', h1, expert_w2) + expert_b2)
        expert_out = jnp.einsum('bsef,efo->bseo', h2, expert_w3) + expert_b3
        sel = jnp.take_along_axis(expert_out, top_i[:, :, :, None], axis=2)
        combined = jnp.sum(sel * routing_weights[..., None], axis=2)
        return combined
    h = _L0_tok_ref(x, L0_tok_W_q, L0_tok_W_k, L0_tok_W_v, L0_tok_W_o1, L0_tok_b_o1, L0_tok_ln_g, L0_tok_ln_b, L0_tok_W_o2, L0_tok_b_o2)
    h = jnp.concatenate([h, _L0_txt_ref(x_txt, itok_BS_0_4999, fside_BS_outcomes, fside_BS_delta_ts, L0_txt_h_qa, L0_txt_h_v, L0_txt_h_r, L0_txt_E_type_w, L0_txt_W_o, L0_txt_W_delta, L0_txt_W_proj_w, L0_txt_W_proj_b, L0_txt_ln_gamma, L0_txt_ln_beta)], axis=1)
    h = h + _L0_attn_ref(_layernorm(h, axis=-1), L0_attn_Wk, L0_attn_Wq, L0_attn_Wv, L0_attn_Wlr, L0_attn_blr, L0_attn_Ws, L0_attn_bs)
    h = h + _L0_ffn_ref(_layernorm(h, axis=-1), L0_ffn_router_w1, L0_ffn_router_b1, L0_ffn_router_w2, L0_ffn_router_b2, L0_ffn_expert_w1, L0_ffn_expert_b1, L0_ffn_expert_w2, L0_ffn_expert_b2, L0_ffn_expert_w3, L0_ffn_expert_b3)
    return h

_drawn_inputs = setup_inputs


def setup_inputs(seed=0):
    import zlib

    import numpy as np

    out = dict(_drawn_inputs(seed))
    spreads = {'L0_tok_b_o1': (0.0, 0.1),
     'L0_tok_ln_g': (1.0, 0.2),
     'L0_tok_ln_b': (0.0, 0.1),
     'L0_tok_b_o2': (0.0, 0.1),
     'L0_txt_W_proj_b': (0.0, 0.1),
     'L0_txt_ln_gamma': (1.0, 0.2),
     'L0_txt_ln_beta': (0.0, 0.1),
     'L0_attn_bs': (0.0, 0.1),
     'L0_ffn_router_b1': (0.0, 0.1),
     'L0_ffn_router_b2': (0.0, 0.1),
     'L0_ffn_expert_b1': (0.0, 0.386),
     'L0_ffn_expert_b2': (0.0, 0.1),
     'L0_ffn_expert_b3': (0.0, 0.1)}
    factors = {'fside_BS_outcomes': 3.367,
     'fside_BS_delta_ts': 2.965,
     'L0_attn_Wk': 4.133,
     'L0_attn_Wv': 4.314,
     'L0_attn_Wlr': 8.0}
    for name, (base, spread) in spreads.items():
        noise = np.random.default_rng([zlib.crc32(name.encode()), seed]).standard_normal(out[name].shape)
        drawn = base * np.exp(spread * noise) if base else spread * noise
        out[name] = jnp.asarray(drawn.astype(out[name].dtype))
    for name, factor in factors.items():
        out[name] = (out[name] * factor).astype(out[name].dtype)
    return out
```

```python
from contextlib import ExitStack

import concourse.bass as bass
import numpy as np
from concourse import mybir

F32 = mybir.dt.float32
BF16 = mybir.dt.bfloat16
I32 = mybir.dt.int32
U32 = mybir.dt.uint32
ALU = mybir.AluOpType
ACT = mybir.ActivationFunctionType
AX = mybir.AxisListType.X

P = 128
IMAGES, C, H, W = 8, 64, 128, 128
GRID = H // 4
CHUNKS = 8
POINTS = 8
HEADS = 8
DH = C // HEADS
HID = C // 4
SLOTS = IMAGES + 1
COLS = CHUNKS * C
PAIRS = CHUNKS // 2
TXT_B, TXT_L = 8, 77
TXT_CHUNKS = 5
TXT_ROWS = 5000
TYPE_DIM = 16
CAT = C + TYPE_DIM + 3
EXPERTS = 6
RH = 32
EPAIRS = EXPERTS // 2
LR, WD, MAX_ALR = 0.001, 0.01, 0.1
LN_EPS = 1e-5
RING = 4
PRIME = 8
GELU_C, GELU_A = 0.7978845608028654, 0.044715
ROUND = 8388608.0
RSQRT_SEED = 1597463007.0

EARLY = [("ident", 128), ("wq2", 128), ("wo1", 2 * HID), ("wo2", 128), ("wk2", 128), ("wv2", 128),
         ("bo1", 128), ("lng", 128), ("lnb", 128), ("bo2", 128), ("refw", 32), ("refpx", 16)]
LATE = [("mk", 128), ("mv", 128), ("mlr", 128), ("mq", 128), ("mw1", 128), ("mw2", 128), ("mw2t", 128),
        ("mkrep", 128), ("par", 2 * C + 2), ("blr", 1), ("stack", 128), ("gmask", 256), ("lossw", 512),
        ("rw1", 2 * RH), ("rb1", 1), ("rw2", 2 * EXPERTS), ("rb2", CHUNKS * EXPERTS), ("first", CHUNKS * EXPERTS),
        ("ew1", EPAIRS * 128), ("eb1", EPAIRS), ("ew2", EPAIRS * 128), ("eb2", EPAIRS), ("ew3", EPAIRS * C),
        ("eb3", COLS), ("sel", EPAIRS * 128), ("txtw", C), ("txtg", C), ("txtb", C), ("txts", 2),
        ("outc", TXT_CHUNKS), ("dt", TXT_CHUNKS)]


def columns(entries):
    at, where = 0, {}
    for name, n in entries:
        where[name] = (at, n)
        at += n
    return where, at


def build(nc, x_pairs, x_ref, early, late, txt_idx, txt_table, type_table, out):
    with ExitStack() as ctx:
        def sb(name, shape, dt=F32):
            return ctx.enter_context(nc.sbuf_tensor(name, shape, dt))

        def bank(name):
            return ctx.enter_context(nc.psum_tensor(name, [P, 512], F32))

        sems = {}

        def sem(name):
            if name not in sems:
                sems[name] = ctx.enter_context(nc.semaphore(name))
            return sems[name]

        w_early = sb("w_early", [P, columns(EARLY)[1]])
        w_late = sb("w_late", [P, columns(LATE)[1]])

        def par(name, rows=P):
            tile, entries = (w_early, EARLY) if name in dict(EARLY) else (w_late, LATE)
            at, n = columns(entries)[0][name]
            return tile[0:rows, at:at + n]

        txt_i = sb("txt_i", [P, 2 * TXT_CHUNKS], I32)
        txt_row = sb("txt_row", [P, TXT_CHUNKS], I32)
        txt_cat = sb("txt_cat", [P, TXT_CHUNKS, CAT])
        xref = sb("xref", [P, 4, CHUNKS, C])
        xrefw = sb("xrefw", [P, 4, CHUNKS, C])
        qfT = sb("qfT", [P, COLS])
        qry_next = sb("qry_next", [P, COLS])
        qry = sb("qry", [P, COLS])
        oh = sb("oh", [P, 128])
        ot = sb("ot", [P, 128])
        otanh = sb("otanh", [P, 128])
        ogT = sb("ogT", [P, 128])
        refb = sb("refb", [P, CHUNKS, POINTS, 2])
        px = sb("px", [P, CHUNKS * POINTS, 2])
        corner = sb("corner", [P, CHUNKS * POINTS, 2])
        frac = sb("frac", [P, 2, CHUNKS * POINTS, 2])
        wts_next = sb("wts_next", [P, CHUNKS * POINTS, 2, 2])
        wts = sb("wts", [P, CHUNKS, POINTS * 4])
        row_next = sb("row_next", [P, CHUNKS * POINTS])
        row_base = sb("row_base", [P, 1])
        row = sb("row", [P, CHUNKS * POINTS], I32)
        stat = sb("stat", [P, 8, CHUNKS])
        seed = sb("seed", [P, CHUNKS], I32)
        gath = sb("gath", [P, RING, POINTS, 4 * C])
        gathw = sb("gathw", [P, 2, 4, POINTS * C])
        smpT = sb("smpT", [P, 2, 512])
        qk = sb("qk", [P, POINTS * C])
        score = sb("score", [P, 2, POINTS, HEADS])
        prob = sb("prob", [P, 2, POINTS, HEADS])
        av = sb("av", [P, POINTS * C])
        ha = sb("ha", [P, 4, HEADS])
        ho = sb("ho", [P, C])
        h_all = sb("h_all", [P, SLOTS, COLS])
        q_all = sb("q_all", [P, SLOTS, COLS])
        T = {n: sb("t_" + n, [P, COLS]) for n in
             "u uT k0 sg1 s1 k1 d1 sg2 s2 d2 res lr dp dz2 dz1 k1t dz2t dz1t sq".split()}
        ones = sb("ones", [P, 1])
        grad = sb("grad", [P, 258])
        grad2 = sb("grad2", [P, 258])
        gpar = sb("gpar", [P, 2 * C + 2])
        gtmp = sb("gtmp", [P, 2 * C + 2])
        npar = sb("npar", [P, 2 * C + 2])
        nw = sb("nw", [P, 2, 128])
        hnb = sb("hnb", [P, 2])
        hb = sb("hb", [P, 3])

        ident_b = sb("ident_b", [P, P], BF16)
        sel_b = sb("sel_b", [18, EPAIRS * P], BF16)
        ring = gath[:, :, :, :].rearrange("p r (a b) (m c) -> p r a (b m c)", a=4, m=1)
        h2, u2T = ring[:, 0, 0:2, :], ring[:, 0, 2:4, :]
        e1, e2 = ring[:, 1, 0:2, :], ring[:, 1, 2:4, :]
        e2r, y = ring[:, 2, 0:2, :], ring[:, 2, 2:4, :]
        rhT = sb("rhT", [2 * RH, COLS])
        NE = CHUNKS * EXPERTS
        lg = sb("lg", [P, NE])
        pe_ = sb("pe_", [P, NE])
        prb = sb("prb", [P, NE])
        hot = sb("hot", [P, 2, NE])
        key = sb("key", [P, NE])
        top = sb("top", [P, 8, CHUNKS])
        rout = sb("rout", [P, NE])
        rest = sb("rest", [P, NE])
        rout3 = sb("rout3", [P, CHUNKS, 3 * EXPERTS], BF16)
        rout3T = sb("rout3T", [3 * EXPERTS, 2, 2 * COLS], BF16)
        routT = sb("routT", [NE, 2, P])

        b_smp = bank("b_smp")
        b_k = [bank("b_k0"), bank("b_k1")]
        b_v = [bank("b_v0"), bank("b_v1")]
        b_g = bank("b_g")
        b_aux = [bank("b_aux0"), bank("b_aux1")]

        params_in, txt_in, late_in, ready = sem("params_in"), sem("txt_in"), sem("late_in"), sem("ready")
        ref_in, ref_used = sem("ref_in"), sem("ref_used")
        gathered = [sem(f"gathered{k}") for k in range(RING)]
        txt_gathered, rows_txt = sem("txt_gathered"), sem("rows_txt")
        rows_a, rows_b = sem("rows_a"), sem("rows_b")
        issued_a, issued_b = sem("issued_a"), sem("issued_b")
        weighed, summed, smp_copied, kv_made = sem("weighed"), sem("summed"), sem("smp_copied"), sem("kv_made")
        scored, exped, attended = sem("scored"), sem("exped"), sem("attended")
        qry_moved = sem("qry_moved")
        s_dve, s_act = sem("s_dve"), sem("s_act")

        def made(name):
            return sem("made_" + name)

        def read(name):
            return sem("read_" + name)

        AUX = ["qf", "qry", "off1", "u", "k0", "z1", "og", "off2", "z2", "v", "lr", "dk", "q", "k1t", "dz2t", "dz1t"]
        AUX_Q = [n for n in AUX if n in ("qf", "qry", "off1", "og", "off2")]
        AUX_B = [n for n in AUX if n not in AUX_Q]
        bank_of = {n: b_aux[k % 2] for k, n in enumerate(AUX)}


        UNITS = 2 * EPAIRS
        CAUX = ["r3", "r48", "z1", "z2", "rt", "u2", "rh", "lg"]
        cbank = {n: b_aux[k % 2] for k, n in enumerate(CAUX)}
        e1_bank, e2_bank, r_bank, y_bank = b_k, b_v, b_smp, b_g
        l1_made, e1_done, l2_made, e2_done = sem("l1_made"), sem("e1_done"), sem("l2_made"), sem("e2_done")
        r_made, e2r_done, l3_made = sem("r_made"), sem("e2r_done"), sem("l3_made")
        y_done = sem("y_done")
        stored = [sem("stored0"), sem("stored1")]
        updated = sem("updated")
        PHASE3_SEMS = ([l1_made, e1_done, l2_made, e2_done, r_made, e2r_done, l3_made, y_done]
                       + [sem(f"{w}_c_{n}") for w in ("made", "read") for n in CAUX]
                       + [sem(n) for n in ("c_k1_done", "c_res_done", "c_sg1_done", "c_sg2_done", "c_lgx_done",
                                           "c_exp_done", "c_gap_done", "c_gape_done", "c_rout_done")])
        cmade = lambda n: sem(f"made_c_{n}")
        cread = lambda n: sem(f"read_c_{n}")

        def slots_loop(eng, one_slot):
            with eng.Fori(0, IMAGES // 2) as j:
                for parity in range(2):
                    one_slot(j * 2 + parity, parity, True)
            one_slot(IMAGES, 0, False)

        def phase3_sync(sp):
            with sp.Fori(0, IMAGES // 2) as j:
                for parity in range(2):
                    s = j * 2 + parity
                    sp.wait_ge(y_done, s + (PRIME + 1))
                    sp.dma_start(out[bass.ds(s, 1)].rearrange("a p n -> (a p) n"), y[:, parity, :]
                                 ).then_inc(stored[parity], 16)
            sp.wait_ge(y_done, PRIME + IMAGES + 1)
            sp.dma_start(out[IMAGES], y[:, 0, :]).then_inc(stored[0], 16)
            sp.wait_ge(stored[0], 16 * (IMAGES // 2 + 2))
            sp.wait_ge(stored[1], 16 * (IMAGES // 2 + 1))

        def phase23_tensor(pe):
            ident = par("ident")

            pe.wait_ge(sem("grad_masked"), 1)
            pe.matmul(b_aux[0][:, 0:258], par("stack"), grad[:, :], start=True, stop=True).then_inc(made("gsum"), 1)
            pe.wait_ge(sem("ghat_done"), 1)
            pe.matmul(b_aux[1][:, 0:C], par("mkrep", C), gtmp[0:C, 0:C], start=True, stop=True
                      ).then_inc(made("gw1"), 1)
            pe.wait_ge(updated, 1)

            def c1(name, slot, n, pred):
                if pred is not None:
                    k = CAUX.index(name)
                    pe.wait_ge(cread(CAUX[k - 2]), pred)
                dst = cbank[name]
                if name == "z1":
                    last = pe.matmul(dst[:, :], nw[:, 0, :], q_all[:, bass.ds(slot, 1), :].rearrange("p a n -> p (a n)"),
                                     start=True, stop=True)
                elif name == "z2":
                    pe.wait_ge(sem("c_k1_done"), n)
                    last = pe.matmul(dst[:, :], nw[:, 1, :], T["k1"][:, :], start=True, stop=True)
                elif name == "rt":
                    pe.wait_ge(sem("c_res_done"), n)
                    for j in range(PAIRS):
                        last = pe.transpose(dst[:, j * 128:(j + 1) * 128], T["res"][:, j * 128:(j + 1) * 128], ident)
                elif name == "u2":
                    pe.wait_ge(sem("normed"), n + SLOTS)
                    for j in range(PAIRS):
                        last = pe.transpose(dst[:, j * 128:(j + 1) * 128], T["u"][:, j * 128:(j + 1) * 128], ident)
                return last.then_inc(cmade(name), 1)

            def c1_router(name, parity, n, pred):
                k = CAUX.index(name)
                pe.wait_ge(cread(CAUX[k - 2]), pred)
                dst = cbank[name]
                if name == "rh":
                    pe.wait_ge(cread("u2"), n)
                    last = pe.matmul(dst[0:2 * RH, :], par("rw1"), u2T[:, parity, :], start=True, stop=True)
                elif name == "lg":
                    pe.wait_ge(cread("rh"), n)
                    for j in range(PAIRS):
                        last = pe.matmul(dst[:, j * 12:(j + 1) * 12], rhT[:, j * 128:(j + 1) * 128],
                                         par("rw2", 2 * RH), start=True, stop=True)
                elif name == "r3":
                    pe.wait_ge(sem("c_rout_done"), n)
                    for c in range(CHUNKS):
                        at = (c % 2) * COLS + (c // 2) * 128
                        last = pe.transpose(dst[:, :].bitcast(BF16)[0:18, at:at + 128], rout3[:, c, :], ident_b[:, :])
                elif name == "r48":
                    pe.sem_inc(sem("r48_started"), 1)
                    last = pe.transpose(dst[0:NE, 0:P], rout[:, :], ident)
                last.then_inc(cmade(name), 1)

            def one_slot(s, parity, more):
                c0, c1n = s + (PRIME + 1), s + (PRIME + 2)
                units = s * UNITS + PRIME

                def l1(m):
                    p, b = m // 2, m % 2
                    rows = slice(b * C, (b + 1) * C)
                    if m == 0:
                        pe.wait_ge(cread("u2"), c0)
                    pe.wait_ge(e1_done, units + (m - 1))
                    pe.matmul(e1_bank[m % 2][:, :], par("ew1")[rows, p * P:(p + 1) * P], u2T[rows, parity, :],
                              start=True, stop=True).then_inc(l1_made, 1)

                def l2(m):
                    p, b = m // 2, m % 2
                    pe.wait_ge(e1_done, units + (m + 1))
                    pe.wait_ge(e2_done, units + (m - 1))
                    pe.matmul(e2_bank[m % 2][:, :], par("ew2")[:, p * P:(p + 1) * P], e1[:, m % 2, :],
                              start=True, stop=True).then_inc(l2_made, 1)
                    if m == 0:
                        pe.wait_ge(cread("r3"), c0)
                    pe.wait_ge(e2r_done, units + m)
                    pe.matmul(r_bank[:, :], sel_b[:, p * P:(p + 1) * P], rout3T[:, parity, b * COLS:(b + 1) * COLS],
                              start=True, stop=True).then_inc(r_made, 1)

                def l3(m):
                    p, b = m // 2, m % 2
                    if m == 0:
                        pe.wait_ge(cread("r48"), c0)
                        pe.wait_ge(y_done, s + PRIME)
                        pe.matmul(y_bank[:, :], routT[:, parity, :], par("eb3", NE), start=True, stop=False,
                                  skip_group_check=True)
                    pe.wait_ge(e2r_done, units + (m + 1))
                    for j in range(PAIRS):
                        at = (2 * j + b) * C
                        last = pe.matmul(y_bank[:, at:at + C], e2r[:, m % 2, j * 128:(j + 1) * 128],
                                         par("ew3")[:, p * C:(p + 1) * C], start=False, stop=(m == UNITS - 1),
                                         skip_group_check=True)
                    last.then_inc(l3_made, 1)

                for m in range(UNITS + 2):
                    if m < UNITS:
                        l1(m)
                    if 1 <= m <= UNITS:
                        l2(m - 1)
                    if m >= 2:
                        l3(m - 2)
                    if m == 0:
                        c1_router("r3", parity, c0, c0)
                        c1_router("r48", parity, c0, c0)
                    if more:
                        if m == 0:
                            c1("z1", s + 1, c1n, c0)
                        if m == 1:
                            c1("z2", s + 1, c1n, c0)
                        if m == 2:
                            c1("rt", s + 1, c1n, c1n)
                        if m == 4:
                            c1("u2", s + 1, c1n, c1n)
                        if m == 5:
                            c1_router("rh", 1 - parity, c1n, c1n)
                        if m == 6:
                            c1_router("lg", 1 - parity, c1n, c1n)

            for name in ("z1", "z2", "rt", "u2"):
                c1(name, 0, PRIME + 1, None if name in ("z1", "z2") else PRIME + 1)
            for name in ("rh", "lg"):
                c1_router(name, 0, PRIME + 1, PRIME + 1)
            slots_loop(pe, one_slot)

        def phase3_scalar(act, chain, link, copy, sigmoid):
            act.wait_ge(updated, 1)

            def c1(r, parity, n):
                if r == 0:
                    act.wait_ge(cmade("z1"), n)
                    sigmoid(T["sg1"][:, :], cbank["z1"][:, :], hnb[:, 0:1]).then_inc(sem("c_sg1_done"), 1)
                if r == 1:
                    act.wait_ge(cmade("z2"), n)
                    sigmoid(T["sg2"][:, :], cbank["z2"][:, :], hnb[:, 1:2]).then_inc(sem("c_sg2_done"), 1)
                if r == 3:
                    act.wait_ge(sem("mean_done"), n + SLOTS)
                    for c in range(CHUNKS):
                        ins = act.activation(T["sq"][:, c * C:(c + 1) * C], h2[:, parity, c * C:(c + 1) * C], ACT.Square,
                                             bias=stat[:, 1, c:c + 1], accum_out=stat[:, 2, c:c + 1])
                    ins.then_inc(sem("var_done"), 1)
                if r == 4:
                    act.wait_ge(cmade("u2"), n)
                    copy(u2T[:, parity, :], cbank["u2"][:, :]).then_inc(cread("u2"), 1)
                if r == 5:
                    act.wait_ge(cmade("rh"), n)
                    act.activation(rhT[:, :], cbank["rh"][0:2 * RH, :], ACT.Relu, bias=par("rb1", 2 * RH)
                                   ).then_inc(cread("rh"), 1)
                if r == 7:
                    act.wait_ge(sem("c_lgx_done"), n)
                    act.activation(pe_[:, :], lg[:, :], ACT.Exp).then_inc(sem("c_exp_done"), 1)
                    act.wait_ge(sem("c_gap_done"), n)
                    act.activation(top[:, 5, :], top[:, 4, :], ACT.Exp).then_inc(sem("c_gape_done"), 1)

            def one_slot(s, parity, more):
                act.sem_clear(s_act)
                chain[0] = 0
                c0, c1n = s + (PRIME + 1), s + (PRIME + 2)
                units = s * UNITS + PRIME

                for m in range(UNITS + 2):
                    if m < UNITS:
                        act.wait_ge(l1_made, units + (m + 1))
                        act.wait_ge(l2_made, units + (m - 1))
                        act.activation(e1[:, m % 2, :], e1_bank[m % 2][:, :], ACT.Relu,
                                       bias=par("eb1")[:, m // 2:m // 2 + 1]).then_inc(e1_done, 1)
                    if 1 <= m <= UNITS:
                        k = m - 1
                        act.wait_ge(l2_made, units + (k + 1))
                        act.wait_ge(e2r_done, units + (k - 1))
                        act.activation(e2[:, k % 2, :], e2_bank[k % 2][:, :], ACT.Relu,
                                       bias=par("eb2")[:, k // 2:k // 2 + 1]).then_inc(e2_done, 1)
                    if m == 0:
                        act.wait_ge(cmade("r3"), c0)
                        copy(rout3T[:, parity, :], cbank["r3"][:, :].bitcast(BF16)[0:18, :]).then_inc(cread("r3"), 1)
                        act.wait_ge(cmade("r48"), c0)
                        copy(routT[:, parity, :], cbank["r48"][0:NE, 0:P]).then_inc(cread("r48"), 1)
                    if more:
                        c1(m, 1 - parity, c1n)

            act.sem_clear(s_act)
            chain[0] = 0
            for r in range(UNITS + 2):
                c1(r, 0, PRIME + 1)
            slots_loop(act, one_slot)

        def phase23_vector(dve, steps, step, sync, link, bc, chunked, rsqrt, normalise):
            dve.wait_ge(sem("grads_added"), PRIME + SLOTS)
            step(dve.tensor_tensor(grad[:, 0:256], b_g[:, 0:256], par("gmask"), ALU.mult))
            step(dve.tensor_copy(ident_b[:, :], par("ident")))
            step(dve.tensor_copy(sel_b[:, :], par("sel", 18)))
            step(dve.memset(nw[:, :, :], 0.0))
            sync()
            dve.tensor_copy(grad[:, 256:258], b_g[:, 256:258]).then_inc(sem("grad_masked"), 1)
            dve.wait_ge(made("gsum"), 1)
            link(dve.tensor_copy(grad2[:, :], b_aux[0][:, 0:258]))
            dve.tensor_tensor(gtmp[:, 0:C], grad2[:, 128:128 + C], grad2[:, 128 + C:256], ALU.add
                              ).then_inc(sem("ghat_done"), 1)
            step(dve.tensor_tensor(gpar[:, C:2 * C], grad2[:, 0:C], grad2[:, C:2 * C], ALU.add))
            step(dve.tensor_copy(gpar[:, 2 * C:], grad2[:, 256:258]))
            dve.wait_ge(made("gw1"), 1)
            link(dve.tensor_copy(gpar[:, 0:C], b_aux[1][:, 0:C]))
            link(dve.scalar_tensor_tensor(gtmp[:, :], gpar[:, :], -1.0, gpar[:, :], ALU.mult, ALU.max))
            link(dve.tensor_scalar(gtmp[:, :], gtmp[:, :], 1e-8, None, ALU.add))
            link(dve.reciprocal(gtmp[:, :], gtmp[:, :]))
            link(dve.tensor_tensor(gtmp[:, :], gtmp[:, :], gpar[:, :], ALU.mult))
            link(dve.tensor_scalar(npar[:, :], par("par"), 1.0 - LR * WD, None, ALU.mult))
            link(dve.scalar_tensor_tensor(npar[:, :], gtmp[:, :], -LR, npar[:, :], ALU.mult, ALU.add))
            for k in range(2):
                for b in range(2):
                    half = slice(b * C, (b + 1) * C)
                    step(dve.tensor_copy(nw[half, k, half], npar[half, k * C:(k + 1) * C]))
            sync()
            dve.tensor_scalar(hnb[:, :], npar[:, 2 * C:], 0.5, None, ALU.mult).then_inc(updated, 1)

            v3 = lambda ap: ap.rearrange("p (n e) -> p n e", n=CHUNKS)

            def pick(which, probs, best):
                link(dve.tensor_reduce(best, v3(probs), AX, ALU.max))
                link(dve.tensor_tensor(v3(key[:, :]), v3(probs), bc(best, EXPERTS), ALU.is_equal))
                link(dve.tensor_tensor(key[:, :], key[:, :], par("first"), ALU.mult))
                link(dve.tensor_reduce(top[:, 7, :], v3(key[:, :]), AX, ALU.max))
                link(dve.tensor_tensor(v3(hot[:, which, :]), v3(key[:, :]), bc(top[:, 7, :], EXPERTS), ALU.is_equal))

            def c1(r, slot, parity, n):
                if r == 0:
                    dve.wait_ge(sem("c_sg1_done"), n)
                    dve.scalar_tensor_tensor(T["s1"][:, :], cbank["z1"][:, :], npar[:, 2 * C:2 * C + 1],
                                             T["sg1"][:, :], ALU.add, ALU.mult).then_inc(cread("z1"), 1)
                    dve.wait_ge(cread("z1"), n)
                    dve.tensor_tensor(T["k1"][:, :], q_all[:, bass.ds(slot, 1), :].rearrange("p a n -> p (a n)"),
                                      T["s1"][:, :], ALU.add).then_inc(sem("c_k1_done"), 1)
                if r == 1:
                    dve.wait_ge(sem("c_sg2_done"), n)
                    dve.scalar_tensor_tensor(T["s2"][:, :], cbank["z2"][:, :], npar[:, 2 * C + 1:2 * C + 2],
                                             T["sg2"][:, :], ALU.add, ALU.mult).then_inc(cread("z2"), 1)
                    dve.wait_ge(cread("z2"), n)
                    dve.tensor_tensor(T["res"][:, :], T["k1"][:, :], T["s2"][:, :], ALU.add
                                      ).then_inc(sem("c_res_done"), 1)
                if r == 2:
                    dve.wait_ge(cmade("rt"), n)
                    dve.tensor_tensor(h2[:, parity, :], h_all[:, bass.ds(slot, 1), :].rearrange("p a n -> p (a n)"),
                                      cbank["rt"][:, :], ALU.add).then_inc(cread("rt"), 1)
                    dve.wait_ge(cread("rt"), n)
                    link(dve.tensor_reduce(stat[:, 0, :], chunked(h2[:, parity, :]), AX, ALU.add))
                    dve.tensor_scalar(stat[:, 1, :], stat[:, 0, :], -1.0 / C, None, ALU.mult
                                      ).then_inc(sem("mean_done"), 1)
                if r == 3:
                    normalise(T["u"], h2[:, parity, :], lambda name: n + SLOTS)
                if r == 6:
                    dve.wait_ge(cmade("lg"), n)
                    dve.tensor_tensor(lg[:, :], cbank["lg"][:, 0:NE], par("rb2"), ALU.add).then_inc(cread("lg"), 1)
                    dve.wait_ge(cread("lg"), n)
                    link(dve.tensor_reduce(top[:, 0, :], v3(lg[:, :]), AX, ALU.max))
                    dve.tensor_tensor(v3(lg[:, :]), v3(lg[:, :]), bc(top[:, 0, :], EXPERTS), ALU.subtract
                                      ).then_inc(sem("c_lgx_done"), 1)
                if r == 7:
                    dve.wait_ge(sem("c_exp_done"), n)
                    link(dve.tensor_reduce(top[:, 0, :], v3(pe_[:, :]), AX, ALU.add))
                    link(dve.reciprocal(top[:, 1, :], top[:, 0, :]))
                    link(dve.tensor_tensor(v3(prb[:, :]), v3(pe_[:, :]), bc(top[:, 1, :], EXPERTS), ALU.mult))
                    pick(0, prb[:, :], top[:, 2, :])
                    link(dve.scalar_tensor_tensor(prb[:, :], hot[:, 0, :], -4.0, prb[:, :], ALU.mult, ALU.add))
                    pick(1, prb[:, :], top[:, 3, :])
                    dve.tensor_tensor(top[:, 4, :], top[:, 3, :], top[:, 2, :], ALU.subtract
                                      ).then_inc(sem("c_gap_done"), 1)
                    dve.wait_ge(sem("c_gape_done"), n)
                    link(dve.tensor_scalar(top[:, 6, :], top[:, 5, :], 1.0, None, ALU.add))
                    link(dve.reciprocal(top[:, 6, :], top[:, 6, :]))
                    link(dve.tensor_tensor(top[:, 5, :], top[:, 5, :], top[:, 6, :], ALU.mult))
                    step(dve.tensor_tensor(v3(hot[:, 0, :]), v3(hot[:, 0, :]), bc(top[:, 6, :], EXPERTS), ALU.mult))
                    link(dve.tensor_tensor(v3(hot[:, 1, :]), v3(hot[:, 1, :]), bc(top[:, 5, :], EXPERTS), ALU.mult))
                    link(dve.tensor_tensor(rout[:, :], hot[:, 0, :], hot[:, 1, :], ALU.add))
                    part = lambda k: rout3[:, :, k * EXPERTS:(k + 1) * EXPERTS]
                    link(dve.tensor_copy(part(0), v3(rout[:, :])))
                    link(dve.tensor_tensor(v3(rest[:, :]), v3(rout[:, :]), part(0), ALU.subtract))
                    link(dve.tensor_copy(part(1), v3(rest[:, :])))
                    dve.tensor_tensor(part(2), v3(rest[:, :]), part(1), ALU.subtract).then_inc(sem("c_rout_done"), 1)

            def one_slot(s, parity, more):
                dve.sem_clear(s_dve)
                steps[0] = 0
                c1n = s + (PRIME + 2)
                units = s * UNITS + PRIME
                for m in range(UNITS + 2):
                    if 1 <= m <= UNITS:
                        k = m - 1
                        dve.wait_ge(e2_done, units + (k + 1))
                        dve.wait_ge(r_made, units + (k + 1))
                        dve.wait_ge(l3_made, units + (k - 1))
                        dve.tensor_tensor(e2r[:, k % 2, :], e2[:, k % 2, :], r_bank[:, :], ALU.mult
                                          ).then_inc(e2r_done, 1)
                    if more:
                        c1(m, s + 1, 1 - parity, c1n)
                dve.wait_ge(l3_made, units + UNITS)
                dve.wait_ge(stored[parity], (s - parity) * 8 + 16)
                dve.tensor_tensor(y[:, parity, :], h2[:, parity, :], y_bank[:, :], ALU.add).then_inc(y_done, 1)
                sync()

            for r in range(UNITS + 2):
                c1(r, 0, 0, PRIME + 1)
            slots_loop(dve, one_slot)

        block = ctx.enter_context(nc.Block())

        @block.sync
        def _(sp):
            sp.dma_start(w_early[:, :], early).then_inc(params_in, 16)
            sp.dma_start(xref[:, :, :, :].rearrange("p k n c -> p (k n c)"), x_ref[0]).then_inc(ref_in, 16)
            sp.dma_start(txt_i[:, :], txt_idx).then_inc(txt_in, 16)
            sp.dma_start(w_late[:, :], late).then_inc(late_in, 16)
            for s in ([ref_used, rows_a, rows_b, issued_a, issued_b, weighed, summed, smp_copied, kv_made, scored,
                       exped, attended, qry_moved] + [made(n) for n in AUX] + [read(n) for n in AUX]
                      + [sem(n) for n in ("gelu_arg", "gelu_tanh", "gelu_done", "mean_done", "var_done", "normed",
                                          "sg1_done", "k1_done", "sg2_done", "dz2_done", "grads_added")]):
                sp.sem_inc(s, PRIME)
            for s in PHASE3_SEMS:
                sp.sem_inc(s, PRIME)
            for s in stored:
                sp.sem_inc(s, 16)
            with sp.Fori(0, IMAGES) as i:
                sp.wait_ge(ref_used, i + (PRIME + 1))
                sp.dma_start(xref[:, :, :, :].rearrange("p k n c -> p (k n c)"),
                             x_ref[bass.ds(i + 1, 1)].rearrange("a p n -> (a p) n")).then_inc(ref_in, 16)
            phase3_sync(sp)

        @block.gpsimd
        def _(pool):
            def gather(dst, table, index, done, index_used=None):
                pool.indirect_dma_start(dst, None, table, bass.IndirectOffsetOnAxis(ap=index.bitcast(U32), axis=0),
                                        engine_sem=index_used).then_inc(done, 16)

            pool.wait_ge(txt_in, 16)
            pool.wait_ge(rows_txt, 1)
            for j in range(TXT_CHUNKS):
                gather(txt_cat[:, j, 0:C], txt_table, txt_row[:, j:j + 1], txt_gathered)
                gather(txt_cat[:, j, C:C + TYPE_DIM], type_table, txt_i[:, j:j + 1], txt_gathered)
            with pool.Fori(0, IMAGES) as i:
                for c in range(CHUNKS):
                    if c == 0:
                        pool.wait_ge(rows_a, i + (PRIME + 1))
                    if c == CHUNKS // 2:
                        pool.wait_ge(rows_b, i + (PRIME + 1))
                    pool.wait_ge(weighed, i * CHUNKS + (PRIME + c - RING + 1))
                    pool.sem_inc(sem("slots_taken"), 1)
                    for n in range(POINTS):
                        k = c * POINTS + n
                        used = {(3, 7): issued_a, (7, 7): issued_b}.get((c, n))
                        gather(gath[:, c % RING, n, :], x_pairs, row[:, k:k + 1], gathered[c % RING], used)

        @block.tensor
        def _(pe):
            ident = par("ident")

            def transpose4(dst, src, width=128):
                for j in range(PAIRS):
                    last = pe.transpose(dst[:, j * 128:(j + 1) * 128], src[:, j * width:j * width + 128], ident)
                return last

            def bank_free(name, order, now, before):
                k = order.index(name)
                if k >= 2:
                    pe.wait_ge(read(order[k - 2]), now(order[k - 2]))
                elif before is not None:
                    pe.wait_ge(read(order[k - 2]), before(order[k - 2]))

            def points_stage(name, order, now, before):
                def mm(dst, lhsT, rhs, **kw):
                    return pe.matmul(dst, lhsT, rhs, start=True, stop=True, **kw)
                bank_free(name, order, now, before)
                dst = bank_of[name]
                if name == "qf":
                    pe.wait_ge(ref_used, now("ref"))
                    for j in range(PAIRS):
                        for k in range(4):
                            last = pe.matmul(dst[:, j * 128:(j + 1) * 128],
                                             xrefw[:, k, 2 * j:2 * j + 2, :].rearrange("p a c -> p (a c)"),
                                             ident, is_transpose=True, start=(k == 0), stop=(k == 3))
                elif name == "qry":
                    pe.wait_ge(read("qf"), now("qf"))
                    for j in range(PAIRS):
                        last = mm(dst[:, j * 128:(j + 1) * 128], qfT[:, j * 128:(j + 1) * 128], par("wq2"))
                elif name == "off1":
                    for j in range(PAIRS):
                        last = mm(dst[:, j * 32:(j + 1) * 32], qfT[:, j * 128:(j + 1) * 128], par("wo1"))
                elif name == "og":
                    pe.wait_ge(sem("gelu_done"), now("g"))
                    last = pe.transpose(dst[:, 0:128], oh[:, :], ident)
                elif name == "off2":
                    pe.wait_ge(read("og"), now("og"))
                    last = mm(dst[:, 0:128], ogT[:, :], par("wo2"))
                last.then_inc(made(name), 1)

            def mlp_stage(name, order, now, before):
                def mm(w, src):
                    return pe.matmul(dst[:, :], w, src[:, :], start=True, stop=True)
                bank_free(name, order, now, before)
                dst = bank_of[name]
                if name == "u":
                    pe.wait_ge(sem("normed"), now("n"))
                    last = transpose4(dst, T["u"])
                elif name == "k0":
                    pe.wait_ge(read("u"), now("u"))
                    last = mm(par("mk"), T["uT"])
                elif name == "z1":
                    pe.wait_ge(read("k0"), now("k0"))
                    last = mm(par("mw1"), T["k0"])
                elif name == "z2":
                    pe.wait_ge(sem("k1_done"), now("k1"))
                    last = mm(par("mw2"), T["k1"])
                elif name == "v":
                    last = mm(par("mv"), T["uT"])
                elif name == "lr":
                    last = mm(par("mlr"), T["uT"])
                elif name == "dk":
                    pe.wait_ge(sem("dz2_done"), now("dz2"))
                    last = mm(par("mw2t"), T["dz2"])
                elif name == "q":
                    last = mm(par("mq"), T["uT"])
                elif name == "k1t":
                    last = transpose4(dst, T["k1"])
                elif name == "dz2t":
                    last = transpose4(dst, T["dz2"])
                elif name == "dz1t":
                    pe.wait_ge(read("dk"), now("dk"))
                    last = transpose4(dst, T["dz1"])
                last.then_inc(made(name), 1)

            def gradients(now):
                for j in range(PAIRS):
                    cols = slice(j * 128, (j + 1) * 128)
                    kw = dict(start=False, stop=False, skip_group_check=True)
                    if j == 0:
                        pe.wait_ge(read("dz2t"), now("dz2t"))
                    pe.matmul(b_g[:, 0:128], T["k1t"][:, cols], T["dz2t"][:, cols], **kw)
                    pe.matmul(b_g[:, 257:258], T["dz2t"][:, cols], ones[:, :], **kw)
                    if j == 0:
                        pe.wait_ge(read("dz1t"), now("dz1t"))
                    pe.matmul(b_g[:, 128:256], T["u"][:, cols], T["dz1t"][:, cols], **kw)
                    last = pe.matmul(b_g[:, 256:257], T["dz1t"][:, cols], ones[:, :], **kw)
                last.then_inc(sem("grads_added"), 1)

            pe.wait_ge(params_in, 16)
            first = lambda name: PRIME + 1
            for name in AUX_Q:
                points_stage(name, AUX_Q, first, None)
            pe.wait_ge(late_in, 16)
            pe.wait_ge(sem("txt_cat_done"), 1)
            pe.wait_ge(txt_gathered, 32 * TXT_CHUNKS)
            pe.wait_ge(read("og"), PRIME + 1)
            pe.wait_ge(read("off2"), PRIME + 1)
            for j in range(TXT_CHUNKS):
                last = pe.transpose(b_aux[j // 4][0:CAT, (j % 4) * 128:(j % 4) * 128 + 128], txt_cat[:, j, :], ident)
            last.then_inc(made("txt_t"), 1)
            pe.wait_ge(read("txt_t"), 1)
            for j in range(TXT_CHUNKS):
                last = pe.matmul(b_aux[0][:, j * C:(j + 1) * C], T["s1" if j == 4 else "k1"][0:CAT, (j % 4) * 128:(j % 4) * 128 + 128],
                                 par("txtw", CAT), start=True, stop=True)
            last.then_inc(made("txt_p"), 1)
            pe.wait_ge(read("txt_p"), 1)
            pe.matmul(b_g[:, 0:258], T["dz1"][:, 0:128], T["dz2"][:, 0:258], start=True, stop=False,
                      skip_group_check=True)

            with pe.Fori(0, IMAGES) as i:
                def now(name):
                    ahead = name in AUX_Q or name in ("ref", "g")
                    return i + (PRIME + (2 if ahead else 1))

                def before(name):
                    return i + PRIME

                def sum_corners(c):
                    pe.wait_ge(weighed, i * CHUNKS + (PRIME + c + 1))
                    pe.wait_ge(smp_copied, i * CHUNKS + (PRIME + c))
                    for j in range(PAIRS):
                        for k in range(4):
                            last = pe.matmul(b_smp[:, j * 128:(j + 1) * 128],
                                             gathw[:, c % 2, k, j * 128:(j + 1) * 128], ident,
                                             is_transpose=True, start=(k == 0), stop=(k == 3))
                    last.then_inc(summed, 1)

                def keys_values(c):
                    pe.wait_ge(smp_copied, i * CHUNKS + (PRIME + c + 1))
                    pe.wait_ge(attended, i * CHUNKS + (PRIME + c - 1))
                    for j in range(PAIRS):
                        cols = slice(j * 128, (j + 1) * 128)
                        pe.matmul(b_k[c % 2][:, cols], smpT[:, c % 2, cols], par("wk2"), start=True, stop=True)
                        last = pe.matmul(b_v[c % 2][:, cols], smpT[:, c % 2, cols], par("wv2"), start=True, stop=True)
                    last.then_inc(kv_made, 1)

                for r in range(CHUNKS + 2):
                    if r < CHUNKS:
                        sum_corners(r)
                    for name in {1: ["qf", "qry", "off1"], 2: ["u", "k0"], 3: ["z1", "og", "off2"], 4: ["z2"],
                                 5: ["v", "lr"], 6: ["dk", "q"], 7: ["k1t", "dz2t"], 8: ["dz1t"]}.get(r, []):
                        (points_stage if name in AUX_Q else mlp_stage)(name, AUX, now, before)
                    if r == 8:
                        gradients(now)
                    if r < CHUNKS:
                        keys_values(r)

            last_now = lambda name: PRIME + IMAGES + 1
            for name in AUX_B:
                mlp_stage(name, AUX_B, last_now, lambda name: PRIME + IMAGES)
            gradients(last_now)
            phase23_tensor(pe)

        @block.scalar
        def _(act):
            chain = [0]

            def link(ins):
                chain[0] += 1
                ins.then_inc(s_act, 1)
                act.wait_ge(s_act, chain[0])

            def copy(dst, src):
                return act.activation(dst, src, ACT.Identity)

            def sigmoid(sg, src, half_bias):
                link(act.activation(sg, src, ACT.Tanh, bias=half_bias, scale=0.5))
                return act.activation(sg, sg, ACT.Copy, bias=0.5, scale=0.5)

            def moved(dst, name, now):
                act.wait_ge(made(name), now(name))
                copy(dst, bank_of[name][:, 0:dst.shape[1]]).then_inc(read(name), 1)

            def squares(slot_ap, now):
                act.wait_ge(sem("mean_done"), now("m"))
                for c in range(CHUNKS):
                    ins = act.activation(T["sq"][:, c * C:(c + 1) * C], slot_ap[:, c * C:(c + 1) * C], ACT.Square,
                                         bias=stat[:, 1, c:c + 1], accum_out=stat[:, 2, c:c + 1])
                ins.then_inc(sem("var_done"), 1)

            def mlp_round(r, now, slot_ap, q_ap):
                if r == 1:
                    squares(slot_ap, now)
                if r == 2:
                    moved(T["uT"][:, :], "u", now)
                    moved(T["k0"][:, :], "k0", now)
                if r == 3:
                    act.wait_ge(made("z1"), now("z1"))
                    sigmoid(T["sg1"][:, :], bank_of["z1"][:, :], hb[:, 0:1]).then_inc(sem("sg1_done"), 1)
                if r == 4:
                    act.wait_ge(made("z2"), now("z2"))
                    sigmoid(T["sg2"][:, :], bank_of["z2"][:, :], hb[:, 1:2]).then_inc(sem("sg2_done"), 1)
                if r == 5:
                    act.wait_ge(made("lr"), now("lr"))
                    act.activation(T["lr"][:, :], bank_of["lr"][:, :], ACT.Tanh, bias=hb[:, 2:3], scale=0.5
                                   ).then_inc(read("lr"), 1)
                if r == 6:
                    act.wait_ge(made("q"), now("q"))
                    copy(q_ap, bank_of["q"][:, :]).then_inc(read("q"), 1)
                if r == 7:
                    moved(T["k1t"][:, :], "k1t", now)
                    moved(T["dz2t"][:, :], "dz2t", now)
                if r == 8:
                    moved(T["dz1t"][:, :], "dz1t", now)

            def points_round(r, now):
                if r == 1:
                    moved(qfT[:, :], "qf", now)
                    moved(qry_next[:, :], "qry", now)
                if r == 2:
                    act.wait_ge(sem("gelu_arg"), now("a"))
                    act.activation(otanh[:, :], ot[:, :], ACT.Tanh, scale=GELU_C).then_inc(sem("gelu_tanh"), 1)
                if r == 3:
                    moved(ogT[:, :], "og", now)

            first = lambda name: PRIME + 1
            act.wait_ge(params_in, 16)
            for r in range(1, 4):
                points_round(r, first)
            act.wait_ge(read("qry"), PRIME + 1)
            copy(qry[:, :], qry_next[:, :]).then_inc(qry_moved, 1)
            act.wait_ge(made("txt_t"), 1)
            copy(T["k1"][0:CAT, 0:512], b_aux[0][0:CAT, :])
            copy(T["s1"][0:CAT, 0:128], b_aux[1][0:CAT, 0:128]).then_inc(read("txt_t"), 1)
            act.wait_ge(late_in, 16)
            link(act.activation(hb[:, 0:2], par("par")[:, 2 * C:2 * C + 2], ACT.Copy, scale=0.5))
            link(act.activation(hb[:, 2:3], par("blr"), ACT.Copy, scale=0.5))

            with act.Fori(0, IMAGES) as i:
                act.sem_clear(s_act)
                chain[0] = 0
                now = lambda name: i + (PRIME + (2 if name in AUX_Q or name == "a" else 1))
                for r in range(CHUNKS + 2):
                    if r < CHUNKS:
                        act.wait_ge(summed, i * CHUNKS + (PRIME + r + 1))
                        act.wait_ge(kv_made, i * CHUNKS + (PRIME + r - 1))
                        copy(smpT[:, r % 2, :], b_smp[:, :]).then_inc(smp_copied, 1)
                    points_round(r, now)
                    mlp_round(r, now, h_all[:, bass.ds(i, 1), :].rearrange("p a n -> p (a n)"),
                              q_all[:, bass.ds(i, 1), :].rearrange("p a n -> p (a n)"))
                    if 1 <= r <= CHUNKS:
                        c = r - 1
                        act.wait_ge(scored, i * CHUNKS + (PRIME + c + 1))
                        act.activation(prob[:, c % 2, :, :], score[:, c % 2, :, :], ACT.Exp, scale=DH ** -0.5
                                       ).then_inc(exped, 1)
                    if r == CHUNKS:
                        act.wait_ge(read("qry"), i + (PRIME + 2))
                        copy(qry[:, :], qry_next[:, :]).then_inc(qry_moved, 1)
            act.sem_clear(s_act)
            chain[0] = 0
            for r in range(1, 9):
                mlp_round(r, lambda name: PRIME + IMAGES + 1, h_all[:, IMAGES, :], q_all[:, IMAGES, :])
            phase3_scalar(act, chain, link, copy, sigmoid)

        @block.vector
        def _(dve):
            steps = [0]

            def step(ins):
                steps[0] += 1
                ins.then_inc(s_dve, 1)

            def sync():
                dve.wait_ge(s_dve, steps[0])

            def link(ins):
                step(ins)
                sync()

            def bc(ap, n):
                return ap.unsqueeze(len(ap.shape)).broadcast_to(list(ap.shape) + [n])

            def chunked(ap):
                return ap.rearrange("p (n c) -> p n c", n=CHUNKS)

            def rsqrt(dst, var, tmp):
                link(dve.tensor_scalar(seed[:, :], var.bitcast(I32), 1, None, ALU.logical_shift_right))
                link(dve.tensor_scalar(dst.bitcast(I32), seed[:, :], -1.0, RSQRT_SEED, ALU.mult, ALU.add))
                for _ in range(3):
                    link(dve.scalar_tensor_tensor(tmp, dst, -0.5, var, ALU.mult, ALU.mult))
                    link(dve.tensor_tensor(tmp, tmp, dst, ALU.mult))
                    link(dve.scalar_tensor_tensor(dst, tmp, 1.5, dst, ALU.add, ALU.mult))

            def weigh_reference(now):
                dve.tensor_tensor(xrefw[:, :, :, :].rearrange("p k n c -> p (k n) c"),
                                  xref[:, :, :, :].rearrange("p k n c -> p (k n) c"),
                                  bc(par("refw"), C), ALU.mult).then_inc(ref_used, 1)

            def points_round(r, now, base_done):
                if r == 1:
                    hv = oh[:, :].rearrange("p (n k) -> p n k", n=CHUNKS)
                    tv = ot[:, :].rearrange("p (n k) -> p n k", n=CHUNKS)
                    dve.wait_ge(made("off1"), now("off1"))
                    dve.tensor_tensor(oh[:, :], bank_of["off1"][:, 0:128], par("bo1"), ALU.add).then_inc(read("off1"), 1)
                    dve.wait_ge(read("off1"), now("off1"))
                    link(dve.tensor_reduce(stat[:, 4, :], hv, AX, ALU.add))
                    link(dve.tensor_scalar(stat[:, 4, :], stat[:, 4, :], -1.0 / HID, None, ALU.mult))
                    link(dve.tensor_tensor(hv, hv, bc(stat[:, 4, :], HID), ALU.add))
                    link(dve.tensor_tensor(ot[:, :], oh[:, :], oh[:, :], ALU.mult))
                    link(dve.tensor_reduce(stat[:, 5, :], tv, AX, ALU.add))
                    link(dve.tensor_scalar(stat[:, 5, :], stat[:, 5, :], 1.0 / HID, LN_EPS, ALU.mult, ALU.add))
                    rsqrt(stat[:, 6, :], stat[:, 5, :], stat[:, 7, :])
                    link(dve.tensor_tensor(hv, hv, bc(stat[:, 6, :], HID), ALU.mult))
                    link(dve.tensor_tensor(oh[:, :], oh[:, :], par("lng"), ALU.mult))
                    link(dve.tensor_tensor(oh[:, :], oh[:, :], par("lnb"), ALU.add))
                    link(dve.tensor_tensor(ot[:, :], oh[:, :], oh[:, :], ALU.mult))
                    link(dve.tensor_scalar(ot[:, :], ot[:, :], GELU_A, 1.0, ALU.mult, ALU.add))
                    dve.tensor_tensor(ot[:, :], ot[:, :], oh[:, :], ALU.mult).then_inc(sem("gelu_arg"), 1)
                if r == 2:
                    dve.wait_ge(sem("gelu_tanh"), now("t"))
                    dve.scalar_tensor_tensor(oh[:, :], otanh[:, :], 1.0, oh[:, :], ALU.add, ALU.mult
                                             ).then_inc(sem("gelu_done"), 1)
                if r == 3:
                    pv = px[:, :, :].rearrange("p n a -> p (n a)")
                    cv = corner[:, :, :].rearrange("p n a -> p (n a)")
                    dve.wait_ge(made("off2"), now("off2"))
                    dve.scalar_tensor_tensor(pv, bank_of["off2"][:, 0:128], 2.0,
                                             refb[:, :, :, :].rearrange("p n m a -> p (n m a)"),
                                             ALU.mult, ALU.add).then_inc(read("off2"), 1)
                    dve.wait_ge(read("off2"), now("off2"))
                    link(dve.tensor_scalar(pv, pv, 0.0, float(W - 1), ALU.max, ALU.min))
                    link(dve.tensor_scalar(cv, pv, ROUND - 0.5, ROUND, ALU.add, ALU.subtract))
                    link(dve.tensor_scalar(cv, cv, 0.0, float(W - 2), ALU.max, ALU.min))
                    f1 = frac[:, 1, :, :].rearrange("p n a -> p (n a)")
                    link(dve.tensor_tensor(f1, pv, cv, ALU.subtract))
                    link(dve.tensor_scalar(frac[:, 0, :, :].rearrange("p n a -> p (n a)"), f1, -1.0, 1.0,
                                           ALU.mult, ALU.add))
                    for dx in range(2):
                        step(dve.tensor_tensor(wts_next[:, :, dx, :].rearrange("p n b -> p b n"),
                                               frac[:, dx:dx + 1, :, 0].broadcast_to([P, 2, CHUNKS * POINTS]),
                                               frac[:, :, :, 1], ALU.mult))
                    step(dve.scalar_tensor_tensor(row_next[:, :], corner[:, :, 1], float(W), corner[:, :, 0],
                                                  ALU.mult, ALU.add))

            def rows_live(half, now):
                cols = slice(half * 32, half * 32 + 32)
                dve.tensor_scalar(row[:, cols], row_next[:, cols], row_base[:, 0:1], None, ALU.add
                                  ).then_inc((rows_a, rows_b)[half], 1)

            def mlp_round(r, now, slot_ap, prev):
                if r == 0:
                    link(dve.tensor_reduce(stat[:, 0, :], chunked(slot_ap), AX, ALU.add))
                    dve.tensor_scalar(stat[:, 1, :], stat[:, 0, :], -1.0 / C, None, ALU.mult).then_inc(sem("mean_done"), 1)
                if r == 1:
                    dve.wait_ge(sem("grads_added"), prev)
                    normalise(T["u"], slot_ap, now)
                if r == 3:
                    dve.wait_ge(sem("sg1_done"), now("z1"))
                    dve.scalar_tensor_tensor(T["s1"][:, :], bank_of["z1"][:, :], par("par")[:, 2 * C:2 * C + 1],
                                             T["sg1"][:, :], ALU.add, ALU.mult).then_inc(read("z1"), 1)
                    dve.wait_ge(read("z1"), now("z1"))
                    dve.tensor_tensor(T["k1"][:, :], T["k0"][:, :], T["s1"][:, :], ALU.add).then_inc(sem("k1_done"), 1)
                    link(dve.scalar_tensor_tensor(T["d1"][:, :], T["s1"][:, :], 1.0, T["sg1"][:, :],
                                                  ALU.subtract, ALU.mult))
                    step(dve.tensor_tensor(T["d1"][:, :], T["s1"][:, :], T["d1"][:, :], ALU.subtract))
                if r == 4:
                    dve.wait_ge(sem("sg2_done"), now("z2"))
                    dve.scalar_tensor_tensor(T["s2"][:, :], bank_of["z2"][:, :], par("par")[:, 2 * C + 1:2 * C + 2],
                                             T["sg2"][:, :], ALU.add, ALU.mult).then_inc(read("z2"), 1)
                    dve.wait_ge(read("z2"), now("z2"))
                    step(dve.tensor_tensor(T["res"][:, :], T["k1"][:, :], T["s2"][:, :], ALU.add))
                    link(dve.scalar_tensor_tensor(T["d2"][:, :], T["s2"][:, :], 1.0, T["sg2"][:, :],
                                                  ALU.subtract, ALU.mult))
                    step(dve.tensor_tensor(T["d2"][:, :], T["s2"][:, :], T["d2"][:, :], ALU.subtract))
                if r == 5:
                    dve.wait_ge(made("v"), now("v"))
                    sync()
                    dve.tensor_tensor(T["res"][:, :], T["res"][:, :], bank_of["v"][:, :], ALU.subtract
                                      ).then_inc(read("v"), 1)
                    dve.wait_ge(read("lr"), now("lr"))
                    step(dve.scalar_tensor_tensor(T["dp"][:, :], T["lr"][:, :], 1.0, par("lossw"), ALU.add, ALU.mult))
                    dve.wait_ge(read("v"), now("v"))
                    sync()
                    link(dve.tensor_tensor(T["dp"][:, :], T["dp"][:, :], T["res"][:, :], ALU.mult))
                    dve.tensor_tensor(T["dz2"][:, :], T["dp"][:, :], T["d2"][:, :], ALU.mult).then_inc(sem("dz2_done"), 1)
                if r == 6:
                    dve.wait_ge(made("dk"), now("dk"))
                    link(dve.tensor_tensor(T["dp"][:, :], T["dp"][:, :], bank_of["dk"][:, :], ALU.add))
                    dve.tensor_tensor(T["dz1"][:, :], T["dp"][:, :], T["d1"][:, :], ALU.mult).then_inc(read("dk"), 1)

            def normalise(dst, src, now):
                dve.wait_ge(sem("var_done"), now("n"))
                link(dve.tensor_scalar(stat[:, 2, :], stat[:, 2, :], 1.0 / C, LN_EPS, ALU.mult, ALU.add))
                rsqrt(stat[:, 3, :], stat[:, 2, :], stat[:, 0, :])
                for c in range(CHUNKS):
                    ins = dve.tensor_scalar(dst[:, c * C:(c + 1) * C], src[:, c * C:(c + 1) * C],
                                            stat[:, 1, c:c + 1], stat[:, 3, c:c + 1], ALU.add, ALU.mult)
                ins.then_inc(sem("normed"), 1)

            first = lambda name: PRIME + 1
            step(dve.memset(ones[:, :], 1.0))
            step(dve.memset(row_base[:, :], 0.0))
            step(dve.memset(T["dz1"][:, :], 0.0))
            step(dve.memset(T["dz2"][:, :], 0.0))
            step(dve.memset(h_all[:, 0, :], 0.0))
            dve.wait_ge(txt_in, 16)
            sync()
            dve.scalar_tensor_tensor(txt_row[:, :], txt_i[:, 0:TXT_CHUNKS], float(TXT_ROWS),
                                     txt_i[:, TXT_CHUNKS:2 * TXT_CHUNKS], ALU.mult, ALU.add).then_inc(rows_txt, 1)
            dve.wait_ge(params_in, 16)
            bo2 = par("bo2").rearrange("p (n m a) -> p n m a", n=CHUNKS, a=2)
            refpx = par("refpx").rearrange("p (n a) -> p n a", a=2)
            for n in range(CHUNKS):
                step(dve.scalar_tensor_tensor(refb[:, n, :, :], bo2[:, n, :, :], 4.0,
                                              refpx[:, n:n + 1, :].broadcast_to([P, POINTS, 2]), ALU.mult, ALU.add))
            sync()
            dve.wait_ge(ref_in, 16)
            weigh_reference(first)
            for r in range(1, 4):
                points_round(r, first, None)
            sync()
            rows_live(0, None)
            rows_live(1, None)
            dve.wait_ge(rows_b, PRIME + 1)
            link(dve.tensor_scalar(row_base[:, :], row_base[:, :], float(H * W), None, ALU.add))
            step(dve.tensor_copy(wts[:, :, :].rearrange("p n k -> p (n k)"),
                                 wts_next[:, :, :, :].rearrange("p n a b -> p (n a b)")))
            dve.wait_ge(late_in, 16)
            step(dve.tensor_scalar(txt_cat[:, :, C + TYPE_DIM], par("outc"), par("txts")[:, 0:1], None, ALU.mult))
            step(dve.tensor_scalar(txt_cat[:, :, C + TYPE_DIM + 1], par("dt"), par("txts")[:, 1:2], None, ALU.mult))
            dve.memset(txt_cat[:, :, CAT - 1:CAT], 1.0).then_inc(sem("txt_cat_done"), 1)
            nt = TXT_CHUNKS
            tx = T["res"][:, 0:nt * C].rearrange("p (n c) -> p n c", n=nt)
            ty = T["sq"][:, 0:nt * C].rearrange("p (n c) -> p n c", n=nt)
            proj = b_aux[0][:, 0:nt * C].rearrange("p (n c) -> p n c", n=nt)
            dve.wait_ge(made("txt_p"), 1)
            link(dve.memset(stat[:, 2, :], 1.0))
            link(dve.tensor_reduce(stat[:, 0, 0:nt], proj, AX, ALU.add))
            link(dve.tensor_scalar(stat[:, 1, 0:nt], stat[:, 0, 0:nt], -1.0 / C, None, ALU.mult))
            dve.tensor_tensor(tx, proj, bc(stat[:, 1, 0:nt], C), ALU.add).then_inc(read("txt_p"), 1)
            dve.wait_ge(read("txt_p"), 1)
            link(dve.tensor_tensor(ty, tx, tx, ALU.mult))
            link(dve.tensor_reduce(stat[:, 2, 0:nt], ty, AX, ALU.add))
            link(dve.tensor_scalar(stat[:, 2, :], stat[:, 2, :], 1.0 / C, LN_EPS, ALU.mult, ALU.add))
            rsqrt(stat[:, 3, :], stat[:, 2, :], stat[:, 0, :])
            link(dve.tensor_tensor(tx, tx, bc(stat[:, 3, 0:nt], C), ALU.mult))
            link(dve.tensor_tensor(tx, tx, par("txtg").unsqueeze(1).broadcast_to([P, nt, C]), ALU.mult))
            link(dve.tensor_tensor(h_all[:, 0, 0:nt * C].rearrange("p (n c) -> p n c", n=nt), tx,
                                   par("txtb").unsqueeze(1).broadcast_to([P, nt, C]), ALU.add))

            with dve.Fori(0, IMAGES) as i:
                dve.sem_clear(s_dve)
                steps[0] = 0
                ahead = AUX_Q + ["t", "a", "g", "ref"]
                now = lambda name: i + (PRIME + (2 if name in ahead else 1))
                slot = lambda k: h_all[:, bass.ds(k, 1), :].rearrange("p a n -> p (a n)")

                def weigh(c):
                    if c < RING:
                        dve.wait_ge(gathered[c], i * (2 * 16 * POINTS) + 16 * POINTS)
                    else:
                        dve.wait_ge(gathered[c % RING], i * (2 * 16 * POINTS) + 2 * 16 * POINTS)
                    dve.wait_ge(summed, i * CHUNKS + (PRIME + c - 1))
                    dve.tensor_tensor(gathw[:, c % 2, :, :].rearrange("p k (n c) -> p n k c", n=POINTS),
                                      gath[:, c % RING, :, :].rearrange("p n (k c) -> p n k c", k=4),
                                      bc(wts[:, c, :].rearrange("p (n k) -> p n k", k=4), C), ALU.mult
                                      ).then_inc(weighed, 1)

                def scores(c):
                    dve.wait_ge(kv_made, i * CHUNKS + (PRIME + c + 1))
                    if c == 0:
                        dve.wait_ge(qry_moved, i + (PRIME + 1))
                    link(dve.tensor_tensor(qk[:, :].rearrange("p (n c) -> p n c", n=POINTS),
                                           b_k[c % 2][:, :].rearrange("p (n c) -> p n c", n=POINTS),
                                           qry[:, c * C:(c + 1) * C].unsqueeze(1).broadcast_to([P, POINTS, C]), ALU.mult))
                    sc = score[:, c % 2, :, :]
                    link(dve.tensor_reduce(sc.rearrange("p n h -> p (n h)"),
                                           qk[:, :].rearrange("p (m d) -> p m d", d=DH), AX, ALU.add))
                    link(dve.tensor_reduce(ha[:, 0, :], sc.rearrange("p n h -> p h n"), AX, ALU.max))
                    dve.tensor_tensor(sc, sc, ha[:, 0:1, :].broadcast_to([P, POINTS, HEADS]), ALU.subtract
                                      ).then_inc(scored, 1)

                def attend(c):
                    dve.wait_ge(exped, i * CHUNKS + (PRIME + c + 1))
                    pr = prob[:, c % 2, :, :]
                    step(dve.tensor_reduce(ha[:, 1, :], pr.rearrange("p n h -> p h n"), AX, ALU.add))
                    step(dve.tensor_tensor(av[:, :].rearrange("p (m d) -> p m d", d=DH),
                                           b_v[c % 2][:, :].rearrange("p (m d) -> p m d", d=DH),
                                           bc(pr.rearrange("p n h -> p (n h)"), DH), ALU.mult))
                    sync()
                    step(dve.reciprocal(ha[:, 2, :], ha[:, 1, :]))
                    link(dve.tensor_reduce(ho[:, :], av[:, :].rearrange("p (n c) -> p c n", n=POINTS), AX, ALU.add))
                    dve.tensor_tensor(slot(i + 1)[:, c * C:(c + 1) * C].rearrange("p (h d) -> p h d", d=DH),
                                      ho[:, :].rearrange("p (h d) -> p h d", d=DH),
                                      bc(ha[:, 2, :], DH), ALU.mult).then_inc(attended, 1)

                for r in range(CHUNKS + 2):
                    if r < CHUNKS:
                        weigh(r)
                    if 1 <= r <= CHUNKS:
                        scores(r - 1)
                    if r >= 2:
                        attend(r - 2)
                    if r == 0:
                        dve.wait_ge(ref_in, i * 16 + 32)
                        dve.wait_ge(made("qf"), i + (PRIME + 1))
                        weigh_reference(now)
                    if r == 0:
                        dve.wait_ge(attended, i * CHUNKS + PRIME)
                    if r < 7:
                        mlp_round(r, now, slot(i), i + PRIME)
                    points_round(r, now, None)
                    if r == 7:
                        link(dve.memset(par("lossw"), MAX_ALR / C))
                        sync()
                        step(dve.tensor_copy(wts[:, :, :].rearrange("p n k -> p (n k)"),
                                             wts_next[:, :, :, :].rearrange("p n a b -> p (n a b)")))
                    if r == 4:
                        dve.wait_ge(issued_a, i + (PRIME + 1))
                        sync()
                        rows_live(0, now)
                    if r == 8:
                        dve.wait_ge(issued_b, i + (PRIME + 1))
                        rows_live(1, now)
                        dve.wait_ge(rows_b, i + (PRIME + 2))
                        link(dve.tensor_scalar(row_base[:, :], row_base[:, :], float(H * W), None, ALU.add))
                sync()
            dve.sem_clear(s_dve)
            steps[0] = 0
            dve.wait_ge(attended, IMAGES * CHUNKS + PRIME)
            for r in range(7):
                mlp_round(r, lambda name: PRIME + IMAGES + 1, h_all[:, IMAGES, :], PRIME + IMAGES)
            phase23_vector(dve, steps, step, sync, link, bc, chunked, rsqrt, normalise)


def blocks(ms):
    out = np.zeros((sum(m.shape[0] for m in ms), sum(m.shape[1] for m in ms)), np.float32)
    r = c = 0
    for m in ms:
        out[r:r + m.shape[0], c:c + m.shape[1]] = m
        r, c = r + m.shape[0], c + m.shape[1]
    return out


def kernel(**inputs):
    import concourse.bacc as _bacc
    from concourse.bass_utils import run_bass_kernel_spmd as _run

    a = {k: np.asarray(v) for k, v in inputs.items()}
    tok = {k[7:]: v for k, v in a.items() if k.startswith("L0_tok_")}
    txt = {k[7:]: v for k, v in a.items() if k.startswith("L0_txt_")}
    mem = {k[8:]: v for k, v in a.items() if k.startswith("L0_attn_")}
    ffn = {k[7:]: v for k, v in a.items() if k.startswith("L0_ffn_")}

    def rows(v, n=P):
        return np.broadcast_to(v.reshape(1, -1), (n, v.size))

    def pack(entries, parts):
        where, total = columns(entries)
        out = np.zeros((P, total), np.float32)
        for name, m in parts.items():
            at, n = where[name]
            assert m.shape[1] == n, (name, m.shape, n)
            out[:m.shape[0], at:at + n] = m
        return out

    x = a["x"].transpose(0, 2, 3, 1)
    below = np.concatenate([x[:, 1:], np.zeros_like(x[:, :1])], axis=1)
    x_pairs = np.ascontiguousarray(np.stack([x, below], axis=3)).reshape(IMAGES * H * W, 2 * C)

    n = np.arange(P * CHUNKS).reshape(P, CHUNKS)
    grid = (np.linspace(-1.0, 1.0, GRID).astype(np.float32) + np.float32(1)) * np.float32(0.5) * np.float32(W - 1)
    rx, ry = grid[n % GRID], grid[n // GRID]
    x0 = np.clip(np.floor(rx), 0, W - 2).astype(np.int64)
    y0 = np.clip(np.floor(ry), 0, H - 2).astype(np.int64)
    fx, fy = rx - x0, ry - y0
    refw = np.stack([wx * wy for wx in (1 - fx, fx) for wy in (1 - fy, fy)], axis=1)
    corners = np.stack([x[:, y0 + dy, x0 + dx] for dx in (0, 1) for dy in (0, 1)], axis=2)
    x_ref = np.concatenate([corners, np.zeros_like(corners[:1])]).reshape(IMAGES + 1, P, 4 * COLS)

    eye = np.eye(P, dtype=np.float32)
    early = pack(EARLY, {
        "ident": eye, "wq2": blocks([tok["W_q"].T] * 2), "wo1": blocks([tok["W_o1"]] * 2),
        "wo2": blocks([tok["W_o2"]] * CHUNKS), "wk2": blocks([tok["W_k"].T] * 2), "wv2": blocks([tok["W_v"].T] * 2),
        "bo1": rows(np.tile(tok["b_o1"], CHUNKS)), "lng": rows(np.tile(tok["ln_g"], CHUNKS)),
        "lnb": rows(np.tile(tok["ln_b"], CHUNKS)), "bo2": rows(np.tile(tok["b_o2"], CHUNKS)),
        "refw": refw.reshape(P, 32), "refpx": np.stack([rx, ry], axis=2).reshape(P, 16)})

    def per_token(v):
        flat = v.reshape(-1)
        return np.concatenate([flat, np.zeros(P * TXT_CHUNKS - flat.size, flat.dtype)]).reshape(P, TXT_CHUNKS)

    chunk = np.arange(CHUNKS)[None]
    live = (chunk < TXT_CHUNKS) & (np.arange(P)[:, None] * TXT_CHUNKS + chunk < TXT_B * TXT_L)
    live = live.reshape(P, PAIRS, 2).transpose(2, 1, 0).reshape(2, 1, COLS)
    lossw = np.broadcast_to(live, (2, C, COLS)).reshape(P, COLS) * np.float32(MAX_ALR / C)
    half = np.kron(np.eye(2), np.ones((C, C)))
    experts = range(EPAIRS)
    sel = np.zeros((18, EPAIRS * P), np.float32)
    for p in experts:
        for e in range(2):
            sel[[2 * p + e, 6 + 2 * p + e, 12 + 2 * p + e], p * P + e * C:p * P + (e + 1) * C] = 1
    w1, w2, w3 = ffn["expert_w1"], ffn["expert_w2"], ffn["expert_w3"]
    col = lambda v: v.reshape(-1, 1)
    late = pack(LATE, {
        "mk": blocks([mem["Wk"]] * 2), "mv": blocks([mem["Wv"]] * 2), "mq": blocks([mem["Wq"]] * 2),
        "mlr": blocks([np.broadcast_to(mem["Wlr"], (C, C))] * 2),
        "mw1": blocks([mem["Ws"][0]] * 2), "mw2": blocks([mem["Ws"][1]] * 2), "mw2t": blocks([mem["Ws"][1].T] * 2),
        "mkrep": np.tile(mem["Wk"], (1, 2)),
        "par": np.tile(np.concatenate([mem["Ws"][0], mem["Ws"][1], col(mem["bs"][0]), col(mem["bs"][1])], axis=1), (2, 1)),
        "blr": rows(mem["blr"]), "stack": np.tile(np.eye(C, dtype=np.float32), (2, 2)),
        "gmask": np.tile(half.astype(np.float32), (1, 2)), "lossw": lossw,
        "rw1": blocks([ffn["router_w1"]] * 2), "rb1": col(np.tile(ffn["router_b1"], 2)),
        "rw2": blocks([ffn["router_w2"]] * 2), "rb2": rows(np.tile(ffn["router_b2"], CHUNKS)),
        "first": rows(np.tile(np.arange(EXPERTS, 0, -1).astype(np.float32), CHUNKS)),
        "ew1": np.tile(np.concatenate([w1[e] for e in range(EXPERTS)], axis=1), (2, 1)),
        "eb1": ffn["expert_b1"].reshape(EPAIRS, P).T,
        "ew2": np.concatenate([blocks([w2[2 * p], w2[2 * p + 1]]) for p in experts], axis=1),
        "eb2": ffn["expert_b2"].reshape(EPAIRS, P).T,
        "ew3": np.concatenate([w3[2 * p:2 * p + 2].reshape(P, C) for p in experts], axis=1),
        "eb3": blocks([ffn["expert_b3"]] * CHUNKS), "sel": sel,
        "txtw": np.concatenate([txt["W_proj_w"].T, txt["W_proj_b"].reshape(1, C)]),
        "txtg": rows(txt["ln_gamma"]), "txtb": rows(txt["ln_beta"]),
        "txts": rows(np.concatenate([txt["W_o"], txt["W_delta"]])),
        "outc": per_token(a["fside_BS_outcomes"]), "dt": per_token(a["fside_BS_delta_ts"])})
    txt_idx = np.concatenate([per_token(a["x_txt"].astype(np.int32)),
                              per_token(a["itok_BS_0_4999"].astype(np.int32))], axis=1)
    pad = lambda h: np.concatenate([h, np.zeros((TXT_ROWS - h.shape[0], C), np.float32)])
    table = np.concatenate([pad(txt["h_qa"]), pad(txt["h_v"]), pad(txt["h_r"])])

    arrays = {"x_pairs": x_pairs, "x_ref": x_ref, "early": early, "late": late, "txt_idx": txt_idx,
              "txt_table": table, "type_table": np.ascontiguousarray(txt["E_type_w"])}
    nc = _bacc.Bacc("TRN2", target_bir_lowering=False, num_devices=1)
    args = [nc.dram_tensor(k, v.shape, mybir.dt.from_np(v.dtype), kind="ExternalInput").ap() for k, v in arrays.items()]
    args.append(nc.dram_tensor("tokens_out", (SLOTS, P, COLS), F32, kind="ExternalOutput").ap())
    build(nc, *args)
    got = _run(nc, [arrays], core_ids=[0]).results[0]["tokens_out"]
    image = got[1:].reshape(IMAGES, P * CHUNKS, C)
    text = got[0][:, :TXT_CHUNKS * C].reshape(P * TXT_CHUNKS, C)[:TXT_B * TXT_L].reshape(TXT_B, TXT_L, C)
    return np.concatenate([image, text], axis=1)
```

```python
from contextlib import ExitStack

import concourse.bass as bass
import numpy as np
from concourse import mybir

F32 = mybir.dt.float32
BF16 = mybir.dt.bfloat16
I32 = mybir.dt.int32
U32 = mybir.dt.uint32
ALU = mybir.AluOpType
ACT = mybir.ActivationFunctionType
AX = mybir.AxisListType.X

P = 128
IMAGES, C, H, W = 8, 64, 128, 128
GRID = H // 4
CHUNKS = 8
POINTS = 8
HEADS = 8
DH = C // HEADS
HID = C // 4
SLOTS = IMAGES + 1
COLS = CHUNKS * C
PAIRS = CHUNKS // 2
TXT_B, TXT_L = 8, 77
TXT_CHUNKS = 5
TXT_ROWS = 5000
TYPE_DIM = 16
CAT = C + TYPE_DIM + 3
EXPERTS = 6
RH = 32
EPAIRS = EXPERTS // 2
LR, WD, MAX_ALR = 0.001, 0.01, 0.1
LN_EPS = 1e-5
RING = 4
PRIME = 8
GELU_C, GELU_A = 0.7978845608028654, 0.044715
ROUND = 8388608.0
RSQRT_SEED = 1597463007.0

EARLY = [("ident", 128), ("wq2", 128), ("wo1", 2 * HID), ("wo2", 128), ("wk2", 128), ("wv2", 128),
         ("bo1", 128), ("lng", 128), ("lnb", 128), ("bo2", 128), ("refw", 32), ("refpx", 16)]
LATE = [("mk", 128), ("mv", 128), ("mlr", 128), ("mq", 128), ("mw1", 128), ("mw2", 128), ("mw2t", 128),
        ("mkrep", 128), ("par", 2 * C + 2), ("blr", 1), ("stack", 128), ("gmask", 256), ("lossw", 512),
        ("rw1", 2 * RH), ("rb1", 1), ("rw2", 2 * EXPERTS), ("rb2", CHUNKS * EXPERTS), ("first", CHUNKS * EXPERTS),
        ("ew1", EPAIRS * 128), ("eb1", EPAIRS), ("ew2", EPAIRS * 128), ("eb2", EPAIRS), ("ew3", EPAIRS * C),
        ("eb3", COLS), ("sel", EPAIRS * 128), ("txtw", C), ("txtg", C), ("txtb", C), ("txts", 2),
        ("outc", TXT_CHUNKS), ("dt", TXT_CHUNKS)]


def columns(entries):
    at, where = 0, {}
    for name, n in entries:
        where[name] = (at, n)
        at += n
    return where, at


def build(nc, x_pairs, x_ref, early, late, txt_idx, txt_table, type_table, out):
    with ExitStack() as ctx:
        def sb(name, shape, dt=F32):
            return ctx.enter_context(nc.sbuf_tensor(name, shape, dt))

        def bank(name):
            return ctx.enter_context(nc.psum_tensor(name, [P, 512], F32))

        sems = {}

        def sem(name):
            if name not in sems:
                sems[name] = ctx.enter_context(nc.semaphore(name))
            return sems[name]

        w_early = sb("w_early", [P, columns(EARLY)[1]])
        w_late = sb("w_late", [P, columns(LATE)[1]])

        def par(name, rows=P):
            tile, entries = (w_early, EARLY) if name in dict(EARLY) else (w_late, LATE)
            at, n = columns(entries)[0][name]
            return tile[0:rows, at:at + n]

        txt_i = sb("txt_i", [P, 2 * TXT_CHUNKS], I32)
        txt_row = sb("txt_row", [P, TXT_CHUNKS], I32)
        txt_cat = sb("txt_cat", [P, TXT_CHUNKS, CAT])
        xref = sb("xref", [P, 4, CHUNKS, C])
        xrefw = sb("xrefw", [P, 4, CHUNKS, C])
        qfT = sb("qfT", [P, COLS])
        qry_next = sb("qry_next", [P, COLS])
        qry = sb("qry", [P, COLS])
        oh = sb("oh", [P, 128])
        ot = sb("ot", [P, 128])
        otanh = sb("otanh", [P, 128])
        ogT = sb("ogT", [P, 128])
        refb = sb("refb", [P, CHUNKS, POINTS, 2])
        px = sb("px", [P, CHUNKS * POINTS, 2])
        corner = sb("corner", [P, CHUNKS * POINTS, 2])
        frac = sb("frac", [P, 2, CHUNKS * POINTS, 2])
        wts_next = sb("wts_next", [P, CHUNKS * POINTS, 2, 2])
        wts = sb("wts", [P, CHUNKS, POINTS * 4])
        row_next = sb("row_next", [P, CHUNKS * POINTS])
        row_base = sb("row_base", [P, 1])
        row = sb("row", [P, CHUNKS * POINTS], I32)
        stat = sb("stat", [P, 8, CHUNKS])
        var = sb("var", [P, 2, CHUNKS])
        rstd = sb("rstd", [P, 2, CHUNKS])
        newton = sb("newton", [P, 2, CHUNKS])
        seed = sb("seed", [P, 2, CHUNKS], I32)
        gath = sb("gath", [P, RING, POINTS, 4 * C])
        gathw = sb("gathw", [P, 2, 4, POINTS * C])
        smpT = sb("smpT", [P, 2, 512])
        qk = sb("qk", [P, POINTS * C])
        score = sb("score", [P, 2, POINTS, HEADS])
        prob = sb("prob", [P, 2, POINTS, HEADS])
        av = sb("av", [P, POINTS * C])
        ha = sb("ha", [P, 4, HEADS])
        ho = sb("ho", [P, C])
        h_all = sb("h_all", [P, SLOTS, COLS])
        q_all = sb("q_all", [P, SLOTS, COLS])
        T = {n: sb("t_" + n, [P, COLS]) for n in
             "u uT k0 sg1 s1 k1 d1 sg2 s2 d2 res lr dp dz2 dz1 k1t dz2t dz1t sq".split()}
        ones = sb("ones", [P, 1])
        grad = sb("grad", [P, 258])
        grad2 = sb("grad2", [P, 258])
        gpar = sb("gpar", [P, 2 * C + 2])
        gtmp = sb("gtmp", [P, 2 * C + 2])
        npar = sb("npar", [P, 2 * C + 2])
        nw = sb("nw", [P, 2, 128])
        hnb = sb("hnb", [P, 2])
        hb = sb("hb", [P, 3])

        ident_b = sb("ident_b", [P, P], BF16)
        sel_b = sb("sel_b", [18, EPAIRS * P], BF16)
        ring = gath[:, :, :, :].rearrange("p r (a b) (m c) -> p r a (b m c)", a=4, m=1)
        h2, u2T = ring[:, 0, 0:2, :], ring[:, 0, 2:4, :]
        e1, e2 = ring[:, 1, 0:2, :], ring[:, 1, 2:4, :]
        e2r, y = ring[:, 2, 0:2, :], ring[:, 2, 2:4, :]
        rhT = sb("rhT", [2 * RH, COLS])
        NE = CHUNKS * EXPERTS
        lg = sb("lg", [P, NE])
        pe_ = sb("pe_", [P, NE])
        prb = sb("prb", [P, NE])
        hot = sb("hot", [P, 2, NE])
        key = sb("key", [P, NE])
        top = sb("top", [P, 8, CHUNKS])
        rout = sb("rout", [P, NE])
        rest = sb("rest", [P, NE])
        rout3 = sb("rout3", [P, CHUNKS, 3 * EXPERTS], BF16)
        rout3T = sb("rout3T", [3 * EXPERTS, 2, 2 * COLS], BF16)
        routT = sb("routT", [NE, 2, P])

        b_smp = bank("b_smp")
        b_k = bank("b_k")
        b_v = [bank("b_v0"), bank("b_v1")]
        b_g = bank("b_g")
        b_aux = [bank("b_aux0"), bank("b_aux1"), bank("b_aux2")]

        params_in, txt_in, late_in, ready = sem("params_in"), sem("txt_in"), sem("late_in"), sem("ready")
        ref_in, ref_used = sem("ref_in"), sem("ref_used")
        gathered = [sem(f"gathered{k}") for k in range(RING)]
        txt_gathered, rows_txt = sem("txt_gathered"), sem("rows_txt")
        rows_a, rows_b = sem("rows_a"), sem("rows_b")
        issued_a, issued_b = sem("issued_a"), sem("issued_b")
        weighed, summed, smp_copied, kv_made = sem("weighed"), sem("summed"), sem("smp_copied"), sem("kv_made")
        scored, exped, attended = sem("scored"), sem("exped"), sem("attended")
        keys_read = sem("keys_read")
        qry_moved = sem("qry_moved")
        s_dve, s_act = sem("s_dve"), sem("s_act")

        def made(name):
            return sem("made_" + name)

        def read(name):
            return sem("read_" + name)

        AUX = ["qf", "qry", "off1", "u", "og", "k0", "off2", "z1", "v", "lr", "z2", "q", "k1t", "dz2t", "dk", "dz1t"]
        AUX_Q = [n for n in AUX if n in ("qf", "qry", "off1", "og", "off2")]
        AUX_B = [n for n in AUX if n not in AUX_Q]
        bank_of = {n: b_aux[k % 3] for k, n in enumerate(AUX)}

        def user_before(name, order):
            k = order.index(name)
            same = [n for n in order if bank_of[n] is bank_of[name]]
            earlier = [n for n in same if order.index(n) < k]
            return (earlier[-1], True) if earlier else (same[-1], False)

        UNITS = 2 * EPAIRS
        CAUX = ["r3", "r48", "z1", "z2", "rt", "u2", "rh", "lg"]
        cbank = {n: b_aux[k % 2] for k, n in enumerate(CAUX)}
        e1_bank, e2_bank, r_bank, y_bank = [b_k, b_aux[2]], b_v, b_smp, b_g
        l1_made, e1_done, l2_made, e2_done = sem("l1_made"), sem("e1_done"), sem("l2_made"), sem("e2_done")
        r_made, e2r_done, l3_made = sem("r_made"), sem("e2r_done"), sem("l3_made")
        y_done = sem("y_done")
        stored = [sem("stored0"), sem("stored1")]
        updated = sem("updated")
        PHASE3_SEMS = ([l1_made, e1_done, l2_made, e2_done, r_made, e2r_done, l3_made, y_done]
                       + [sem(f"{w}_c_{n}") for w in ("made", "read") for n in CAUX]
                       + [sem(n) for n in ("c_k1_done", "c_res_done", "c_sg1_done", "c_sg2_done", "c_lgx_done",
                                           "c_exp_done", "c_gap_done", "c_gape_done", "c_rout_done")])
        cmade = lambda n: sem(f"made_c_{n}")
        cread = lambda n: sem(f"read_c_{n}")

        def slots_loop(eng, one_slot):
            with eng.Fori(0, IMAGES // 2) as j:
                for parity in range(2):
                    one_slot(j * 2 + parity, parity, True)
            one_slot(IMAGES, 0, False)

        def phase3_sync(sp):
            with sp.Fori(0, IMAGES // 2) as j:
                for parity in range(2):
                    s = j * 2 + parity
                    sp.wait_ge(y_done, s + (PRIME + 1))
                    sp.dma_start(out[bass.ds(s, 1)].rearrange("a p n -> (a p) n"), y[:, parity, :]
                                 ).then_inc(stored[parity], 16)
            sp.wait_ge(y_done, PRIME + IMAGES + 1)
            sp.dma_start(out[IMAGES], y[:, 0, :]).then_inc(stored[0], 16)
            sp.wait_ge(stored[0], 16 * (IMAGES // 2 + 2))
            sp.wait_ge(stored[1], 16 * (IMAGES // 2 + 1))

        def phase23_tensor(pe):
            ident = par("ident")

            pe.wait_ge(sem("grad_masked"), 1)
            pe.matmul(b_aux[0][:, 0:258], par("stack"), grad[:, :], start=True, stop=True).then_inc(made("gsum"), 1)
            pe.wait_ge(sem("ghat_done"), 1)
            pe.matmul(b_aux[1][:, 0:C], par("mkrep", C), gtmp[0:C, 0:C], start=True, stop=True
                      ).then_inc(made("gw1"), 1)
            pe.wait_ge(updated, 1)

            def c1(name, slot, n, pred):
                if pred is not None:
                    k = CAUX.index(name)
                    pe.wait_ge(cread(CAUX[k - 2]), pred)
                dst = cbank[name]
                if name == "z1":
                    last = pe.matmul(dst[:, :], nw[:, 0, :], q_all[:, bass.ds(slot, 1), :].rearrange("p a n -> p (a n)"),
                                     start=True, stop=True)
                elif name == "z2":
                    pe.wait_ge(sem("c_k1_done"), n)
                    last = pe.matmul(dst[:, :], nw[:, 1, :], T["k1"][:, :], start=True, stop=True)
                elif name == "rt":
                    pe.wait_ge(sem("c_res_done"), n)
                    for j in range(PAIRS):
                        last = pe.transpose(dst[:, j * 128:(j + 1) * 128], T["res"][:, j * 128:(j + 1) * 128], ident)
                elif name == "u2":
                    pe.wait_ge(sem("normed"), n + SLOTS)
                    for j in range(PAIRS):
                        last = pe.transpose(dst[:, j * 128:(j + 1) * 128], T["u"][:, j * 128:(j + 1) * 128], ident)
                return last.then_inc(cmade(name), 1)

            def c1_router(name, parity, n, pred):
                k = CAUX.index(name)
                pe.wait_ge(cread(CAUX[k - 2]), pred)
                dst = cbank[name]
                if name == "rh":
                    pe.wait_ge(cread("u2"), n)
                    last = pe.matmul(dst[0:2 * RH, :], par("rw1"), u2T[:, parity, :], start=True, stop=True)
                elif name == "lg":
                    pe.wait_ge(cread("rh"), n)
                    for j in range(PAIRS):
                        last = pe.matmul(dst[:, j * 12:(j + 1) * 12], rhT[:, j * 128:(j + 1) * 128],
                                         par("rw2", 2 * RH), start=True, stop=True)
                elif name == "r3":
                    pe.wait_ge(sem("c_rout_done"), n)
                    for c in range(CHUNKS):
                        at = (c % 2) * COLS + (c // 2) * 128
                        last = pe.transpose(dst[:, :].bitcast(BF16)[0:18, at:at + 128], rout3[:, c, :], ident_b[:, :])
                elif name == "r48":
                    pe.sem_inc(sem("r48_started"), 1)
                    last = pe.transpose(dst[0:NE, 0:P], rout[:, :], ident)
                last.then_inc(cmade(name), 1)

            def one_slot(s, parity, more):
                c0, c1n = s + (PRIME + 1), s + (PRIME + 2)
                units = s * UNITS + PRIME

                def l1(m):
                    p, b = m // 2, m % 2
                    rows = slice(b * C, (b + 1) * C)
                    if m == 0:
                        pe.wait_ge(cread("u2"), c0)
                    pe.wait_ge(e1_done, units + (m - 1))
                    pe.matmul(e1_bank[m % 2][:, :], par("ew1")[rows, p * P:(p + 1) * P], u2T[rows, parity, :],
                              start=True, stop=True).then_inc(l1_made, 1)

                def l2(m):
                    p, b = m // 2, m % 2
                    pe.wait_ge(e1_done, units + (m + 1))
                    pe.wait_ge(e2_done, units + (m - 1))
                    pe.matmul(e2_bank[m % 2][:, :], par("ew2")[:, p * P:(p + 1) * P], e1[:, m % 2, :],
                              start=True, stop=True).then_inc(l2_made, 1)
                    if m == 0:
                        pe.wait_ge(cread("r3"), c0)
                    pe.wait_ge(e2r_done, units + m)
                    pe.matmul(r_bank[:, :], sel_b[:, p * P:(p + 1) * P], rout3T[:, parity, b * COLS:(b + 1) * COLS],
                              start=True, stop=True).then_inc(r_made, 1)

                def l3(m):
                    p, b = m // 2, m % 2
                    if m == 0:
                        pe.wait_ge(cread("r48"), c0)
                        pe.wait_ge(y_done, s + PRIME)
                        pe.matmul(y_bank[:, :], routT[:, parity, :], par("eb3", NE), start=True, stop=False,
                                  skip_group_check=True)
                    pe.wait_ge(e2r_done, units + (m + 1))
                    for j in range(PAIRS):
                        at = (2 * j + b) * C
                        last = pe.matmul(y_bank[:, at:at + C], e2r[:, m % 2, j * 128:(j + 1) * 128],
                                         par("ew3")[:, p * C:(p + 1) * C], start=False, stop=(m == UNITS - 1),
                                         skip_group_check=True)
                    last.then_inc(l3_made, 1)

                for m in range(UNITS + 2):
                    if m < UNITS:
                        l1(m)
                    if 1 <= m <= UNITS:
                        l2(m - 1)
                    if m >= 2:
                        l3(m - 2)
                    if m == 0:
                        c1_router("r3", parity, c0, c0)
                        c1_router("r48", parity, c0, c0)
                    if more:
                        if m == 0:
                            c1("z1", s + 1, c1n, c0)
                        if m == 1:
                            c1("z2", s + 1, c1n, c0)
                        if m == 2:
                            c1("rt", s + 1, c1n, c1n)
                        if m == 4:
                            c1("u2", s + 1, c1n, c1n)
                        if m == 5:
                            c1_router("rh", 1 - parity, c1n, c1n)
                        if m == 6:
                            c1_router("lg", 1 - parity, c1n, c1n)

            for name in ("z1", "z2", "rt", "u2"):
                c1(name, 0, PRIME + 1, None if name in ("z1", "z2") else PRIME + 1)
            for name in ("rh", "lg"):
                c1_router(name, 0, PRIME + 1, PRIME + 1)
            slots_loop(pe, one_slot)

        def phase3_scalar(act, chain, link, copy, sigmoid, normalise):
            act.wait_ge(updated, 1)

            def c1(r, parity, n):
                if r == 0:
                    act.wait_ge(cmade("z1"), n)
                    sigmoid(T["sg1"][:, :], cbank["z1"][:, :], hnb[:, 0:1]).then_inc(sem("c_sg1_done"), 1)
                if r == 1:
                    act.wait_ge(cmade("z2"), n)
                    sigmoid(T["sg2"][:, :], cbank["z2"][:, :], hnb[:, 1:2]).then_inc(sem("c_sg2_done"), 1)
                if r == 3:
                    act.wait_ge(sem("mean_done"), n + SLOTS)
                    for c in range(CHUNKS):
                        ins = act.activation(T["sq"][:, c * C:(c + 1) * C], h2[:, parity, c * C:(c + 1) * C], ACT.Square,
                                             bias=stat[:, 1, c:c + 1], accum_out=var[:, 0, c:c + 1])
                    ins.then_inc(sem("var_done"), 1)
                    normalise(T["u"], h2[:, parity, :], n + SLOTS)
                if r == 4:
                    act.wait_ge(cmade("u2"), n)
                    copy(u2T[:, parity, :], cbank["u2"][:, :]).then_inc(cread("u2"), 1)
                if r == 5:
                    act.wait_ge(cmade("rh"), n)
                    act.activation(rhT[:, :], cbank["rh"][0:2 * RH, :], ACT.Relu, bias=par("rb1", 2 * RH)
                                   ).then_inc(cread("rh"), 1)
                if r == 7:
                    act.wait_ge(sem("c_lgx_done"), n)
                    act.activation(pe_[:, :], lg[:, :], ACT.Exp).then_inc(sem("c_exp_done"), 1)
                    act.wait_ge(sem("c_gap_done"), n)
                    act.activation(top[:, 5, :], top[:, 4, :], ACT.Exp).then_inc(sem("c_gape_done"), 1)

            def one_slot(s, parity, more):
                act.sem_clear(s_act)
                chain[0] = 0
                c0, c1n = s + (PRIME + 1), s + (PRIME + 2)
                units = s * UNITS + PRIME

                for m in range(UNITS + 2):
                    if m < UNITS:
                        act.wait_ge(l1_made, units + (m + 1))
                        act.wait_ge(l2_made, units + (m - 1))
                        act.activation(e1[:, m % 2, :], e1_bank[m % 2][:, :], ACT.Relu,
                                       bias=par("eb1")[:, m // 2:m // 2 + 1]).then_inc(e1_done, 1)
                    if 1 <= m <= UNITS:
                        k = m - 1
                        act.wait_ge(l2_made, units + (k + 1))
                        act.wait_ge(e2r_done, units + (k - 1))
                        act.activation(e2[:, k % 2, :], e2_bank[k % 2][:, :], ACT.Relu,
                                       bias=par("eb2")[:, k // 2:k // 2 + 1]).then_inc(e2_done, 1)
                    if m == 0:
                        act.wait_ge(cmade("r3"), c0)
                        copy(rout3T[:, parity, :], cbank["r3"][:, :].bitcast(BF16)[0:18, :]).then_inc(cread("r3"), 1)
                        act.wait_ge(cmade("r48"), c0)
                        copy(routT[:, parity, :], cbank["r48"][0:NE, 0:P]).then_inc(cread("r48"), 1)
                    if more:
                        c1(m, 1 - parity, c1n)

            act.sem_clear(s_act)
            chain[0] = 0
            for r in range(UNITS + 2):
                c1(r, 0, PRIME + 1)
            slots_loop(act, one_slot)

        def phase23_vector(dve, steps, step, sync, link, bc, chunked, rsqrt_tokens):
            dve.wait_ge(sem("grads_added"), PRIME + SLOTS)
            step(dve.tensor_tensor(grad[:, 0:256], b_g[:, 0:256], par("gmask"), ALU.mult))
            step(dve.tensor_copy(ident_b[:, :], par("ident")))
            step(dve.tensor_copy(sel_b[:, :], par("sel", 18)))
            step(dve.memset(nw[:, :, :], 0.0))
            sync()
            dve.tensor_copy(grad[:, 256:258], b_g[:, 256:258]).then_inc(sem("grad_masked"), 1)
            dve.wait_ge(made("gsum"), 1)
            link(dve.tensor_copy(grad2[:, :], b_aux[0][:, 0:258]))
            dve.tensor_tensor(gtmp[:, 0:C], grad2[:, 128:128 + C], grad2[:, 128 + C:256], ALU.add
                              ).then_inc(sem("ghat_done"), 1)
            step(dve.tensor_tensor(gpar[:, C:2 * C], grad2[:, 0:C], grad2[:, C:2 * C], ALU.add))
            step(dve.tensor_copy(gpar[:, 2 * C:], grad2[:, 256:258]))
            dve.wait_ge(made("gw1"), 1)
            link(dve.tensor_copy(gpar[:, 0:C], b_aux[1][:, 0:C]))
            link(dve.scalar_tensor_tensor(gtmp[:, :], gpar[:, :], -1.0, gpar[:, :], ALU.mult, ALU.max))
            link(dve.tensor_scalar(gtmp[:, :], gtmp[:, :], 1e-8, None, ALU.add))
            link(dve.reciprocal(gtmp[:, :], gtmp[:, :]))
            link(dve.tensor_tensor(gtmp[:, :], gtmp[:, :], gpar[:, :], ALU.mult))
            link(dve.tensor_scalar(npar[:, :], par("par"), 1.0 - LR * WD, None, ALU.mult))
            link(dve.scalar_tensor_tensor(npar[:, :], gtmp[:, :], -LR, npar[:, :], ALU.mult, ALU.add))
            for k in range(2):
                for b in range(2):
                    half = slice(b * C, (b + 1) * C)
                    step(dve.tensor_copy(nw[half, k, half], npar[half, k * C:(k + 1) * C]))
            sync()
            dve.tensor_scalar(hnb[:, :], npar[:, 2 * C:], 0.5, None, ALU.mult).then_inc(updated, 1)

            v3 = lambda ap: ap.rearrange("p (n e) -> p n e", n=CHUNKS)

            def pick(which, probs, best):
                link(dve.tensor_reduce(best, v3(probs), AX, ALU.max))
                link(dve.tensor_tensor(v3(key[:, :]), v3(probs), bc(best, EXPERTS), ALU.is_equal))
                link(dve.tensor_tensor(key[:, :], key[:, :], par("first"), ALU.mult))
                link(dve.tensor_reduce(top[:, 7, :], v3(key[:, :]), AX, ALU.max))
                link(dve.tensor_tensor(v3(hot[:, which, :]), v3(key[:, :]), bc(top[:, 7, :], EXPERTS), ALU.is_equal))

            def c1(r, slot, parity, n):
                if r == 0:
                    dve.wait_ge(sem("c_sg1_done"), n)
                    dve.scalar_tensor_tensor(T["s1"][:, :], cbank["z1"][:, :], npar[:, 2 * C:2 * C + 1],
                                             T["sg1"][:, :], ALU.add, ALU.mult).then_inc(cread("z1"), 1)
                    dve.wait_ge(cread("z1"), n)
                    dve.tensor_tensor(T["k1"][:, :], q_all[:, bass.ds(slot, 1), :].rearrange("p a n -> p (a n)"),
                                      T["s1"][:, :], ALU.add).then_inc(sem("c_k1_done"), 1)
                if r == 1:
                    dve.wait_ge(sem("c_sg2_done"), n)
                    dve.scalar_tensor_tensor(T["s2"][:, :], cbank["z2"][:, :], npar[:, 2 * C + 1:2 * C + 2],
                                             T["sg2"][:, :], ALU.add, ALU.mult).then_inc(cread("z2"), 1)
                    dve.wait_ge(cread("z2"), n)
                    dve.tensor_tensor(T["res"][:, :], T["k1"][:, :], T["s2"][:, :], ALU.add
                                      ).then_inc(sem("c_res_done"), 1)
                if r == 2:
                    dve.wait_ge(cmade("rt"), n)
                    dve.tensor_tensor(h2[:, parity, :], h_all[:, bass.ds(slot, 1), :].rearrange("p a n -> p (a n)"),
                                      cbank["rt"][:, :], ALU.add).then_inc(cread("rt"), 1)
                    dve.wait_ge(cread("rt"), n)
                    link(dve.tensor_reduce(stat[:, 0, :], chunked(h2[:, parity, :]), AX, ALU.add))
                    dve.tensor_scalar(stat[:, 1, :], stat[:, 0, :], -1.0 / C, None, ALU.mult
                                      ).then_inc(sem("mean_done"), 1)
                if r == 3:
                    rsqrt_tokens(n + SLOTS)
                if r == 6:
                    dve.wait_ge(cmade("lg"), n)
                    dve.tensor_tensor(lg[:, :], cbank["lg"][:, 0:NE], par("rb2"), ALU.add).then_inc(cread("lg"), 1)
                    dve.wait_ge(cread("lg"), n)
                    link(dve.tensor_reduce(top[:, 0, :], v3(lg[:, :]), AX, ALU.max))
                    dve.tensor_tensor(v3(lg[:, :]), v3(lg[:, :]), bc(top[:, 0, :], EXPERTS), ALU.subtract
                                      ).then_inc(sem("c_lgx_done"), 1)
                if r == 7:
                    dve.wait_ge(sem("c_exp_done"), n)
                    link(dve.tensor_reduce(top[:, 0, :], v3(pe_[:, :]), AX, ALU.add))
                    link(dve.reciprocal(top[:, 1, :], top[:, 0, :]))
                    link(dve.tensor_tensor(v3(prb[:, :]), v3(pe_[:, :]), bc(top[:, 1, :], EXPERTS), ALU.mult))
                    pick(0, prb[:, :], top[:, 2, :])
                    link(dve.scalar_tensor_tensor(prb[:, :], hot[:, 0, :], -4.0, prb[:, :], ALU.mult, ALU.add))
                    pick(1, prb[:, :], top[:, 3, :])
                    dve.tensor_tensor(top[:, 4, :], top[:, 3, :], top[:, 2, :], ALU.subtract
                                      ).then_inc(sem("c_gap_done"), 1)
                    dve.wait_ge(sem("c_gape_done"), n)
                    link(dve.tensor_scalar(top[:, 6, :], top[:, 5, :], 1.0, None, ALU.add))
                    link(dve.reciprocal(top[:, 6, :], top[:, 6, :]))
                    link(dve.tensor_tensor(top[:, 5, :], top[:, 5, :], top[:, 6, :], ALU.mult))
                    step(dve.tensor_tensor(v3(hot[:, 0, :]), v3(hot[:, 0, :]), bc(top[:, 6, :], EXPERTS), ALU.mult))
                    link(dve.tensor_tensor(v3(hot[:, 1, :]), v3(hot[:, 1, :]), bc(top[:, 5, :], EXPERTS), ALU.mult))
                    link(dve.tensor_tensor(rout[:, :], hot[:, 0, :], hot[:, 1, :], ALU.add))
                    part = lambda k: rout3[:, :, k * EXPERTS:(k + 1) * EXPERTS]
                    link(dve.tensor_copy(part(0), v3(rout[:, :])))
                    link(dve.tensor_tensor(v3(rest[:, :]), v3(rout[:, :]), part(0), ALU.subtract))
                    link(dve.tensor_copy(part(1), v3(rest[:, :])))
                    dve.tensor_tensor(part(2), v3(rest[:, :]), part(1), ALU.subtract).then_inc(sem("c_rout_done"), 1)

            def one_slot(s, parity, more):
                dve.sem_clear(s_dve)
                steps[0] = 0
                c1n = s + (PRIME + 2)
                units = s * UNITS + PRIME
                for m in range(UNITS + 2):
                    if 1 <= m <= UNITS:
                        k = m - 1
                        dve.wait_ge(e2_done, units + (k + 1))
                        dve.wait_ge(r_made, units + (k + 1))
                        dve.wait_ge(l3_made, units + (k - 1))
                        dve.tensor_tensor(e2r[:, k % 2, :], e2[:, k % 2, :], r_bank[:, :], ALU.mult
                                          ).then_inc(e2r_done, 1)
                    if more:
                        c1(m, s + 1, 1 - parity, c1n)
                dve.wait_ge(l3_made, units + UNITS)
                dve.wait_ge(stored[parity], (s - parity) * 8 + 16)
                dve.tensor_tensor(y[:, parity, :], h2[:, parity, :], y_bank[:, :], ALU.add).then_inc(y_done, 1)
                sync()

            for r in range(UNITS + 2):
                c1(r, 0, 0, PRIME + 1)
            slots_loop(dve, one_slot)

        block = ctx.enter_context(nc.Block())

        @block.sync
        def _(sp):
            sp.dma_start(w_early[:, :], early).then_inc(params_in, 16)
            sp.dma_start(xref[:, :, :, :].rearrange("p k n c -> p (k n c)"), x_ref[0]).then_inc(ref_in, 16)
            sp.dma_start(txt_i[:, :], txt_idx).then_inc(txt_in, 16)
            sp.dma_start(w_late[:, :], late).then_inc(late_in, 16)
            for s in ([ref_used, rows_a, rows_b, issued_a, issued_b, weighed, summed, smp_copied, kv_made,
                       qry_moved] + [made(n) for n in AUX] + [read(n) for n in AUX]
                      + [sem(n) for n in ("gelu_arg", "gelu_tanh", "gelu_done", "mean_done", "var_done", "rstd_done",
                                          "normed", "sg1_done", "k1_done", "sg2_done", "dz2_done", "dz1_done")]):
                sp.sem_inc(s, PRIME)
            for s in (keys_read, scored, exped, sem("grads_added")):
                sp.sem_inc(s, PRIME - 1)
            sp.sem_inc(attended, PRIME - 2)
            for s in PHASE3_SEMS:
                sp.sem_inc(s, PRIME)
            for s in stored:
                sp.sem_inc(s, 16)
            with sp.Fori(0, IMAGES) as i:
                sp.wait_ge(ref_used, i + (PRIME + 1))
                sp.dma_start(xref[:, :, :, :].rearrange("p k n c -> p (k n c)"),
                             x_ref[bass.ds(i + 1, 1)].rearrange("a p n -> (a p) n")).then_inc(ref_in, 16)
            phase3_sync(sp)

        @block.gpsimd
        def _(pool):
            def gather(dst, table, index, done, index_used=None):
                pool.indirect_dma_start(dst, None, table, bass.IndirectOffsetOnAxis(ap=index.bitcast(U32), axis=0),
                                        engine_sem=index_used).then_inc(done, 16)

            pool.wait_ge(txt_in, 16)
            pool.wait_ge(rows_txt, 1)
            for j in range(TXT_CHUNKS):
                gather(txt_cat[:, j, 0:C], txt_table, txt_row[:, j:j + 1], txt_gathered)
                gather(txt_cat[:, j, C:C + TYPE_DIM], type_table, txt_i[:, j:j + 1], txt_gathered)
            with pool.Fori(0, IMAGES) as i:
                for c in range(CHUNKS):
                    if c == 0:
                        pool.wait_ge(rows_a, i + (PRIME + 1))
                    if c == CHUNKS // 2:
                        pool.wait_ge(rows_b, i + (PRIME + 1))
                    pool.wait_ge(weighed, i * CHUNKS + (PRIME + c - RING + 1))
                    pool.sem_inc(sem("slots_taken"), 1)
                    for n in range(POINTS):
                        k = c * POINTS + n
                        used = {(3, 7): issued_a, (7, 7): issued_b}.get((c, n))
                        gather(gath[:, c % RING, n, :], x_pairs, row[:, k:k + 1], gathered[c % RING], used)

        @block.tensor
        def _(pe):
            ident = par("ident")

            def transpose4(dst, src, width=128):
                for j in range(PAIRS):
                    last = pe.transpose(dst[:, j * 128:(j + 1) * 128], src[:, j * width:j * width + 128], ident)
                return last

            def bank_free(name, order, now, before):
                user, same_turn = user_before(name, order)
                if same_turn:
                    pe.wait_ge(read(user), now(user))
                elif before is not None:
                    pe.wait_ge(read(user), before(user))

            def points_stage(name, order, now, before):
                def mm(dst, lhsT, rhs, **kw):
                    return pe.matmul(dst, lhsT, rhs, start=True, stop=True, **kw)
                bank_free(name, order, now, before)
                dst = bank_of[name]
                if name == "qf":
                    pe.wait_ge(ref_used, now("ref"))
                    for j in range(PAIRS):
                        for k in range(4):
                            last = pe.matmul(dst[:, j * 128:(j + 1) * 128],
                                             xrefw[:, k, 2 * j:2 * j + 2, :].rearrange("p a c -> p (a c)"),
                                             ident, is_transpose=True, start=(k == 0), stop=(k == 3))
                elif name == "qry":
                    pe.wait_ge(read("qf"), now("qf"))
                    for j in range(PAIRS):
                        last = mm(dst[:, j * 128:(j + 1) * 128], qfT[:, j * 128:(j + 1) * 128], par("wq2"))
                elif name == "off1":
                    for j in range(PAIRS):
                        last = mm(dst[:, j * 32:(j + 1) * 32], qfT[:, j * 128:(j + 1) * 128], par("wo1"))
                elif name == "og":
                    pe.wait_ge(sem("gelu_done"), now("g"))
                    last = pe.transpose(dst[:, 0:128], oh[:, :], ident)
                elif name == "off2":
                    pe.wait_ge(read("og"), now("og"))
                    last = mm(dst[:, 0:128], ogT[:, :], par("wo2"))
                last.then_inc(made(name), 1)

            def mlp_stage(name, order, now, before):
                def mm(w, src):
                    return pe.matmul(dst[:, :], w, src[:, :], start=True, stop=True)
                bank_free(name, order, now, before)
                dst = bank_of[name]
                if name == "u":
                    pe.wait_ge(sem("normed"), now("n"))
                    last = transpose4(dst, T["u"])
                elif name == "k0":
                    pe.wait_ge(read("u"), now("u"))
                    last = mm(par("mk"), T["uT"])
                elif name == "z1":
                    pe.wait_ge(read("k0"), now("k0"))
                    last = mm(par("mw1"), T["k0"])
                elif name == "v":
                    last = mm(par("mv"), T["uT"])
                elif name == "lr":
                    last = mm(par("mlr"), T["uT"])
                elif name == "z2":
                    pe.wait_ge(sem("k1_done"), now("k1"))
                    last = mm(par("mw2"), T["k1"])
                elif name == "q":
                    last = mm(par("mq"), T["uT"])
                elif name == "k1t":
                    last = transpose4(dst, T["k1"])
                elif name == "dz2t":
                    pe.wait_ge(sem("dz2_done"), now("dz2"))
                    last = transpose4(dst, T["dz2"])
                elif name == "dk":
                    last = mm(par("mw2t"), T["dz2"])
                elif name == "dz1t":
                    pe.wait_ge(sem("dz1_done"), now("dz1"))
                    last = transpose4(dst, T["dz1"])
                last.then_inc(made(name), 1)

            def gradients(n):
                pe.wait_ge(read("dz2t"), n)
                pe.wait_ge(read("dz1t"), n)
                for j in range(PAIRS):
                    cols = slice(j * 128, (j + 1) * 128)
                    kw = dict(start=False, stop=False, skip_group_check=True)
                    pe.matmul(b_g[:, 0:128], T["k1t"][:, cols], T["dz2t"][:, cols], **kw)
                    pe.matmul(b_g[:, 257:258], T["dz2t"][:, cols], ones[:, :], **kw)
                    pe.matmul(b_g[:, 128:256], T["u"][:, cols], T["dz1t"][:, cols], **kw)
                    last = pe.matmul(b_g[:, 256:257], T["dz1t"][:, cols], ones[:, :], **kw)
                last.then_inc(sem("grads_added"), 1)

            pe.wait_ge(params_in, 16)
            first = lambda name: PRIME + 1
            for name in AUX_Q:
                points_stage(name, AUX_Q, first, None)
            pe.wait_ge(late_in, 16)
            pe.wait_ge(sem("txt_cat_done"), 1)
            pe.wait_ge(txt_gathered, 32 * TXT_CHUNKS)
            pe.wait_ge(read("og"), PRIME + 1)
            pe.wait_ge(read("off2"), PRIME + 1)
            for j in range(TXT_CHUNKS):
                last = pe.transpose(b_aux[j // 4][0:CAT, (j % 4) * 128:(j % 4) * 128 + 128], txt_cat[:, j, :], ident)
            last.then_inc(made("txt_t"), 1)
            pe.wait_ge(read("txt_t"), 1)
            for j in range(TXT_CHUNKS):
                last = pe.matmul(b_aux[0][:, j * C:(j + 1) * C], T["s1" if j == 4 else "k1"][0:CAT, (j % 4) * 128:(j % 4) * 128 + 128],
                                 par("txtw", CAT), start=True, stop=True)
            last.then_inc(made("txt_p"), 1)
            pe.wait_ge(read("txt_p"), 1)
            pe.matmul(b_g[:, 0:258], T["dz1t"][:, 0:128], T["dz2t"][:, 0:258], start=True, stop=False,
                      skip_group_check=True)

            with pe.Fori(0, IMAGES) as i:
                def now(name):
                    ahead = name in AUX_Q or name in ("ref", "g")
                    return i + (PRIME + (2 if ahead else 1))

                def before(name):
                    return i + PRIME

                def sum_corners(c):
                    pe.wait_ge(weighed, i * CHUNKS + (PRIME + c + 1))
                    pe.wait_ge(smp_copied, i * CHUNKS + (PRIME + c))
                    for j in range(PAIRS):
                        for k in range(4):
                            last = pe.matmul(b_smp[:, j * 128:(j + 1) * 128],
                                             gathw[:, c % 2, k, j * 128:(j + 1) * 128], ident,
                                             is_transpose=True, start=(k == 0), stop=(k == 3))
                    last.then_inc(summed, 1)

                def keys_values(c):
                    pe.wait_ge(smp_copied, i * CHUNKS + (PRIME + c + 1))
                    pe.wait_ge(keys_read, i * CHUNKS + (PRIME + c))
                    pe.wait_ge(attended, i * CHUNKS + (PRIME + c - 1))
                    for j in range(PAIRS):
                        cols = slice(j * 128, (j + 1) * 128)
                        pe.matmul(b_k[:, cols], smpT[:, c % 2, cols], par("wk2"), start=True, stop=True)
                        last = pe.matmul(b_v[c % 2][:, cols], smpT[:, c % 2, cols], par("wv2"), start=True, stop=True)
                    last.then_inc(kv_made, 1)

                EARLIER = {1: ["qf"], 3: ["u"], 4: ["off2", "z1"], 6: ["k1t"], 7: ["dz2t", "dk"]}
                LATER = {1: ["qry", "off1"], 3: ["og", "k0"], 4: ["v", "lr"], 5: ["z2", "q"], 7: ["dz1t"]}
                for r in range(CHUNKS):
                    sum_corners(r)
                    if r == 0:
                        gradients(i + PRIME)
                    for name in EARLIER.get(r, []):
                        (points_stage if name in AUX_Q else mlp_stage)(name, AUX, now, before)
                    keys_values(r)
                    for name in LATER.get(r, []):
                        (points_stage if name in AUX_Q else mlp_stage)(name, AUX, now, before)

            gradients(PRIME + IMAGES)
            last_now = lambda name: PRIME + IMAGES + 1
            for name in AUX_B:
                mlp_stage(name, AUX_B, last_now, lambda name: PRIME + IMAGES)
            gradients(PRIME + IMAGES + 1)
            phase23_tensor(pe)

        @block.scalar
        def _(act):
            chain = [0]

            def link(ins):
                chain[0] += 1
                ins.then_inc(s_act, 1)
                act.wait_ge(s_act, chain[0])

            def copy(dst, src):
                return act.activation(dst, src, ACT.Identity)

            def sigmoid(sg, src, half_bias):
                link(act.activation(sg, src, ACT.Tanh, bias=half_bias, scale=0.5))
                return act.activation(sg, sg, ACT.Copy, bias=0.5, scale=0.5)

            def moved(dst, name, now):
                act.wait_ge(made(name), now(name))
                copy(dst, bank_of[name][:, 0:dst.shape[1]]).then_inc(read(name), 1)

            def squares(slot_ap, now):
                act.wait_ge(sem("mean_done"), now("m"))
                for c in range(CHUNKS):
                    ins = act.activation(T["sq"][:, c * C:(c + 1) * C], slot_ap[:, c * C:(c + 1) * C], ACT.Square,
                                         bias=stat[:, 1, c:c + 1], accum_out=var[:, 0, c:c + 1])
                ins.then_inc(sem("var_done"), 1)

            def normalise(dst, src, n):
                act.wait_ge(sem("rstd_done"), n)
                act.sem_inc(sem("normalise_started"), 1)
                for c in range(CHUNKS):
                    ins = act.activation(dst[:, c * C:(c + 1) * C], src[:, c * C:(c + 1) * C], ACT.Identity,
                                         bias=stat[:, 3, c:c + 1], scale=rstd[:, 0, c:c + 1])
                ins.then_inc(sem("normed"), 1)

            def mlp_part(part, now, slot_ap, q_ap):
                if part == "squares":
                    squares(slot_ap, now)
                if part == "normalise":
                    act.wait_ge(sem("grads_added"), now("grads_before"))
                    normalise(T["u"], slot_ap, now("rstd"))
                if part == "sg1":
                    act.wait_ge(made("z1"), now("z1"))
                    sigmoid(T["sg1"][:, :], bank_of["z1"][:, :], hb[:, 0:1]).then_inc(sem("sg1_done"), 1)
                if part == "sg2":
                    act.wait_ge(made("z2"), now("z2"))
                    sigmoid(T["sg2"][:, :], bank_of["z2"][:, :], hb[:, 1:2]).then_inc(sem("sg2_done"), 1)
                if part == "lr":
                    act.wait_ge(made("lr"), now("lr"))
                    act.activation(T["lr"][:, :], bank_of["lr"][:, :], ACT.Tanh, bias=hb[:, 2:3], scale=0.5
                                   ).then_inc(read("lr"), 1)
                if part == "q":
                    act.wait_ge(made("q"), now("q"))
                    copy(q_ap, bank_of["q"][:, :]).then_inc(read("q"), 1)
                if part == "u":
                    moved(T["uT"][:, :], "u", now)
                if part in ("k0", "k1t", "dz2t", "dz1t"):
                    moved(T[part][:, :], part, now)

            def points_part(part, now):
                if part == "qf":
                    moved(qfT[:, :], "qf", now)
                if part == "qry":
                    moved(qry_next[:, :], "qry", now)
                if part == "gelu":
                    act.wait_ge(sem("gelu_arg"), now("a"))
                    act.activation(otanh[:, :], ot[:, :], ACT.Tanh, scale=GELU_C).then_inc(sem("gelu_tanh"), 1)
                if part == "og":
                    moved(ogT[:, :], "og", now)

            first = lambda name: PRIME + 1
            act.wait_ge(params_in, 16)
            for part in ("qf", "qry", "gelu", "og"):
                points_part(part, first)
            act.wait_ge(made("txt_t"), 1)
            copy(T["k1"][0:CAT, 0:512], b_aux[0][0:CAT, :])
            copy(T["s1"][0:CAT, 0:128], b_aux[1][0:CAT, 0:128]).then_inc(read("txt_t"), 1)
            act.wait_ge(late_in, 16)
            link(act.activation(hb[:, 0:2], par("par")[:, 2 * C:2 * C + 2], ACT.Copy, scale=0.5))
            link(act.activation(hb[:, 2:3], par("blr"), ACT.Copy, scale=0.5))

            with act.Fori(0, IMAGES) as i:
                act.sem_clear(s_act)
                chain[0] = 0
                def now(name):
                    return i + (PRIME + (2 if name in AUX_Q or name == "a" else 0 if name == "grads_before" else 1))

                EARLIER = {2: ["squares"], 3: ["gelu", "normalise"], 4: ["k0"], 5: ["lr"], 6: ["sg2", "q"]}
                LATER = {1: ["qf", "qry"], 3: ["u", "og"], 4: ["sg1"], 6: ["k1t"], 7: ["dz2t", "dz1t"]}

                def parts(names):
                    for part in names:
                        if part in ("qf", "qry", "gelu", "og"):
                            points_part(part, now)
                        else:
                            mlp_part(part, now, h_all[:, bass.ds(i, 1), :].rearrange("p a n -> p (a n)"),
                                     q_all[:, bass.ds(i, 1), :].rearrange("p a n -> p (a n)"))

                for r in range(CHUNKS):
                    parts(EARLIER.get(r, []))
                    act.wait_ge(summed, i * CHUNKS + (PRIME + r + 1))
                    act.wait_ge(kv_made, i * CHUNKS + (PRIME + r - 1))
                    copy(smpT[:, r % 2, :], b_smp[:, :]).then_inc(smp_copied, 1)
                    c = (r - 1) % CHUNKS
                    act.wait_ge(scored, i * CHUNKS + (PRIME + r))
                    act.activation(prob[:, c % 2, :, :], score[:, c % 2, :, :], ACT.Exp, scale=DH ** -0.5
                                   ).then_inc(exped, 1)
                    if r == 0:
                        act.wait_ge(read("qry"), i + (PRIME + 1))
                        copy(qry[:, :], qry_next[:, :]).then_inc(qry_moved, 1)
                    parts(LATER.get(r, []))
                    if r == 7:
                        act.activation(par("lossw"), par("lossw"), ACT.Copy, bias=MAX_ALR / C, scale=0.0
                                       ).then_inc(sem("lossw_set"), 1)
            act.sem_clear(s_act)
            chain[0] = 0
            act.wait_ge(scored, IMAGES * CHUNKS + PRIME)
            act.activation(prob[:, 1, :, :], score[:, 1, :, :], ACT.Exp, scale=DH ** -0.5).then_inc(exped, 1)
            last_now = lambda name: PRIME + IMAGES + (0 if name == "grads_before" else 1)
            for part in ("squares", "normalise", "u", "k0", "sg1", "lr", "sg2", "q", "k1t", "dz2t", "dz1t"):
                mlp_part(part, last_now, h_all[:, IMAGES, :], q_all[:, IMAGES, :])
            phase3_scalar(act, chain, link, copy, sigmoid, normalise)

        @block.vector
        def _(dve):
            steps = [0]

            def step(ins):
                steps[0] += 1
                ins.then_inc(s_dve, 1)
                return steps[0]

            def sync():
                dve.wait_ge(s_dve, steps[0])

            def link(ins):
                step(ins)
                sync()

            def bc(ap, n):
                return ap.unsqueeze(len(ap.shape)).broadcast_to(list(ap.shape) + [n])

            def chunked(ap):
                return ap.rearrange("p (n c) -> p n c", n=CHUNKS)

            def rsqrt():
                v, y, t = (x[:, :, :].rearrange("p a n -> p (a n)") for x in (var, rstd, newton))
                s = seed[:, :, :].rearrange("p a n -> p (a n)")
                link(dve.tensor_scalar(s, v.bitcast(I32), 1, None, ALU.logical_shift_right))
                link(dve.tensor_scalar(y.bitcast(I32), s, -1.0, RSQRT_SEED, ALU.mult, ALU.add))
                for _ in range(3):
                    link(dve.scalar_tensor_tensor(t, y, -0.5, v, ALU.mult, ALU.mult))
                    link(dve.tensor_tensor(t, t, y, ALU.mult))
                    link(dve.scalar_tensor_tensor(y, t, 1.5, y, ALU.add, ALU.mult))

            def rsqrt_tokens(n):
                dve.wait_ge(sem("var_done"), n)
                link(dve.tensor_scalar(var[:, 0, :], var[:, 0, :], 1.0 / C, LN_EPS, ALU.mult, ALU.add))
                rsqrt()
                dve.tensor_tensor(stat[:, 3, :], stat[:, 1, :], rstd[:, 0, :], ALU.mult).then_inc(sem("rstd_done"), 1)

            def weigh_reference(now):
                dve.tensor_tensor(xrefw[:, :, :, :].rearrange("p k n c -> p (k n) c"),
                                  xref[:, :, :, :].rearrange("p k n c -> p (k n) c"),
                                  bc(par("refw"), C), ALU.mult).then_inc(ref_used, 1)

            def points_round(r, now, tokens):
                if r == 2:
                    hv = oh[:, :].rearrange("p (n k) -> p n k", n=CHUNKS)
                    tv = ot[:, :].rearrange("p (n k) -> p n k", n=CHUNKS)
                    dve.wait_ge(made("off1"), now("off1"))
                    dve.tensor_tensor(oh[:, :], bank_of["off1"][:, 0:128], par("bo1"), ALU.add).then_inc(read("off1"), 1)
                    dve.wait_ge(read("off1"), now("off1"))
                    link(dve.tensor_reduce(stat[:, 4, :], hv, AX, ALU.add))
                    link(dve.tensor_scalar(stat[:, 4, :], stat[:, 4, :], -1.0 / HID, None, ALU.mult))
                    link(dve.tensor_tensor(hv, hv, bc(stat[:, 4, :], HID), ALU.add))
                    link(dve.tensor_tensor(ot[:, :], oh[:, :], oh[:, :], ALU.mult))
                    link(dve.tensor_reduce(stat[:, 5, :], tv, AX, ALU.add))
                    link(dve.tensor_scalar(var[:, 1, :], stat[:, 5, :], 1.0 / HID, LN_EPS, ALU.mult, ALU.add))
                    if tokens is not None:
                        rsqrt_tokens(tokens)
                    else:
                        rsqrt()
                    link(dve.tensor_tensor(hv, hv, bc(rstd[:, 1, :], HID), ALU.mult))
                    link(dve.tensor_tensor(oh[:, :], oh[:, :], par("lng"), ALU.mult))
                    link(dve.tensor_tensor(oh[:, :], oh[:, :], par("lnb"), ALU.add))
                    link(dve.tensor_tensor(ot[:, :], oh[:, :], oh[:, :], ALU.mult))
                    link(dve.tensor_scalar(ot[:, :], ot[:, :], GELU_A, 1.0, ALU.mult, ALU.add))
                    dve.tensor_tensor(ot[:, :], ot[:, :], oh[:, :], ALU.mult).then_inc(sem("gelu_arg"), 1)
                if r == 3:
                    dve.wait_ge(sem("gelu_tanh"), now("t"))
                    dve.scalar_tensor_tensor(oh[:, :], otanh[:, :], 1.0, oh[:, :], ALU.add, ALU.mult
                                             ).then_inc(sem("gelu_done"), 1)
                if r == 4:
                    pv = px[:, :, :].rearrange("p n a -> p (n a)")
                    cv = corner[:, :, :].rearrange("p n a -> p (n a)")
                    dve.wait_ge(made("off2"), now("off2"))
                    dve.scalar_tensor_tensor(pv, bank_of["off2"][:, 0:128], 2.0,
                                             refb[:, :, :, :].rearrange("p n m a -> p (n m a)"),
                                             ALU.mult, ALU.add).then_inc(read("off2"), 1)
                    dve.wait_ge(read("off2"), now("off2"))
                    link(dve.tensor_scalar(pv, pv, 0.0, float(W - 1), ALU.max, ALU.min))
                    link(dve.tensor_scalar(cv, pv, ROUND - 0.5, ROUND, ALU.add, ALU.subtract))
                    link(dve.tensor_scalar(cv, cv, 0.0, float(W - 2), ALU.max, ALU.min))
                    f1 = frac[:, 1, :, :].rearrange("p n a -> p (n a)")
                    link(dve.tensor_tensor(f1, pv, cv, ALU.subtract))
                    link(dve.tensor_scalar(frac[:, 0, :, :].rearrange("p n a -> p (n a)"), f1, -1.0, 1.0,
                                           ALU.mult, ALU.add))
                    for dx in range(2):
                        step(dve.tensor_tensor(wts_next[:, :, dx, :].rearrange("p n b -> p b n"),
                                               frac[:, dx:dx + 1, :, 0].broadcast_to([P, 2, CHUNKS * POINTS]),
                                               frac[:, :, :, 1], ALU.mult))
                    step(dve.scalar_tensor_tensor(row_next[:, :], corner[:, :, 1], float(W), corner[:, :, 0],
                                                  ALU.mult, ALU.add))

            def rows_live(half, now):
                cols = slice(half * 32, half * 32 + 32)
                dve.tensor_scalar(row[:, cols], row_next[:, cols], row_base[:, 0:1], None, ALU.add
                                  ).then_inc((rows_a, rows_b)[half], 1)

            def mlp_round(r, now, slot_ap):
                if r == 1:
                    link(dve.tensor_reduce(stat[:, 0, :], chunked(slot_ap), AX, ALU.add))
                    dve.tensor_scalar(stat[:, 1, :], stat[:, 0, :], -1.0 / C, None, ALU.mult).then_inc(sem("mean_done"), 1)
                if r == 5:
                    dve.wait_ge(sem("sg1_done"), now("z1"))
                    dve.scalar_tensor_tensor(T["s1"][:, :], bank_of["z1"][:, :], par("par")[:, 2 * C:2 * C + 1],
                                             T["sg1"][:, :], ALU.add, ALU.mult).then_inc(read("z1"), 1)
                    dve.wait_ge(read("z1"), now("z1"))
                    dve.tensor_tensor(T["k1"][:, :], T["k0"][:, :], T["s1"][:, :], ALU.add).then_inc(sem("k1_done"), 1)
                    link(dve.scalar_tensor_tensor(T["d1"][:, :], T["s1"][:, :], 1.0, T["sg1"][:, :],
                                                  ALU.subtract, ALU.mult))
                    step(dve.tensor_tensor(T["d1"][:, :], T["s1"][:, :], T["d1"][:, :], ALU.subtract))
                    dve.wait_ge(made("v"), now("v"))
                    dve.wait_ge(sem("k1_done"), now("k1"))
                    dve.tensor_tensor(T["res"][:, :], T["k1"][:, :], bank_of["v"][:, :], ALU.subtract
                                      ).then_inc(read("v"), 1)
                if r == 6:
                    dve.wait_ge(read("lr"), now("lr"))
                    step(dve.scalar_tensor_tensor(T["dp"][:, :], T["lr"][:, :], 1.0, par("lossw"), ALU.add, ALU.mult))
                    dve.wait_ge(sem("sg2_done"), now("z2"))
                    dve.scalar_tensor_tensor(T["s2"][:, :], bank_of["z2"][:, :], par("par")[:, 2 * C + 1:2 * C + 2],
                                             T["sg2"][:, :], ALU.add, ALU.mult).then_inc(read("z2"), 1)
                    dve.wait_ge(read("z2"), now("z2"))
                    dve.wait_ge(read("v"), now("v"))
                    step(dve.scalar_tensor_tensor(T["d2"][:, :], T["s2"][:, :], 1.0, T["sg2"][:, :],
                                                  ALU.subtract, ALU.mult))
                    step(dve.tensor_tensor(T["res"][:, :], T["res"][:, :], T["s2"][:, :], ALU.add))
                    sync()
                    step(dve.tensor_tensor(T["d2"][:, :], T["s2"][:, :], T["d2"][:, :], ALU.subtract))
                    step(dve.tensor_tensor(T["dp"][:, :], T["dp"][:, :], T["res"][:, :], ALU.mult))
                    sync()
                    dve.tensor_tensor(T["dz2"][:, :], T["dp"][:, :], T["d2"][:, :], ALU.mult).then_inc(sem("dz2_done"), 1)
                if r == 7:
                    dve.wait_ge(made("dk"), now("dk"))
                    dve.tensor_tensor(T["dp"][:, :], T["dp"][:, :], bank_of["dk"][:, :], ALU.add
                                      ).then_inc(read("dk"), 1)
                    dve.wait_ge(read("dk"), now("dk"))
                    dve.tensor_tensor(T["dz1"][:, :], T["dp"][:, :], T["d1"][:, :], ALU.mult).then_inc(sem("dz1_done"), 1)

            def scores_and_attention(r, base, dst):
                c, a = (r - 1) % CHUNKS, (r - 2) % CHUNKS
                sc, pr = score[:, c % 2, :, :], prob[:, a % 2, :, :]
                if r <= CHUNKS:
                    dve.wait_ge(kv_made, base + r)
                    dve.tensor_tensor(qk[:, :].rearrange("p (n c) -> p n c", n=POINTS),
                                      b_k[:, :].rearrange("p (n c) -> p n c", n=POINTS),
                                      qry[:, c * C:(c + 1) * C].unsqueeze(1).broadcast_to([P, POINTS, C]), ALU.mult
                                      ).then_inc(keys_read, 1)
                dve.wait_ge(exped, base + (r - 1))
                total = step(dve.tensor_reduce(ha[:, 1, :], pr.rearrange("p n h -> p h n"), AX, ALU.add))
                weighed_values = step(dve.tensor_tensor(
                    av[:, :].rearrange("p (m d) -> p m d", d=DH),
                    b_v[a % 2][:, :].rearrange("p (m d) -> p m d", d=DH),
                    bc(pr.rearrange("p n h -> p (n h)"), DH), ALU.mult))
                if r <= CHUNKS:
                    dve.wait_ge(keys_read, base + r)
                    raw = step(dve.tensor_reduce(sc.rearrange("p n h -> p (n h)"),
                                                 qk[:, :].rearrange("p (m d) -> p m d", d=DH), AX, ALU.add))
                dve.wait_ge(s_dve, total)
                step(dve.reciprocal(ha[:, 2, :], ha[:, 1, :]))
                dve.wait_ge(s_dve, weighed_values)
                summed_values = step(dve.tensor_reduce(ho[:, :], av[:, :].rearrange("p (n c) -> p c n", n=POINTS),
                                                       AX, ALU.add))
                if r <= CHUNKS:
                    dve.wait_ge(s_dve, raw)
                    largest = step(dve.tensor_reduce(ha[:, 0, :], sc.rearrange("p n h -> p h n"), AX, ALU.max))
                dve.wait_ge(s_dve, summed_values)
                dve.tensor_tensor(dst[:, a * C:(a + 1) * C].rearrange("p (h d) -> p h d", d=DH),
                                  ho[:, :].rearrange("p (h d) -> p h d", d=DH),
                                  bc(ha[:, 2, :], DH), ALU.mult).then_inc(attended, 1)
                if r <= CHUNKS:
                    dve.wait_ge(s_dve, largest)
                    dve.tensor_tensor(sc, sc, ha[:, 0:1, :].broadcast_to([P, POINTS, HEADS]), ALU.subtract
                                      ).then_inc(scored, 1)

            first = lambda name: PRIME + 1
            step(dve.memset(ones[:, :], 1.0))
            step(dve.memset(row_base[:, :], 0.0))
            for name in ("k1t", "dz2t", "dz1t", "u"):
                step(dve.memset(T[name][:, :], 0.0))
            for tile in (b_k, b_v[0], b_v[1], qry, h_all[:, 0, :]):
                step(dve.memset(tile[:, :], 0.0))
            step(dve.memset(prob[:, :, :, :], 1.0))
            step(dve.memset(var[:, :, :], 1.0))
            dve.wait_ge(txt_in, 16)
            sync()
            dve.scalar_tensor_tensor(txt_row[:, :], txt_i[:, 0:TXT_CHUNKS], float(TXT_ROWS),
                                     txt_i[:, TXT_CHUNKS:2 * TXT_CHUNKS], ALU.mult, ALU.add).then_inc(rows_txt, 1)
            dve.wait_ge(params_in, 16)
            bo2 = par("bo2").rearrange("p (n m a) -> p n m a", n=CHUNKS, a=2)
            refpx = par("refpx").rearrange("p (n a) -> p n a", a=2)
            for n in range(CHUNKS):
                step(dve.scalar_tensor_tensor(refb[:, n, :, :], bo2[:, n, :, :], 4.0,
                                              refpx[:, n:n + 1, :].broadcast_to([P, POINTS, 2]), ALU.mult, ALU.add))
            sync()
            dve.wait_ge(ref_in, 16)
            weigh_reference(first)
            for r in range(2, 5):
                points_round(r, first, None)
            sync()
            rows_live(0, None)
            rows_live(1, None)
            dve.wait_ge(rows_b, PRIME + 1)
            link(dve.tensor_scalar(row_base[:, :], row_base[:, :], float(H * W), None, ALU.add))
            step(dve.tensor_copy(wts[:, :, :].rearrange("p n k -> p (n k)"),
                                 wts_next[:, :, :, :].rearrange("p n a b -> p (n a b)")))
            dve.wait_ge(late_in, 16)
            step(dve.tensor_scalar(txt_cat[:, :, C + TYPE_DIM], par("outc"), par("txts")[:, 0:1], None, ALU.mult))
            step(dve.tensor_scalar(txt_cat[:, :, C + TYPE_DIM + 1], par("dt"), par("txts")[:, 1:2], None, ALU.mult))
            dve.memset(txt_cat[:, :, CAT - 1:CAT], 1.0).then_inc(sem("txt_cat_done"), 1)
            nt = TXT_CHUNKS
            tx = T["res"][:, 0:nt * C].rearrange("p (n c) -> p n c", n=nt)
            ty = T["sq"][:, 0:nt * C].rearrange("p (n c) -> p n c", n=nt)
            proj = b_aux[0][:, 0:nt * C].rearrange("p (n c) -> p n c", n=nt)
            dve.wait_ge(made("txt_p"), 1)
            link(dve.tensor_reduce(stat[:, 0, 0:nt], proj, AX, ALU.add))
            link(dve.tensor_scalar(stat[:, 1, 0:nt], stat[:, 0, 0:nt], -1.0 / C, None, ALU.mult))
            dve.tensor_tensor(tx, proj, bc(stat[:, 1, 0:nt], C), ALU.add).then_inc(read("txt_p"), 1)
            dve.wait_ge(read("txt_p"), 1)
            link(dve.tensor_tensor(ty, tx, tx, ALU.mult))
            link(dve.tensor_reduce(var[:, 0, 0:nt], ty, AX, ALU.add))
            link(dve.tensor_scalar(var[:, 0, :], var[:, 0, :], 1.0 / C, LN_EPS, ALU.mult, ALU.add))
            rsqrt()
            link(dve.tensor_tensor(tx, tx, bc(rstd[:, 0, 0:nt], C), ALU.mult))
            link(dve.tensor_tensor(tx, tx, par("txtg").unsqueeze(1).broadcast_to([P, nt, C]), ALU.mult))
            link(dve.tensor_tensor(h_all[:, 0, 0:nt * C].rearrange("p (n c) -> p n c", n=nt), tx,
                                   par("txtb").unsqueeze(1).broadcast_to([P, nt, C]), ALU.add))

            with dve.Fori(0, IMAGES) as i:
                dve.sem_clear(s_dve)
                steps[0] = 0
                ahead = AUX_Q + ["t", "a", "g", "ref"]
                now = lambda name: i + (PRIME + (2 if name in ahead else 1))
                slot = lambda k: h_all[:, bass.ds(k, 1), :].rearrange("p a n -> p (a n)")

                def weigh(c):
                    if c < RING:
                        dve.wait_ge(gathered[c], i * (2 * 16 * POINTS) + 16 * POINTS)
                    else:
                        dve.wait_ge(gathered[c % RING], i * (2 * 16 * POINTS) + 2 * 16 * POINTS)
                    dve.wait_ge(summed, i * CHUNKS + (PRIME + c - 1))
                    dve.tensor_tensor(gathw[:, c % 2, :, :].rearrange("p k (n c) -> p n k c", n=POINTS),
                                      gath[:, c % RING, :, :].rearrange("p n (k c) -> p n k c", k=4),
                                      bc(wts[:, c, :].rearrange("p (n k) -> p n k", k=4), C), ALU.mult
                                      ).then_inc(weighed, 1)

                for r in range(CHUNKS):
                    weigh(r)
                    if r == 1:
                        dve.wait_ge(qry_moved, i + (PRIME + 1))
                    scores_and_attention(r, i * CHUNKS + PRIME, slot(i) if r < 2 else slot(i + 1))
                    if r == 0:
                        dve.wait_ge(ref_in, i * 16 + 32)
                        dve.wait_ge(made("qf"), i + (PRIME + 1))
                        weigh_reference(now)
                    if r == 1:
                        dve.wait_ge(attended, i * CHUNKS + PRIME)
                    mlp_round(r, now, slot(i))
                    points_round(r, now, i + (PRIME + 1))
                    if r == 4:
                        dve.wait_ge(issued_a, i + (PRIME + 1))
                        sync()
                        rows_live(0, now)
                    if r == 7:
                        step(dve.tensor_copy(wts[:, :, :].rearrange("p n k -> p (n k)"),
                                             wts_next[:, :, :, :].rearrange("p n a b -> p (n a b)")))
                        dve.wait_ge(issued_b, i + (PRIME + 1))
                        rows_live(1, now)
                        dve.wait_ge(rows_b, i + (PRIME + 2))
                        step(dve.tensor_scalar(row_base[:, :], row_base[:, :], float(H * W), None, ALU.add))
                sync()
            dve.sem_clear(s_dve)
            steps[0] = 0
            for r in range(CHUNKS, CHUNKS + 2):
                scores_and_attention(r, (IMAGES - 1) * CHUNKS + PRIME, h_all[:, IMAGES, :])
            dve.wait_ge(attended, IMAGES * CHUNKS + PRIME)
            last_now = lambda name: PRIME + IMAGES + 1
            mlp_round(1, last_now, h_all[:, IMAGES, :])
            rsqrt_tokens(PRIME + IMAGES + 1)
            for r in range(5, 8):
                mlp_round(r, last_now, h_all[:, IMAGES, :])
            phase23_vector(dve, steps, step, sync, link, bc, chunked, rsqrt_tokens)


def blocks(ms):
    out = np.zeros((sum(m.shape[0] for m in ms), sum(m.shape[1] for m in ms)), np.float32)
    r = c = 0
    for m in ms:
        out[r:r + m.shape[0], c:c + m.shape[1]] = m
        r, c = r + m.shape[0], c + m.shape[1]
    return out


def kernel(**inputs):
    import concourse.bacc as _bacc
    from concourse.bass_utils import run_bass_kernel_spmd as _run

    a = {k: np.asarray(v) for k, v in inputs.items()}
    tok = {k[7:]: v for k, v in a.items() if k.startswith("L0_tok_")}
    txt = {k[7:]: v for k, v in a.items() if k.startswith("L0_txt_")}
    mem = {k[8:]: v for k, v in a.items() if k.startswith("L0_attn_")}
    ffn = {k[7:]: v for k, v in a.items() if k.startswith("L0_ffn_")}

    def rows(v, n=P):
        return np.broadcast_to(v.reshape(1, -1), (n, v.size))

    def pack(entries, parts):
        where, total = columns(entries)
        out = np.zeros((P, total), np.float32)
        for name, m in parts.items():
            at, n = where[name]
            assert m.shape[1] == n, (name, m.shape, n)
            out[:m.shape[0], at:at + n] = m
        return out

    x = a["x"].transpose(0, 2, 3, 1)
    below = np.concatenate([x[:, 1:], np.zeros_like(x[:, :1])], axis=1)
    x_pairs = np.ascontiguousarray(np.stack([x, below], axis=3)).reshape(IMAGES * H * W, 2 * C)

    n = np.arange(P * CHUNKS).reshape(P, CHUNKS)
    grid = (np.linspace(-1.0, 1.0, GRID).astype(np.float32) + np.float32(1)) * np.float32(0.5) * np.float32(W - 1)
    rx, ry = grid[n % GRID], grid[n // GRID]
    x0 = np.clip(np.floor(rx), 0, W - 2).astype(np.int64)
    y0 = np.clip(np.floor(ry), 0, H - 2).astype(np.int64)
    fx, fy = rx - x0, ry - y0
    refw = np.stack([wx * wy for wx in (1 - fx, fx) for wy in (1 - fy, fy)], axis=1)
    corners = np.stack([x[:, y0 + dy, x0 + dx] for dx in (0, 1) for dy in (0, 1)], axis=2)
    x_ref = np.concatenate([corners, np.zeros_like(corners[:1])]).reshape(IMAGES + 1, P, 4 * COLS)

    eye = np.eye(P, dtype=np.float32)
    early = pack(EARLY, {
        "ident": eye, "wq2": blocks([tok["W_q"].T] * 2), "wo1": blocks([tok["W_o1"]] * 2),
        "wo2": blocks([tok["W_o2"]] * CHUNKS), "wk2": blocks([tok["W_k"].T] * 2), "wv2": blocks([tok["W_v"].T] * 2),
        "bo1": rows(np.tile(tok["b_o1"], CHUNKS)), "lng": rows(np.tile(tok["ln_g"], CHUNKS)),
        "lnb": rows(np.tile(tok["ln_b"], CHUNKS)), "bo2": rows(np.tile(tok["b_o2"], CHUNKS)),
        "refw": refw.reshape(P, 32), "refpx": np.stack([rx, ry], axis=2).reshape(P, 16)})

    def per_token(v):
        flat = v.reshape(-1)
        return np.concatenate([flat, np.zeros(P * TXT_CHUNKS - flat.size, flat.dtype)]).reshape(P, TXT_CHUNKS)

    chunk = np.arange(CHUNKS)[None]
    live = (chunk < TXT_CHUNKS) & (np.arange(P)[:, None] * TXT_CHUNKS + chunk < TXT_B * TXT_L)
    live = live.reshape(P, PAIRS, 2).transpose(2, 1, 0).reshape(2, 1, COLS)
    lossw = np.broadcast_to(live, (2, C, COLS)).reshape(P, COLS) * np.float32(MAX_ALR / C)
    half = np.kron(np.eye(2), np.ones((C, C)))
    experts = range(EPAIRS)
    sel = np.zeros((18, EPAIRS * P), np.float32)
    for p in experts:
        for e in range(2):
            sel[[2 * p + e, 6 + 2 * p + e, 12 + 2 * p + e], p * P + e * C:p * P + (e + 1) * C] = 1
    w1, w2, w3 = ffn["expert_w1"], ffn["expert_w2"], ffn["expert_w3"]
    col = lambda v: v.reshape(-1, 1)
    late = pack(LATE, {
        "mk": blocks([mem["Wk"]] * 2), "mv": blocks([mem["Wv"]] * 2), "mq": blocks([mem["Wq"]] * 2),
        "mlr": blocks([np.broadcast_to(mem["Wlr"], (C, C))] * 2),
        "mw1": blocks([mem["Ws"][0]] * 2), "mw2": blocks([mem["Ws"][1]] * 2), "mw2t": blocks([mem["Ws"][1].T] * 2),
        "mkrep": np.tile(mem["Wk"], (1, 2)),
        "par": np.tile(np.concatenate([mem["Ws"][0], mem["Ws"][1], col(mem["bs"][0]), col(mem["bs"][1])], axis=1), (2, 1)),
        "blr": rows(mem["blr"]), "stack": np.tile(np.eye(C, dtype=np.float32), (2, 2)),
        "gmask": np.tile(half.astype(np.float32), (1, 2)), "lossw": lossw,
        "rw1": blocks([ffn["router_w1"]] * 2), "rb1": col(np.tile(ffn["router_b1"], 2)),
        "rw2": blocks([ffn["router_w2"]] * 2), "rb2": rows(np.tile(ffn["router_b2"], CHUNKS)),
        "first": rows(np.tile(np.arange(EXPERTS, 0, -1).astype(np.float32), CHUNKS)),
        "ew1": np.tile(np.concatenate([w1[e] for e in range(EXPERTS)], axis=1), (2, 1)),
        "eb1": ffn["expert_b1"].reshape(EPAIRS, P).T,
        "ew2": np.concatenate([blocks([w2[2 * p], w2[2 * p + 1]]) for p in experts], axis=1),
        "eb2": ffn["expert_b2"].reshape(EPAIRS, P).T,
        "ew3": np.concatenate([w3[2 * p:2 * p + 2].reshape(P, C) for p in experts], axis=1),
        "eb3": blocks([ffn["expert_b3"]] * CHUNKS), "sel": sel,
        "txtw": np.concatenate([txt["W_proj_w"].T, txt["W_proj_b"].reshape(1, C)]),
        "txtg": rows(txt["ln_gamma"]), "txtb": rows(txt["ln_beta"]),
        "txts": rows(np.concatenate([txt["W_o"], txt["W_delta"]])),
        "outc": per_token(a["fside_BS_outcomes"]), "dt": per_token(a["fside_BS_delta_ts"])})
    txt_idx = np.concatenate([per_token(a["x_txt"].astype(np.int32)),
                              per_token(a["itok_BS_0_4999"].astype(np.int32))], axis=1)
    pad = lambda h: np.concatenate([h, np.zeros((TXT_ROWS - h.shape[0], C), np.float32)])
    table = np.concatenate([pad(txt["h_qa"]), pad(txt["h_v"]), pad(txt["h_r"])])

    arrays = {"x_pairs": x_pairs, "x_ref": x_ref, "early": early, "late": late, "txt_idx": txt_idx,
              "txt_table": table, "type_table": np.ascontiguousarray(txt["E_type_w"])}
    nc = _bacc.Bacc("TRN2", target_bir_lowering=False, num_devices=1)
    args = [nc.dram_tensor(k, v.shape, mybir.dt.from_np(v.dtype), kind="ExternalInput").ap() for k, v in arrays.items()]
    args.append(nc.dram_tensor("tokens_out", (SLOTS, P, COLS), F32, kind="ExternalOutput").ap())
    build(nc, *args)
    got = _run(nc, [arrays], core_ids=[0]).results[0]["tokens_out"]
    image = got[1:].reshape(IMAGES, P * CHUNKS, C)
    text = got[0][:, :TXT_CHUNKS * C].reshape(P * TXT_CHUNKS, C)[:TXT_B * TXT_L].reshape(TXT_B, TXT_L, C)
    return np.concatenate([image, text], axis=1)
```

```python
from contextlib import ExitStack

import concourse.bass as bass
import numpy as np
from concourse import mybir

F32 = mybir.dt.float32
BF16 = mybir.dt.bfloat16
I32 = mybir.dt.int32
U32 = mybir.dt.uint32
ALU = mybir.AluOpType
ACT = mybir.ActivationFunctionType
AX = mybir.AxisListType.X

P = 128
IMAGES, C, H, W = 8, 64, 128, 128
GRID = H // 4
CHUNKS = 8
POINTS = 8
HEADS = 8
DH = C // HEADS
HID = C // 4
SLOTS = IMAGES + 1
GROUP = 3
COLS = CHUNKS * C
PAIRS = CHUNKS // 2
TXT_B, TXT_L = 8, 77
TXT_CHUNKS = 5
TXT_ROWS = 5000
TYPE_DIM = 16
CAT = C + TYPE_DIM + 3
EXPERTS = 6
RH = 32
EPAIRS = EXPERTS // 2
LR, WD, MAX_ALR = 0.001, 0.01, 0.1
LN_EPS = 1e-5
RING = 4
PRIME = 8
GELU_C, GELU_A = 0.7978845608028654, 0.044715
ROUND = 8388608.0
RSQRT_SEED = 1597463007.0

EARLY = [("ident", 128), ("wq2", 128), ("wo1", 2 * HID), ("wo2", 128), ("wk2", 128), ("wv2", 128),
         ("bo1", 128), ("lng", 128), ("lnb", 128), ("bo2", 128), ("refw", 32), ("refpx", 16)]
LATE = [("mk", 128), ("mv", 128), ("mlr", 128), ("mq", 128), ("mw1", 128), ("mw2", 128), ("mw2t", 128),
        ("mkrep", 128), ("par", 2 * C + 2), ("blr", 1), ("stack", 128), ("gmask", 256), ("lossw", 512),
        ("rw1", 2 * RH), ("rb1", 1), ("rw2", 2 * EXPERTS), ("rb2", CHUNKS * EXPERTS), ("first", CHUNKS * EXPERTS),
        ("ew1", EPAIRS * 128), ("eb1", EPAIRS), ("ew2", EPAIRS * 128), ("eb2", EPAIRS), ("ew3", EPAIRS * C),
        ("eb3", COLS), ("sel", EPAIRS * 128), ("txtw", C), ("txtg", C), ("txtb", C), ("txts", 2),
        ("outc", TXT_CHUNKS), ("dt", TXT_CHUNKS)]


def columns(entries):
    at, where = 0, {}
    for name, n in entries:
        where[name] = (at, n)
        at += n
    return where, at


def build(nc, x_pairs, x_ref, early, late, txt_idx, txt_table, type_table, out):
    with ExitStack() as ctx:
        def sb(name, shape, dt=F32):
            return ctx.enter_context(nc.sbuf_tensor(name, shape, dt))

        def bank(name):
            return ctx.enter_context(nc.psum_tensor(name, [P, 512], F32))

        sems = {}

        def sem(name):
            if name not in sems:
                sems[name] = ctx.enter_context(nc.semaphore(name))
            return sems[name]

        w_early = sb("w_early", [P, columns(EARLY)[1]])
        w_late = sb("w_late", [P, columns(LATE)[1]])

        def par(name, rows=P):
            tile, entries = (w_early, EARLY) if name in dict(EARLY) else (w_late, LATE)
            at, n = columns(entries)[0][name]
            return tile[0:rows, at:at + n]

        txt_i = sb("txt_i", [P, 2 * TXT_CHUNKS], I32)
        txt_row = sb("txt_row", [P, TXT_CHUNKS], I32)
        txt_cat = sb("txt_cat", [P, TXT_CHUNKS, CAT])
        xref = sb("xref", [P, 4, CHUNKS, C])
        xrefw = sb("xrefw", [P, 4, CHUNKS, C])
        qfT = sb("qfT", [P, COLS])
        qry_next = sb("qry_next", [P, COLS])
        qry = sb("qry", [P, COLS])
        oh = sb("oh", [P, 128])
        ot = sb("ot", [P, 128])
        otanh = sb("otanh", [P, 128])
        ogT = sb("ogT", [P, 128])
        refb = sb("refb", [P, CHUNKS, POINTS, 2])
        px = sb("px", [P, CHUNKS * POINTS, 2])
        corner = sb("corner", [P, CHUNKS * POINTS, 2])
        frac = sb("frac", [P, 2, CHUNKS * POINTS, 2])
        wts_next = sb("wts_next", [P, CHUNKS * POINTS, 2, 2])
        wts = sb("wts", [P, CHUNKS, POINTS * 4])
        row_next = sb("row_next", [P, CHUNKS * POINTS])
        row_base = sb("row_base", [P, 1])
        row = sb("row", [P, CHUNKS * POINTS], I32)
        stat = sb("stat", [P, 8, CHUNKS])
        var = sb("var", [P, 2, CHUNKS])
        rstd = sb("rstd", [P, 2, CHUNKS])
        newton = sb("newton", [P, 2, CHUNKS])
        seed = sb("seed", [P, 2, CHUNKS], I32)
        gath = sb("gath", [P, RING, POINTS, 4 * C])
        gathw = sb("gathw", [P, 2, 4, POINTS * C])
        smpT = sb("smpT", [P, 2, 512])
        qk = sb("qk", [P, POINTS * C])
        score = sb("score", [P, 2, POINTS, HEADS])
        prob = sb("prob", [P, 2, POINTS, HEADS])
        av = sb("av", [P, POINTS * C])
        ha = sb("ha", [P, 4, HEADS])
        ho = sb("ho", [P, C])
        h_all = sb("h_all", [P, SLOTS, COLS])
        q_all = sb("q_all", [P, SLOTS, COLS])
        T = {n: sb("t_" + n, [P, COLS]) for n in
             "u uT k0 sg1 s1 k1 d1 sg2 s2 d2 res lr dp dz2 dz1 k1t dz2t dz1t sq".split()}
        mvk = sb("mvk", [P, 128])
        ones = sb("ones", [P, 1])
        grad = sb("grad", [P, 258])
        grad2 = sb("grad2", [P, 258])
        gpar = sb("gpar", [P, 2 * C + 2])
        gtmp = sb("gtmp", [P, 2 * C + 2])
        npar = sb("npar", [P, 2 * C + 2])
        nw = sb("nw", [P, 2, 128])
        hnb = sb("hnb", [P, 2])
        hb = sb("hb", [P, 3])

        ident_b = sb("ident_b", [P, P], BF16)
        sel_b = sb("sel_b", [18, EPAIRS * P], BF16)
        ring = gath[:, :, :, :].rearrange("p r a b -> p r (a b)")
        e1 = ring[:, 0, 0:2 * COLS].rearrange("p (k n) -> p k n", k=2)
        e2 = ring[:, 0, 2 * COLS:4 * COLS].rearrange("p (k n) -> p k n", k=2)
        e2r = ring[:, 1, 0:2 * COLS].rearrange("p (k n) -> p k n", k=2)
        rhT = sb("rhT", [2 * RH, 2, COLS])
        NE = CHUNKS * EXPERTS
        routT = ring[0:NE, 1, 2 * COLS:2 * COLS + GROUP * P].rearrange("p (k n) -> p k n", k=GROUP)
        ew1_half = ring[:, 2, 0:2 * EPAIRS * P].rearrange("p (b n) -> p b n", b=2)
        neg_mean = sb("neg_mean", [P, GROUP, CHUNKS])
        cvar = sb("cvar", [P, GROUP, CHUNKS])
        crstd = sb("crstd", [P, GROUP, CHUNKS])
        cnewton = sb("cnewton", [P, GROUP, CHUNKS])
        cseed = sb("cseed", [P, GROUP, CHUNKS], I32)
        lg = sb("lg", [P, GROUP, NE])
        pe_ = sb("pe_", [P, GROUP, NE])
        prb = sb("prb", [P, GROUP, NE])
        hot = sb("hot", [P, 2, GROUP, NE])
        key = sb("key", [P, GROUP, NE])
        top = sb("top", [P, 8, GROUP * CHUNKS])
        rout = sb("rout", [P, GROUP, NE])
        rest = sb("rest", [P, GROUP, NE])
        rout3 = sb("rout3", [P, GROUP * CHUNKS, 3 * EXPERTS], BF16)
        rout3T = sb("rout3T", [3 * EXPERTS, GROUP, 2 * COLS], BF16)

        b_smp = bank("b_smp")
        b_k = bank("b_k")
        b_v = [bank("b_v0"), bank("b_v1")]
        b_g = bank("b_g")
        b_aux = [bank("b_aux0"), bank("b_aux1"), bank("b_aux2")]

        params_in, txt_in, late_in, ready = sem("params_in"), sem("txt_in"), sem("late_in"), sem("ready")
        ref_in, ref_used = sem("ref_in"), sem("ref_used")
        gathered = [sem(f"gathered{k}") for k in range(RING)]
        txt_gathered, rows_txt = sem("txt_gathered"), sem("rows_txt")
        rows_a, rows_b = sem("rows_a"), sem("rows_b")
        issued_a, issued_b = sem("issued_a"), sem("issued_b")
        weighed, summed, smp_copied, kv_made = sem("weighed"), sem("summed"), sem("smp_copied"), sem("kv_made")
        scored, exped, attended = sem("scored"), sem("exped"), sem("attended")
        keys_read = sem("keys_read")
        qry_moved = sem("qry_moved")
        s_dve, s_act = sem("s_dve"), sem("s_act")

        def made(name):
            return sem("made_" + name)

        def read(name):
            return sem("read_" + name)

        AUX = ["qf", "off1", "qry", "u", "og", "k0", "off2", "z1", "v", "z2", "lr", "q", "k1t", "dk", "dz2t", "dz1t"]
        AUX_Q = [n for n in AUX if n in ("qf", "qry", "off1", "og", "off2")]
        AUX_B = ["u", "z1", "k0", "v", "z2", "lr", "q", "k1t", "dk", "dz2t", "dz1t"]
        bank_of = {n: b_aux[k % 3] for k, n in enumerate(AUX)}

        def user_before(name, order):
            k = order.index(name)
            same = [n for n in order if bank_of[n] is bank_of[name]]
            earlier = [n for n in same if order.index(n) < k]
            return (earlier[-1], True) if earlier else (same[-1], False)

        UNITS = 2 * EPAIRS
        GUNITS = GROUP * UNITS
        GROUPS = SLOTS // GROUP
        e1_bank, e2_bank, r_bank, y_bank = b_k, b_v, b_smp, b_g
        PE_WITHIN = {5: [("rt", 0)], 6: [("rt", 1)], 7: [("rt", 2)], 12: [("rh", 1)], 13: [("rh", 2)]}
        PE_ROUNDS = {0: [("z1", 0), ("z1", 1)], 1: [("z1", 2)], 2: [("z2", 0)], 3: [("z2", 1)], 4: [("z2", 2)],
                     10: [("u2", 0), ("u2", 1)], 11: [("rh", 0), ("u2", 2)], 12: [("lg", 0)],
                     13: [("lg", 1), ("lg", 2)]}
        ACT_ROUNDS = {0: [("sg1", 0)], 1: [("sg1", 1)], 2: [("sg1", 2)], 3: [("sg2", 0)], 4: [("sg2", 1)],
                      5: [("sg2", 2)], 6: [("squares", 0)], 7: [("squares", 1)], 8: [("squares", 2)],
                      10: [("u2", 0), ("u2", 1)], 11: [("rh", 0), ("u2", 2)], 12: [("rh", 1)], 13: [("rh", 2)],
                      14: [("exp", None)], 17: [("gap", None)]}
        OWN_ROUNDS = {0: [("r48", 0), ("r3", 0)], 1: [("r48", 1)], 2: [("r3", 1)], 3: [("r48", 2)], 4: [("r3", 2)]}
        DVE_ROUNDS = {0: [("s1", 0)], 1: [("s1", 1)], 2: [("s1", 2)], 3: [("s2", 0)], 4: [("s2", 1)],
                      5: [("s2", 2), ("h2", 0)], 6: [("h2", 1)], 7: [("h2", 2), ("var", 0)],
                      8: [("var", 1), ("var", 2), ("rstd", None)],
                      9: [("normal", 0), ("normal", 1), ("normal", 2)],
                      13: [("lg", 0)], 14: [("lg", 1), ("lg", 2), ("shift", None)], 15: [("best", None)],
                      16: [("second", None)], 18: [("weights", None)]}
        CAUX = [x for m in range(GUNITS) for x in PE_WITHIN.get(m, []) + PE_ROUNDS.get(m, [])]
        RAUX = [x for m in sorted(OWN_ROUNDS) for x in OWN_ROUNDS[m]]
        cbank = {x: b_aux[k % 2] for k, x in enumerate(CAUX)} | {x: b_aux[2] for x in RAUX}
        l1_made, e1_done, l2_made, e2_done = sem("l1_made"), sem("e1_done"), sem("l2_made"), sem("e2_done")
        r_made, e2r_done, l3_made = sem("r_made"), sem("e2r_done"), sem("l3_made")
        y_done, stored, updated = sem("y_done"), sem("stored"), sem("updated")
        CNAMES = ["z1", "z2", "rt", "u2", "rh", "lg", "r3", "r48"]
        PHASE3_SEMS = ([l1_made, e1_done, l2_made, e2_done, r_made, e2r_done, l3_made, y_done]
                       + [sem(f"{w}_c_{n}") for w in ("made", "read") for n in CNAMES]
                       + [sem(n) for n in ("c_k1_done", "c_res_done", "c_sg1_done", "c_sg2_done", "c_mean_done",
                                           "c_var_done", "c_normed", "c_lgx_done",
                                           "c_exp_done", "c_gap_done", "c_gape_done", "c_rout_done")])
        cmade = lambda n: sem(f"made_c_{n}")
        cread = lambda n: sem(f"read_c_{n}")
        SG = [T[n] for n in ("sg1", "sg2", "lr")]
        SI = [T[n] for n in ("s1", "s2", "d2")]
        K1 = [T[n] for n in ("k1", "dp", "dz2")]
        RES = [T[n] for n in ("res", "dz1", "k1t")]
        UN = [T[n] for n in ("u", "k0", "uT")]

        def h_of(slot):
            return h_all[:, bass.ds(slot, 1), :].rearrange("p a n -> p (a n)")

        def q_of(slot):
            return q_all[:, bass.ds(slot, 1), :].rearrange("p a n -> p (a n)")

        def groups_loop(eng, one_group):
            with eng.Fori(0, GROUPS - 1) as g:
                one_group(g, True)
            one_group(GROUPS - 1, False)

        def phase3_sync(sp):
            with sp.Fori(0, SLOTS) as s:
                sp.wait_ge(y_done, s + (PRIME + 1))
                sp.dma_start(out[bass.ds(s, 1)].rearrange("a p n -> (a p) n"), h_of(s)).then_inc(stored, 16)
            sp.wait_ge(stored, 16 * SLOTS)

        def phase23_tensor(pe):
            ident = par("ident")

            pe.wait_ge(sem("grad_masked"), 1)
            pe.matmul(b_aux[0][:, 0:258], par("stack"), grad[:, :], start=True, stop=True).then_inc(made("gsum"), 1)
            pe.wait_ge(sem("ghat_done"), 1)
            pe.matmul(b_aux[1][:, 0:C], par("mkrep", C), gtmp[0:C, 0:C], start=True, stop=True
                      ).then_inc(made("gw1"), 1)
            pe.wait_ge(updated, 1)

            def c1(name, k, base):
                slot = base + k
                n = slot + (PRIME + 1)
                order, banks = (RAUX, 1) if name in ("r3", "r48") else (CAUX, 2)
                at = order.index((name, k))
                before, kb = order[at - banks]
                pe.wait_ge(cread(before), base + (kb + PRIME + 1 - (0 if at >= banks else GROUP)))
                dst = cbank[(name, k)]
                if name == "z1":
                    last = pe.matmul(dst[:, :], nw[:, 0, :], q_of(slot), start=True, stop=True)
                elif name == "z2":
                    pe.wait_ge(sem("c_k1_done"), n)
                    last = pe.matmul(dst[:, :], nw[:, 1, :], K1[k][:, :], start=True, stop=True)
                elif name == "rt":
                    pe.wait_ge(sem("c_res_done"), n)
                    for j in range(PAIRS):
                        last = pe.transpose(dst[:, j * 128:(j + 1) * 128], RES[k][:, j * 128:(j + 1) * 128], ident)
                elif name == "u2":
                    pe.wait_ge(sem("c_normed"), n)
                    for j in range(PAIRS):
                        last = pe.transpose(dst[:, j * 128:(j + 1) * 128], UN[k][:, j * 128:(j + 1) * 128], ident)
                elif name == "rh":
                    pe.wait_ge(cread("u2"), n)
                    pe.sem_inc(sem("rh_started"), 1)
                    last = pe.matmul(dst[0:2 * RH, :], par("rw1"), q_of(slot), start=True, stop=True)
                elif name == "lg":
                    pe.wait_ge(cread("rh"), n)
                    for j in range(PAIRS):
                        last = pe.matmul(dst[:, j * 12:(j + 1) * 12], rhT[:, k % 2, j * 128:(j + 1) * 128],
                                         par("rw2", 2 * RH), start=True, stop=True)
                elif name == "r3":
                    for c in range(CHUNKS):
                        col = (c % 2) * COLS + (c // 2) * 128
                        last = pe.transpose(dst[:, :].bitcast(BF16)[0:18, col:col + 128],
                                            rout3[:, k * CHUNKS + c, :], ident_b[:, :])
                elif name == "r48":
                    pe.wait_ge(sem("c_rout_done"), n)
                    pe.sem_inc(sem("r48_started"), 1)
                    last = pe.transpose(dst[0:NE, 0:P], rout[:, k, :], ident)
                last.then_inc(cmade(name), 1)

            def one_group(g, more):
                units = g * GUNITS + PRIME

                def l1(m):
                    k, p, b = m // UNITS, m % UNITS // 2, m % 2
                    pe.wait_ge(e1_done, units + m)
                    pe.matmul(e1_bank[:, :], ew1_half[:, b, p * P:(p + 1) * P], q_of(g * GROUP + k),
                              start=True, stop=True).then_inc(l1_made, 1)

                def l2(m):
                    k, p, b = m // UNITS, m % UNITS // 2, m % 2
                    pe.wait_ge(e1_done, units + (m + 1))
                    pe.wait_ge(e2_done, units + (m - 1))
                    pe.matmul(e2_bank[m % 2][:, :], par("ew2")[:, p * P:(p + 1) * P], e1[:, m % 2, :],
                              start=True, stop=True).then_inc(l2_made, 1)
                    if m % UNITS == 0:
                        pe.wait_ge(cread("r3"), g * GROUP + (k + PRIME + 1))
                    pe.wait_ge(e2r_done, units + m)
                    pe.matmul(r_bank[:, :], sel_b[:, p * P:(p + 1) * P], rout3T[:, k, b * COLS:(b + 1) * COLS],
                              start=True, stop=True).then_inc(r_made, 1)

                def l3(m):
                    k, p, b = m // UNITS, m % UNITS // 2, m % 2
                    if m % UNITS == 0:
                        pe.wait_ge(cread("r48"), g * GROUP + (k + PRIME + 1))
                        pe.wait_ge(y_done, g * GROUP + (k + PRIME))
                        pe.matmul(y_bank[:, :], routT[:, k, :], par("eb3", NE), start=True, stop=False,
                                  skip_group_check=True)
                    pe.wait_ge(e2r_done, units + (m + 1))
                    for j in range(PAIRS):
                        at = (2 * j + b) * C
                        last = pe.matmul(y_bank[:, at:at + C], e2r[:, m % 2, j * 128:(j + 1) * 128],
                                         par("ew3")[:, p * C:(p + 1) * C], start=False,
                                         stop=(m % UNITS == UNITS - 1), skip_group_check=True)
                    last.then_inc(l3_made, 1)

                for m in range(GUNITS + 2):
                    if m < GUNITS:
                        l1(m)
                    if 1 <= m <= GUNITS:
                        l2(m - 1)
                    if more:
                        for name, k in PE_WITHIN.get(m, []):
                            c1(name, k, g * GROUP + GROUP)
                    if m >= 2:
                        l3(m - 2)
                    if more:
                        for name, k in PE_ROUNDS.get(m, []):
                            c1(name, k, g * GROUP + GROUP)
                    for name, k in OWN_ROUNDS.get(m, []):
                        c1(name, k, g * GROUP)

            for m in range(GUNITS + 2):
                for name, k in PE_WITHIN.get(m, []) + PE_ROUNDS.get(m, []):
                    c1(name, k, 0)
            groups_loop(pe, one_group)

        def phase3_scalar(act, chain, link, copy, sigmoid):
            act.wait_ge(updated, 1)

            def c1(name, k, base):
                slot = base + (k or 0)
                n = slot + (PRIME + 1)
                if name in ("sg1", "sg2"):
                    z, layer = ("z1", 0) if name == "sg1" else ("z2", 1)
                    act.wait_ge(cmade(z), n)
                    sigmoid(SG[k][:, :], cbank[(z, k)][:, :], hnb[:, layer:layer + 1]).then_inc(sem(f"c_{name}_done"), 1)
                if name == "squares":
                    act.wait_ge(sem("c_mean_done"), n)
                    act.activation(SI[k][:, :], UN[k][:, :], ACT.Square).then_inc(sem("c_var_done"), 1)
                if name == "u2":
                    act.wait_ge(cmade("u2"), n)
                    copy(q_of(slot), cbank[("u2", k)][:, :]).then_inc(cread("u2"), 1)
                if name == "rh":
                    act.wait_ge(cmade("rh"), n)
                    act.activation(rhT[:, k % 2, :], cbank[("rh", k)][0:2 * RH, :], ACT.Relu, bias=par("rb1", 2 * RH)
                                   ).then_inc(cread("rh"), 1)
                if name == "exp":
                    act.wait_ge(sem("c_lgx_done"), n)
                    act.activation(pe_[:, :, :], lg[:, :, :], ACT.Exp).then_inc(sem("c_exp_done"), GROUP)
                if name == "gap":
                    act.wait_ge(sem("c_gap_done"), n)
                    act.activation(top[:, 5, :], top[:, 4, :], ACT.Exp).then_inc(sem("c_gape_done"), GROUP)
                if name == "r3":
                    act.wait_ge(cmade("r3"), n)
                    copy(rout3T[:, k, :], cbank[("r3", k)][:, :].bitcast(BF16)[0:18, :]).then_inc(cread("r3"), 1)
                if name == "r48":
                    act.wait_ge(cmade("r48"), n)
                    copy(routT[:, k, :], cbank[("r48", k)][0:NE, 0:P]).then_inc(cread("r48"), 1)

            def one_group(g, more):
                act.sem_clear(s_act)
                chain[0] = 0
                units = g * GUNITS + PRIME
                for m in range(GUNITS + 2):
                    if m < GUNITS:
                        act.wait_ge(l1_made, units + (m + 1))
                        act.wait_ge(l2_made, units + (m - 1))
                        p = m % UNITS // 2
                        act.activation(e1[:, m % 2, :], e1_bank[:, :], ACT.Relu,
                                       bias=par("eb1")[:, p:p + 1]).then_inc(e1_done, 1)
                    if 1 <= m <= GUNITS:
                        u = m - 1
                        p = u % UNITS // 2
                        act.wait_ge(l2_made, units + (u + 1))
                        act.wait_ge(e2r_done, units + (u - 1))
                        act.activation(e2[:, u % 2, :], e2_bank[u % 2][:, :], ACT.Relu,
                                       bias=par("eb2")[:, p:p + 1]).then_inc(e2_done, 1)
                    if more:
                        for name, k in ACT_ROUNDS.get(m, []):
                            c1(name, k, g * GROUP + GROUP)
                    for name, k in OWN_ROUNDS.get(m, []):
                        c1(name, k, g * GROUP)

            act.sem_clear(s_act)
            chain[0] = 0
            for m in range(GUNITS + 2):
                for name, k in ACT_ROUNDS.get(m, []):
                    c1(name, k, 0)
            groups_loop(act, one_group)

        def phase23_vector(dve, steps, step, sync, link, bc, chunked, rsqrt_of):
            link(dve.memset(ew1_half[:, :, :], 0.0))
            for b in range(2):
                half = slice(b * C, (b + 1) * C)
                step(dve.tensor_copy(ew1_half[half, b, :], par("ew1")[half, :]))
            step(dve.tensor_copy(ident_b[:, :], par("ident")))
            step(dve.tensor_copy(sel_b[:, :], par("sel", 18)))
            step(dve.memset(nw[:, :, :], 0.0))
            step(dve.tensor_scalar(npar[:, :], par("par"), 1.0 - LR * WD, None, ALU.mult))
            dve.wait_ge(sem("grads_added"), PRIME + SLOTS)
            step(dve.tensor_tensor(grad[:, 0:256], b_g[:, 0:256], par("gmask"), ALU.mult))
            sync()
            dve.tensor_copy(grad[:, 256:258], b_g[:, 256:258]).then_inc(sem("grad_masked"), 1)
            dve.wait_ge(made("gsum"), 1)
            link(dve.tensor_copy(grad2[:, :], b_aux[0][:, 0:258]))
            dve.tensor_tensor(gtmp[:, 0:C], grad2[:, 128:128 + C], grad2[:, 128 + C:256], ALU.add
                              ).then_inc(sem("ghat_done"), 1)
            step(dve.tensor_tensor(gpar[:, C:2 * C], grad2[:, 0:C], grad2[:, C:2 * C], ALU.add))
            step(dve.tensor_copy(gpar[:, 2 * C:], grad2[:, 256:258]))
            dve.wait_ge(made("gw1"), 1)
            link(dve.tensor_copy(gpar[:, 0:C], b_aux[1][:, 0:C]))
            link(dve.scalar_tensor_tensor(gtmp[:, :], gpar[:, :], -1.0, gpar[:, :], ALU.mult, ALU.max))
            link(dve.tensor_scalar(gtmp[:, :], gtmp[:, :], 1e-8, None, ALU.add))
            link(dve.reciprocal(gtmp[:, :], gtmp[:, :]))
            link(dve.tensor_tensor(gtmp[:, :], gtmp[:, :], gpar[:, :], ALU.mult))
            link(dve.scalar_tensor_tensor(npar[:, :], gtmp[:, :], -LR, npar[:, :], ALU.mult, ALU.add))
            for k in range(2):
                for b in range(2):
                    half = slice(b * C, (b + 1) * C)
                    step(dve.tensor_copy(nw[half, k, half], npar[half, k * C:(k + 1) * C]))
            sync()
            dve.tensor_scalar(hnb[:, :], npar[:, 2 * C:], 0.5, None, ALU.mult).then_inc(updated, 1)

            flat = lambda t: t.rearrange("p k x -> p (k x)")
            v3 = lambda t: flat(t).rearrange("p (n e) -> p n e", e=EXPERTS)

            def pick(which, probs, best):
                link(dve.tensor_reduce(best, v3(probs), AX, ALU.max))
                link(dve.tensor_tensor(v3(key[:, :, :]), v3(probs), bc(best, EXPERTS), ALU.is_equal))
                link(dve.tensor_tensor(key[:, :, :], key[:, :, :],
                                       par("first").unsqueeze(1).broadcast_to([P, GROUP, NE]), ALU.mult))
                link(dve.tensor_reduce(top[:, 7, :], v3(key[:, :, :]), AX, ALU.max))
                link(dve.tensor_tensor(v3(hot[:, which, :, :]), v3(key[:, :, :]), bc(top[:, 7, :], EXPERTS),
                                       ALU.is_equal))

            def c1(name, k, base):
                slot = base + (k or 0)
                n = slot + (PRIME + 1)
                if name == "s1":
                    dve.wait_ge(sem("c_sg1_done"), n)
                    dve.scalar_tensor_tensor(SI[k][:, :], cbank[("z1", k)][:, :], npar[:, 2 * C:2 * C + 1],
                                             SG[k][:, :], ALU.add, ALU.mult).then_inc(cread("z1"), 1)
                    dve.wait_ge(cread("z1"), n)
                    dve.tensor_tensor(K1[k][:, :], q_of(slot), SI[k][:, :], ALU.add).then_inc(sem("c_k1_done"), 1)
                if name == "s2":
                    dve.wait_ge(sem("c_sg2_done"), n)
                    dve.scalar_tensor_tensor(SI[k][:, :], cbank[("z2", k)][:, :], npar[:, 2 * C + 1:2 * C + 2],
                                             SG[k][:, :], ALU.add, ALU.mult).then_inc(cread("z2"), 1)
                    dve.wait_ge(cread("z2"), n)
                    dve.tensor_tensor(RES[k][:, :], K1[k][:, :], SI[k][:, :], ALU.add).then_inc(sem("c_res_done"), 1)
                if name == "h2":
                    dve.wait_ge(cmade("rt"), n)
                    dve.tensor_tensor(h_of(slot), h_of(slot), cbank[("rt", k)][:, :], ALU.add).then_inc(cread("rt"), 1)
                    dve.wait_ge(cread("rt"), n)
                    dve.sem_inc(sem("mean_started"), 1)
                    link(dve.tensor_reduce(neg_mean[:, k, :], chunked(h_of(slot)), AX, ALU.add))
                    link(dve.tensor_scalar(neg_mean[:, k, :], neg_mean[:, k, :], -1.0 / C, None, ALU.mult))
                    dve.tensor_tensor(chunked(UN[k][:, :]), chunked(h_of(slot)), bc(neg_mean[:, k, :], C), ALU.add
                                      ).then_inc(sem("c_mean_done"), 1)
                if name == "var":
                    dve.wait_ge(sem("c_var_done"), n)
                    step(dve.tensor_reduce(cvar[:, k, :], chunked(SI[k][:, :]), AX, ALU.add))
                if name == "rstd":
                    sync()
                    link(dve.tensor_scalar(flat(cvar[:, :, :]), flat(cvar[:, :, :]), 1.0 / C, LN_EPS, ALU.mult, ALU.add))
                    rsqrt_of(cvar, crstd, cnewton, cseed)
                if name == "normal":
                    dve.tensor_tensor(chunked(UN[k][:, :]), chunked(UN[k][:, :]), bc(crstd[:, k, :], C), ALU.mult
                                      ).then_inc(sem("c_normed"), 1)
                if name == "lg":
                    dve.wait_ge(cmade("lg"), n)
                    dve.tensor_tensor(lg[:, k, :], cbank[("lg", k)][:, 0:NE], par("rb2"), ALU.add
                                      ).then_inc(cread("lg"), 1)
                if name == "shift":
                    dve.wait_ge(cread("lg"), base + (PRIME + GROUP))
                    link(dve.tensor_reduce(top[:, 0, :], v3(lg[:, :, :]), AX, ALU.max))
                    dve.tensor_tensor(v3(lg[:, :, :]), v3(lg[:, :, :]), bc(top[:, 0, :], EXPERTS), ALU.subtract
                                      ).then_inc(sem("c_lgx_done"), GROUP)
                if name == "best":
                    dve.wait_ge(sem("c_exp_done"), n)
                    link(dve.tensor_reduce(top[:, 0, :], v3(pe_[:, :, :]), AX, ALU.add))
                    link(dve.reciprocal(top[:, 1, :], top[:, 0, :]))
                    link(dve.tensor_tensor(v3(prb[:, :, :]), v3(pe_[:, :, :]), bc(top[:, 1, :], EXPERTS), ALU.mult))
                    pick(0, prb[:, :, :], top[:, 2, :])
                if name == "second":
                    link(dve.scalar_tensor_tensor(flat(prb[:, :, :]), flat(hot[:, 0, :, :]), -4.0, flat(prb[:, :, :]),
                                                  ALU.mult, ALU.add))
                    pick(1, prb[:, :, :], top[:, 3, :])
                    dve.tensor_tensor(top[:, 4, :], top[:, 3, :], top[:, 2, :], ALU.subtract
                                      ).then_inc(sem("c_gap_done"), GROUP)
                if name == "weights":
                    dve.wait_ge(sem("c_gape_done"), n)
                    link(dve.tensor_scalar(top[:, 6, :], top[:, 5, :], 1.0, None, ALU.add))
                    link(dve.reciprocal(top[:, 6, :], top[:, 6, :]))
                    link(dve.tensor_tensor(top[:, 5, :], top[:, 5, :], top[:, 6, :], ALU.mult))
                    step(dve.tensor_tensor(v3(hot[:, 0, :, :]), v3(hot[:, 0, :, :]), bc(top[:, 6, :], EXPERTS), ALU.mult))
                    link(dve.tensor_tensor(v3(hot[:, 1, :, :]), v3(hot[:, 1, :, :]), bc(top[:, 5, :], EXPERTS), ALU.mult))
                    link(dve.tensor_tensor(rout[:, :, :], hot[:, 0, :, :], hot[:, 1, :, :], ALU.add))
                    part = lambda i: rout3[:, :, i * EXPERTS:(i + 1) * EXPERTS]
                    link(dve.tensor_copy(part(0), v3(rout[:, :, :])))
                    link(dve.tensor_tensor(v3(rest[:, :, :]), v3(rout[:, :, :]), part(0), ALU.subtract))
                    link(dve.tensor_copy(part(1), v3(rest[:, :, :])))
                    dve.tensor_tensor(part(2), v3(rest[:, :, :]), part(1), ALU.subtract
                                      ).then_inc(sem("c_rout_done"), GROUP)

            def one_group(g, more):
                dve.sem_clear(s_dve)
                steps[0] = 0
                units = g * GUNITS + PRIME
                for m in range(GUNITS + 2):
                    if 1 <= m <= GUNITS:
                        u = m - 1
                        dve.wait_ge(e2_done, units + (u + 1))
                        dve.wait_ge(r_made, units + (u + 1))
                        dve.wait_ge(l3_made, units + (u - 1))
                        dve.tensor_tensor(e2r[:, u % 2, :], e2[:, u % 2, :], r_bank[:, :], ALU.mult
                                          ).then_inc(e2r_done, 1)
                    if m >= 2 and (m - 1) % UNITS == 0:
                        k = (m - 2) // UNITS
                        dve.wait_ge(l3_made, units + (m - 1))
                        dve.tensor_tensor(h_of(g * GROUP + k), h_of(g * GROUP + k), y_bank[:, :], ALU.add
                                          ).then_inc(y_done, 1)
                    if more:
                        for name, k in DVE_ROUNDS.get(m, []):
                            c1(name, k, g * GROUP + GROUP)
                sync()

            for m in range(GUNITS + 2):
                for name, k in DVE_ROUNDS.get(m, []):
                    c1(name, k, 0)
            groups_loop(dve, one_group)

        block = ctx.enter_context(nc.Block())

        @block.sync
        def _(sp):
            sp.dma_start(w_early[:, :], early).then_inc(params_in, 16)
            sp.dma_start(xref[:, :, :, :].rearrange("p k n c -> p (k n c)"), x_ref[0]).then_inc(ref_in, 16)
            sp.dma_start(txt_i[:, :], txt_idx).then_inc(txt_in, 16)
            sp.dma_start(w_late[:, :], late).then_inc(late_in, 16)
            for s in ([ref_used, rows_a, rows_b, issued_a, issued_b, weighed, summed, smp_copied, kv_made,
                       qry_moved] + [made(n) for n in AUX] + [read(n) for n in AUX]
                      + [sem(n) for n in ("hidden_done", "gelu_square", "gelu_arg", "gelu_tanh", "gelu_done", "mean_done", "var_done", "rstd_done",
                                          "normed", "sg1_done", "sg2_done", "dz2_done", "dz1_done")]):
                sp.sem_inc(s, PRIME)
            for s in (keys_read, scored, exped, sem("grads_added")):
                sp.sem_inc(s, PRIME - 1)
            sp.sem_inc(attended, PRIME - 2)
            for s in PHASE3_SEMS:
                sp.sem_inc(s, PRIME)
            with sp.Fori(0, IMAGES) as i:
                sp.wait_ge(ref_used, i + (PRIME + 1))
                sp.dma_start(xref[:, :, :, :].rearrange("p k n c -> p (k n c)"),
                             x_ref[bass.ds(i + 1, 1)].rearrange("a p n -> (a p) n")).then_inc(ref_in, 16)
            phase3_sync(sp)

        @block.gpsimd
        def _(pool):
            def gather(dst, table, index, done, index_used=None):
                pool.indirect_dma_start(dst, None, table, bass.IndirectOffsetOnAxis(ap=index.bitcast(U32), axis=0),
                                        engine_sem=index_used).then_inc(done, 16)

            pool.wait_ge(txt_in, 16)
            pool.wait_ge(rows_txt, 1)
            for j in range(TXT_CHUNKS):
                gather(txt_cat[:, j, 0:C], txt_table, txt_row[:, j:j + 1], txt_gathered)
                gather(txt_cat[:, j, C:C + TYPE_DIM], type_table, txt_i[:, j:j + 1], txt_gathered)
            with pool.Fori(0, IMAGES) as i:
                for c in range(CHUNKS):
                    if c == 0:
                        pool.wait_ge(rows_a, i + (PRIME + 1))
                    if c == CHUNKS // 2:
                        pool.wait_ge(rows_b, i + (PRIME + 1))
                    pool.wait_ge(weighed, i * CHUNKS + (PRIME + c - RING + 1))
                    pool.sem_inc(sem("slots_taken"), 1)
                    for n in range(POINTS):
                        k = c * POINTS + n
                        used = {(3, 7): issued_a, (7, 7): issued_b}.get((c, n))
                        gather(gath[:, c % RING, n, :], x_pairs, row[:, k:k + 1], gathered[c % RING], used)

        @block.tensor
        def _(pe):
            ident = par("ident")

            def transpose4(dst, src, width=128):
                for j in range(PAIRS):
                    last = pe.transpose(dst[:, j * 128:(j + 1) * 128], src[:, j * width:j * width + 128], ident)
                return last

            def bank_free(name, order, now, before):
                user, same_turn = user_before(name, order)
                if same_turn:
                    pe.wait_ge(read(user), now(user))
                elif before is not None:
                    pe.wait_ge(read(user), before(user))

            def points_stage(name, order, now, before):
                def mm(dst, lhsT, rhs, **kw):
                    return pe.matmul(dst, lhsT, rhs, start=True, stop=True, **kw)
                bank_free(name, order, now, before)
                dst = bank_of[name]
                if name == "qf":
                    pe.wait_ge(ref_used, now("ref"))
                    for j in range(PAIRS):
                        for k in range(4):
                            last = pe.matmul(dst[:, j * 128:(j + 1) * 128],
                                             xrefw[:, k, 2 * j:2 * j + 2, :].rearrange("p a c -> p (a c)"),
                                             ident, is_transpose=True, start=(k == 0), stop=(k == 3))
                elif name == "qry":
                    for j in range(PAIRS):
                        last = mm(dst[:, j * 128:(j + 1) * 128], qfT[:, j * 128:(j + 1) * 128], par("wq2"))
                elif name == "off1":
                    pe.wait_ge(read("qf"), now("qf"))
                    pe.wait_ge(sem("weights_ready"), 1)
                    for j in range(PAIRS):
                        last = mm(dst[:, j * 32:(j + 1) * 32], qfT[:, j * 128:(j + 1) * 128], par("wo1"))
                elif name == "og":
                    pe.wait_ge(sem("gelu_done"), now("g"))
                    last = pe.transpose(dst[:, 0:128], oh[:, :], ident)
                elif name == "off2":
                    pe.wait_ge(read("og"), now("og"))
                    last = mm(dst[:, 0:128], ogT[:, :], par("wo2"))
                last.then_inc(made(name), 1)

            def mlp_stage(name, order, now, before):
                def mm(w, src):
                    return pe.matmul(dst[:, :], w, src[:, :], start=True, stop=True)
                bank_free(name, order, now, before)
                dst = bank_of[name]
                if name == "u":
                    pe.wait_ge(sem("normed"), now("n"))
                    last = transpose4(dst, T["u"])
                elif name == "k0":
                    pe.wait_ge(read("u"), now("u"))
                    last = mm(par("mk"), T["uT"])
                elif name == "z1":
                    pe.wait_ge(read("u"), now("u"))
                    last = mm(par("mw1"), T["uT"])
                elif name == "v":
                    last = mm(mvk[:, :], T["uT"])
                elif name == "lr":
                    last = mm(par("mlr"), T["uT"])
                elif name == "z2":
                    pe.wait_ge(read("k0"), now("k0"))
                    pe.wait_ge(read("z1"), now("z1"))
                    pe.matmul(dst[:, :], par("mw2"), T["k0"][:, :], start=True, stop=False)
                    last = pe.matmul(dst[:, :], par("mw2"), T["s1"][:, :], start=False, stop=True)
                elif name == "q":
                    last = mm(par("mq"), T["uT"])
                elif name == "k1t":
                    for j in range(PAIRS):
                        cols = slice(j * 128, (j + 1) * 128)
                        for part, first in (("k0", True), ("s1", False)):
                            last = pe.matmul(dst[:, cols], T[part][:, cols], ident, is_transpose=True,
                                             start=first, stop=not first)
                elif name == "dk":
                    pe.wait_ge(sem("dz2_done"), now("dz2"))
                    last = mm(par("mw2t"), T["dz2"])
                elif name == "dz2t":
                    last = transpose4(dst, T["dz2"])
                elif name == "dz1t":
                    pe.wait_ge(sem("dz1_done"), now("dz1"))
                    last = transpose4(dst, T["dz1"])
                last.then_inc(made(name), 1)

            def gradients(n):
                kw = dict(start=False, stop=False, skip_group_check=True)
                pe.wait_ge(read("dz2t"), n)
                for j in range(PAIRS):
                    cols = slice(j * 128, (j + 1) * 128)
                    pe.matmul(b_g[:, 0:128], T["k1t"][:, cols], T["dz2t"][:, cols], **kw)
                    pe.matmul(b_g[:, 257:258], T["dz2t"][:, cols], ones[:, :], **kw)
                pe.wait_ge(read("dz1t"), n)
                for j in range(PAIRS):
                    cols = slice(j * 128, (j + 1) * 128)
                    pe.matmul(b_g[:, 128:256], T["u"][:, cols], T["dz1t"][:, cols], **kw)
                    last = pe.matmul(b_g[:, 256:257], T["dz1t"][:, cols], ones[:, :], **kw)
                last.then_inc(sem("grads_added"), 1)

            pe.wait_ge(params_in, 16)
            first = lambda name: PRIME + 1
            for name in AUX_Q:
                points_stage(name, AUX_Q, first, None)
            pe.wait_ge(late_in, 16)
            pe.wait_ge(sem("txt_cat_done"), 1)
            pe.wait_ge(txt_gathered, 32 * TXT_CHUNKS)
            pe.wait_ge(read("og"), PRIME + 1)
            pe.wait_ge(read("off2"), PRIME + 1)
            pe.wait_ge(read("qry"), PRIME + 1)
            pe.transpose(b_aux[2][:, 0:128], par("mk"), ident).then_inc(made("mkt"), 1)
            pe.wait_ge(read("mkt"), 1)
            pe.matmul(b_aux[2][:, 128:256], T["sg1"][:, 0:128], par("mw1"), start=True, stop=True
                      ).then_inc(made("mkw1"), 1)
            for j in range(TXT_CHUNKS):
                last = pe.transpose(b_aux[j // 4][0:CAT, (j % 4) * 128:(j % 4) * 128 + 128], txt_cat[:, j, :], ident)
            last.then_inc(made("txt_t"), 1)
            pe.wait_ge(read("txt_t"), 1)
            for j in range(TXT_CHUNKS):
                last = pe.matmul(b_aux[0][:, j * C:(j + 1) * C], T["s1" if j == 4 else "k1"][0:CAT, (j % 4) * 128:(j % 4) * 128 + 128],
                                 par("txtw", CAT), start=True, stop=True)
            last.then_inc(made("txt_p"), 1)
            pe.wait_ge(read("txt_p"), 1)
            pe.wait_ge(read("mkw1"), 1)
            pe.matmul(b_g[:, 0:258], T["dz1t"][:, 0:128], T["dz2t"][:, 0:258], start=True, stop=False,
                      skip_group_check=True)

            with pe.Fori(0, IMAGES) as i:
                def now(name):
                    ahead = name in AUX_Q or name in ("ref", "g")
                    return i + (PRIME + (2 if ahead else 1))

                def before(name):
                    return i + PRIME

                def sum_corners(c):
                    pe.wait_ge(weighed, i * CHUNKS + (PRIME + c + 1))
                    pe.wait_ge(smp_copied, i * CHUNKS + (PRIME + c))
                    for j in range(PAIRS):
                        for k in range(4):
                            last = pe.matmul(b_smp[:, j * 128:(j + 1) * 128],
                                             gathw[:, c % 2, k, j * 128:(j + 1) * 128], ident,
                                             is_transpose=True, start=(k == 0), stop=(k == 3))
                    last.then_inc(summed, 1)

                def keys_values(c):
                    pe.wait_ge(smp_copied, i * CHUNKS + (PRIME + c + 1))
                    pe.wait_ge(keys_read, i * CHUNKS + (PRIME + c))
                    pe.wait_ge(attended, i * CHUNKS + (PRIME + c - 1))
                    for j in range(PAIRS):
                        cols = slice(j * 128, (j + 1) * 128)
                        pe.matmul(b_k[:, cols], smpT[:, c % 2, cols], par("wk2"), start=True, stop=True)
                        last = pe.matmul(b_v[c % 2][:, cols], smpT[:, c % 2, cols], par("wv2"), start=True, stop=True)
                    last.then_inc(kv_made, 1)

                EARLIER = {1: ["qf"], 3: ["u"], 4: ["off2", "z1"], 7: ["dk", "dz2t"]}
                LATER = {1: ["off1", "qry"], 3: ["og", "k0"], 4: ["v"], 5: ["z2", "lr", "q"], 6: ["k1t"],
                         7: ["dz1t"]}
                for r in range(CHUNKS):
                    sum_corners(r)
                    if r == 0:
                        gradients(i + PRIME)
                    for name in EARLIER.get(r, []):
                        (points_stage if name in AUX_Q else mlp_stage)(name, AUX, now, before)
                    keys_values(r)
                    for name in LATER.get(r, []):
                        (points_stage if name in AUX_Q else mlp_stage)(name, AUX, now, before)

            gradients(PRIME + IMAGES)
            last_now = lambda name: PRIME + IMAGES + 1
            for name in AUX_B:
                mlp_stage(name, AUX_B, last_now, lambda name: PRIME + IMAGES)
            gradients(PRIME + IMAGES + 1)
            phase23_tensor(pe)

        @block.scalar
        def _(act):
            chain = [0]

            def link(ins):
                chain[0] += 1
                ins.then_inc(s_act, 1)
                act.wait_ge(s_act, chain[0])

            def copy(dst, src):
                return act.activation(dst, src, ACT.Identity)

            def sigmoid(sg, src, half_bias):
                link(act.activation(sg, src, ACT.Tanh, bias=half_bias, scale=0.5))
                return act.activation(sg, sg, ACT.Copy, bias=0.5, scale=0.5)

            def moved(dst, name, now):
                act.wait_ge(made(name), now(name))
                copy(dst, bank_of[name][:, 0:dst.shape[1]]).then_inc(read(name), 1)

            def squares(slot_ap, now):
                act.wait_ge(sem("mean_done"), now("m"))
                for c in range(CHUNKS):
                    ins = act.activation(T["sq"][:, c * C:(c + 1) * C], slot_ap[:, c * C:(c + 1) * C], ACT.Square,
                                         bias=stat[:, 1, c:c + 1], accum_out=var[:, 0, c:c + 1])
                ins.then_inc(sem("var_done"), 1)

            def normalise(dst, src, n):
                act.wait_ge(sem("rstd_done"), n)
                act.sem_inc(sem("normalise_started"), 1)
                for c in range(CHUNKS):
                    ins = act.activation(dst[:, c * C:(c + 1) * C], src[:, c * C:(c + 1) * C], ACT.Identity,
                                         bias=stat[:, 3, c:c + 1], scale=rstd[:, 0, c:c + 1])
                ins.then_inc(sem("normed"), 1)

            def mlp_part(part, now, slot_ap, q_ap):
                if part == "squares":
                    squares(slot_ap, now)
                if part == "normalise":
                    act.wait_ge(sem("grads_added"), now("grads_before"))
                    normalise(T["u"], slot_ap, now("rstd"))
                if part == "sg1":
                    act.wait_ge(made("z1"), now("z1"))
                    sigmoid(T["sg1"][:, :], bank_of["z1"][:, :], hb[:, 0:1]).then_inc(sem("sg1_done"), 1)
                if part == "sg2":
                    act.wait_ge(made("z2"), now("z2"))
                    sigmoid(T["sg2"][:, :], bank_of["z2"][:, :], hb[:, 1:2]).then_inc(sem("sg2_done"), 1)
                if part == "lr":
                    act.wait_ge(made("lr"), now("lr"))
                    act.activation(T["lr"][:, :], bank_of["lr"][:, :], ACT.Tanh, bias=hb[:, 2:3], scale=0.5
                                   ).then_inc(read("lr"), 1)
                if part == "q":
                    act.wait_ge(made("q"), now("q"))
                    copy(q_ap, bank_of["q"][:, :]).then_inc(read("q"), 1)
                if part == "u":
                    moved(T["uT"][:, :], "u", now)
                if part in ("k0", "k1t", "dz2t", "dz1t"):
                    moved(T[part][:, :], part, now)

            def points_part(part, now):
                if part == "qf":
                    moved(qfT[:, :], "qf", now)
                if part == "qry":
                    moved(qry_next[:, :], "qry", now)
                if part == "square":
                    act.wait_ge(sem("hidden_done"), now("a"))
                    act.activation(ot[:, :], oh[:, :], ACT.Square, scale=GELU_A ** 0.5).then_inc(sem("gelu_square"), 1)
                if part == "gelu":
                    act.wait_ge(sem("gelu_arg"), now("a"))
                    act.activation(otanh[:, :], ot[:, :], ACT.Tanh, scale=GELU_C).then_inc(sem("gelu_tanh"), 1)
                if part == "og":
                    moved(ogT[:, :], "og", now)

            first = lambda name: PRIME + 1
            act.wait_ge(sem("ones_set"), 1)
            act.activation(otanh[:, 0:1], ones[:, :], ACT.Tanh)
            act.wait_ge(params_in, 16)
            for part in ("qf", "qry", "square", "gelu", "og"):
                points_part(part, first)
            act.wait_ge(made("mkt"), 1)
            copy(T["sg1"][:, 0:128], b_aux[2][:, 0:128]).then_inc(read("mkt"), 1)
            act.wait_ge(made("mkw1"), 1)
            copy(par("mw1"), b_aux[2][:, 128:256]).then_inc(read("mkw1"), 1)
            act.wait_ge(made("txt_t"), 1)
            copy(T["k1"][0:CAT, 0:512], b_aux[0][0:CAT, :])
            copy(T["s1"][0:CAT, 0:128], b_aux[1][0:CAT, 0:128]).then_inc(read("txt_t"), 1)
            act.wait_ge(late_in, 16)
            link(act.activation(hb[:, 0:2], par("par")[:, 2 * C:2 * C + 2], ACT.Copy, scale=0.5))
            link(act.activation(hb[:, 2:3], par("blr"), ACT.Copy, scale=0.5))

            with act.Fori(0, IMAGES) as i:
                act.sem_clear(s_act)
                chain[0] = 0
                def now(name):
                    return i + (PRIME + (2 if name in AUX_Q or name == "a" else 0 if name == "grads_before" else 1))

                EARLIER = {2: ["squares"], 3: ["square", "normalise"], 4: ["k0"], 6: ["sg2", "lr", "q"], 7: ["k1t"]}
                LATER = {1: ["qf", "qry"], 3: ["gelu", "u", "og"], 4: ["sg1"], 7: ["dz2t", "dz1t"]}

                def parts(names):
                    for part in names:
                        if part in ("qf", "qry", "square", "gelu", "og"):
                            points_part(part, now)
                        else:
                            mlp_part(part, now, h_all[:, bass.ds(i, 1), :].rearrange("p a n -> p (a n)"),
                                     q_all[:, bass.ds(i, 1), :].rearrange("p a n -> p (a n)"))

                for r in range(CHUNKS):
                    parts(EARLIER.get(r, []))
                    act.wait_ge(summed, i * CHUNKS + (PRIME + r + 1))
                    act.wait_ge(kv_made, i * CHUNKS + (PRIME + r - 1))
                    copy(smpT[:, r % 2, :], b_smp[:, :]).then_inc(smp_copied, 1)
                    c = (r - 1) % CHUNKS
                    act.wait_ge(scored, i * CHUNKS + (PRIME + r))
                    act.activation(prob[:, c % 2, :, :], score[:, c % 2, :, :], ACT.Exp, scale=DH ** -0.5
                                   ).then_inc(exped, 1)
                    if r == 0:
                        act.wait_ge(read("qry"), i + (PRIME + 1))
                        copy(qry[:, :], qry_next[:, :]).then_inc(qry_moved, 1)
                    parts(LATER.get(r, []))
                    if r == 7:
                        act.activation(par("lossw"), par("lossw"), ACT.Copy, bias=MAX_ALR / C, scale=0.0
                                       ).then_inc(sem("lossw_set"), 1)
            act.sem_clear(s_act)
            chain[0] = 0
            act.wait_ge(scored, IMAGES * CHUNKS + PRIME)
            act.activation(prob[:, 1, :, :], score[:, 1, :, :], ACT.Exp, scale=DH ** -0.5).then_inc(exped, 1)
            last_now = lambda name: PRIME + IMAGES + (0 if name == "grads_before" else 1)
            act.wait_ge(sem("mean_done"), PRIME + IMAGES + 1)
            act.activation(T["sq"][:, :], T["u"][:, :], ACT.Square).then_inc(sem("var_done"), 1)
            for part in ("u", "sg1", "k0", "sg2", "lr", "q", "k1t", "dz2t", "dz1t"):
                mlp_part(part, last_now, h_all[:, IMAGES, :], q_all[:, IMAGES, :])
            phase3_scalar(act, chain, link, copy, sigmoid)

        @block.vector
        def _(dve):
            steps = [0]

            def step(ins):
                steps[0] += 1
                ins.then_inc(s_dve, 1)
                return steps[0]

            def sync():
                dve.wait_ge(s_dve, steps[0])

            def link(ins):
                step(ins)
                sync()

            def bc(ap, n):
                return ap.unsqueeze(len(ap.shape)).broadcast_to(list(ap.shape) + [n])

            def chunked(ap):
                return ap.rearrange("p (n c) -> p n c", n=CHUNKS)

            def rsqrt_of(*tiles):
                v, y, t, s = (x[:, :, :].rearrange("p a n -> p (a n)") for x in tiles)
                link(dve.tensor_scalar(s, v.bitcast(I32), 1, None, ALU.logical_shift_right))
                link(dve.tensor_scalar(y.bitcast(I32), s, -1.0, RSQRT_SEED, ALU.mult, ALU.add))
                for _ in range(3):
                    link(dve.scalar_tensor_tensor(t, y, -0.5, v, ALU.mult, ALU.mult))
                    link(dve.tensor_tensor(t, t, y, ALU.mult))
                    link(dve.scalar_tensor_tensor(y, t, 1.5, y, ALU.add, ALU.mult))

            def rsqrt():
                rsqrt_of(var, rstd, newton, seed)

            def rsqrt_tokens(n):
                dve.wait_ge(sem("var_done"), n)
                link(dve.tensor_scalar(var[:, 0, :], var[:, 0, :], 1.0 / C, LN_EPS, ALU.mult, ALU.add))
                rsqrt()
                dve.tensor_tensor(stat[:, 3, :], stat[:, 1, :], rstd[:, 0, :], ALU.mult).then_inc(sem("rstd_done"), 1)

            def weigh_reference(now):
                dve.tensor_tensor(xrefw[:, :, :, :].rearrange("p k n c -> p (k n) c"),
                                  xref[:, :, :, :].rearrange("p k n c -> p (k n) c"),
                                  bc(par("refw"), C), ALU.mult).then_inc(ref_used, 1)

            def points_round(r, now, tokens):
                if r == 2:
                    hv = oh[:, :].rearrange("p (n k) -> p n k", n=CHUNKS)
                    tv = ot[:, :].rearrange("p (n k) -> p n k", n=CHUNKS)
                    dve.wait_ge(made("off1"), now("off1"))
                    dve.tensor_tensor(oh[:, :], bank_of["off1"][:, 0:128], par("bo1"), ALU.add).then_inc(read("off1"), 1)
                    dve.wait_ge(read("off1"), now("off1"))
                    link(dve.tensor_tensor(ot[:, :], oh[:, :], oh[:, :], ALU.mult))
                    link(dve.tensor_reduce(stat[:, 5, :], tv, AX, ALU.add))
                    link(dve.tensor_scalar(var[:, 1, :], stat[:, 5, :], 1.0 / HID, LN_EPS, ALU.mult, ALU.add))
                    if tokens is not None:
                        rsqrt_tokens(tokens)
                    else:
                        rsqrt()
                    link(dve.tensor_tensor(hv, hv, bc(rstd[:, 1, :], HID), ALU.mult))
                    link(dve.tensor_tensor(oh[:, :], oh[:, :], par("lng"), ALU.mult))
                    dve.tensor_tensor(oh[:, :], oh[:, :], par("lnb"), ALU.add).then_inc(sem("hidden_done"), 1)
                if r == "gelu_arg":
                    dve.wait_ge(sem("gelu_square"), now("t"))
                    dve.scalar_tensor_tensor(ot[:, :], ot[:, :], 1.0, oh[:, :], ALU.add, ALU.mult
                                             ).then_inc(sem("gelu_arg"), 1)
                if r == 3:
                    dve.wait_ge(sem("gelu_tanh"), now("t"))
                    dve.scalar_tensor_tensor(oh[:, :], otanh[:, :], 1.0, oh[:, :], ALU.add, ALU.mult
                                             ).then_inc(sem("gelu_done"), 1)
                if r == 4:
                    pv = px[:, :, :].rearrange("p n a -> p (n a)")
                    cv = corner[:, :, :].rearrange("p n a -> p (n a)")
                    dve.wait_ge(made("off2"), now("off2"))
                    dve.scalar_tensor_tensor(pv, bank_of["off2"][:, 0:128], 2.0,
                                             refb[:, :, :, :].rearrange("p n m a -> p (n m a)"),
                                             ALU.mult, ALU.add).then_inc(read("off2"), 1)
                    dve.wait_ge(read("off2"), now("off2"))
                    link(dve.tensor_scalar(pv, pv, 0.0, float(W - 1), ALU.max, ALU.min))
                    link(dve.tensor_scalar(cv, pv, ROUND - 0.5, ROUND, ALU.add, ALU.subtract))
                    link(dve.tensor_scalar(cv, cv, 0.0, float(W - 2), ALU.max, ALU.min))
                    f1 = frac[:, 1, :, :].rearrange("p n a -> p (n a)")
                    link(dve.tensor_tensor(f1, pv, cv, ALU.subtract))
                    link(dve.tensor_scalar(frac[:, 0, :, :].rearrange("p n a -> p (n a)"), f1, -1.0, 1.0,
                                           ALU.mult, ALU.add))
                    for dx in range(2):
                        step(dve.tensor_tensor(wts_next[:, :, dx, :].rearrange("p n b -> p b n"),
                                               frac[:, dx:dx + 1, :, 0].broadcast_to([P, 2, CHUNKS * POINTS]),
                                               frac[:, :, :, 1], ALU.mult))
                    step(dve.scalar_tensor_tensor(row_next[:, :], corner[:, :, 1], float(W), corner[:, :, 0],
                                                  ALU.mult, ALU.add))

            def rows_live(half, now):
                cols = slice(half * 32, half * 32 + 32)
                dve.tensor_scalar(row[:, cols], row_next[:, cols], row_base[:, 0:1], None, ALU.add
                                  ).then_inc((rows_a, rows_b)[half], 1)

            def mlp_round(r, now, slot_ap):
                if r == 1:
                    link(dve.tensor_reduce(stat[:, 0, :], chunked(slot_ap), AX, ALU.add))
                    dve.tensor_scalar(stat[:, 1, :], stat[:, 0, :], -1.0 / C, None, ALU.mult).then_inc(sem("mean_done"), 1)
                if r == 5:
                    dve.wait_ge(sem("sg1_done"), now("z1"))
                    dve.scalar_tensor_tensor(T["s1"][:, :], bank_of["z1"][:, :], par("par")[:, 2 * C:2 * C + 1],
                                             T["sg1"][:, :], ALU.add, ALU.mult).then_inc(read("z1"), 1)
                    dve.wait_ge(read("z1"), now("z1"))
                    link(dve.scalar_tensor_tensor(T["d1"][:, :], T["s1"][:, :], 1.0, T["sg1"][:, :],
                                                  ALU.subtract, ALU.mult))
                    step(dve.tensor_tensor(T["d1"][:, :], T["s1"][:, :], T["d1"][:, :], ALU.subtract))
                    dve.wait_ge(made("v"), now("v"))
                    dve.tensor_tensor(T["res"][:, :], T["s1"][:, :], bank_of["v"][:, :], ALU.subtract
                                      ).then_inc(read("v"), 1)
                if r == 6:
                    dve.wait_ge(sem("sg2_done"), now("z2"))
                    dve.scalar_tensor_tensor(T["s2"][:, :], bank_of["z2"][:, :], par("par")[:, 2 * C + 1:2 * C + 2],
                                             T["sg2"][:, :], ALU.add, ALU.mult).then_inc(read("z2"), 1)
                    dve.wait_ge(read("z2"), now("z2"))
                    dve.wait_ge(read("v"), now("v"))
                    step(dve.scalar_tensor_tensor(T["d2"][:, :], T["s2"][:, :], 1.0, T["sg2"][:, :],
                                                  ALU.subtract, ALU.mult))
                    step(dve.tensor_tensor(T["res"][:, :], T["res"][:, :], T["s2"][:, :], ALU.add))
                    dve.wait_ge(read("lr"), now("lr"))
                    step(dve.scalar_tensor_tensor(T["dp"][:, :], T["lr"][:, :], 1.0, par("lossw"), ALU.add, ALU.mult))
                    sync()
                    step(dve.tensor_tensor(T["d2"][:, :], T["s2"][:, :], T["d2"][:, :], ALU.subtract))
                    step(dve.tensor_tensor(T["dp"][:, :], T["dp"][:, :], T["res"][:, :], ALU.mult))
                    sync()
                    dve.tensor_tensor(T["dz2"][:, :], T["dp"][:, :], T["d2"][:, :], ALU.mult).then_inc(sem("dz2_done"), 1)
                if r == 7:
                    dve.wait_ge(made("dk"), now("dk"))
                    dve.tensor_tensor(T["dp"][:, :], T["dp"][:, :], bank_of["dk"][:, :], ALU.add
                                      ).then_inc(read("dk"), 1)
                    dve.wait_ge(read("dk"), now("dk"))
                    dve.tensor_tensor(T["dz1"][:, :], T["dp"][:, :], T["d1"][:, :], ALU.mult).then_inc(sem("dz1_done"), 1)

            def scores_and_attention(r, base, dst):
                c, a = (r - 1) % CHUNKS, (r - 2) % CHUNKS
                sc, pr = score[:, c % 2, :, :], prob[:, a % 2, :, :]
                if r <= CHUNKS:
                    dve.wait_ge(kv_made, base + r)
                    dve.tensor_tensor(qk[:, :].rearrange("p (n c) -> p n c", n=POINTS),
                                      b_k[:, :].rearrange("p (n c) -> p n c", n=POINTS),
                                      qry[:, c * C:(c + 1) * C].unsqueeze(1).broadcast_to([P, POINTS, C]), ALU.mult
                                      ).then_inc(keys_read, 1)
                dve.wait_ge(exped, base + (r - 1))
                total = step(dve.tensor_reduce(ha[:, 1, :], pr.rearrange("p n h -> p h n"), AX, ALU.add))
                weighed_values = step(dve.tensor_tensor(
                    av[:, :].rearrange("p (m d) -> p m d", d=DH),
                    b_v[a % 2][:, :].rearrange("p (m d) -> p m d", d=DH),
                    bc(pr.rearrange("p n h -> p (n h)"), DH), ALU.mult))
                if r <= CHUNKS:
                    dve.wait_ge(keys_read, base + r)
                    raw = step(dve.tensor_reduce(sc.rearrange("p n h -> p (n h)"),
                                                 qk[:, :].rearrange("p (m d) -> p m d", d=DH), AX, ALU.add))
                dve.wait_ge(s_dve, total)
                step(dve.reciprocal(ha[:, 2, :], ha[:, 1, :]))
                dve.wait_ge(s_dve, weighed_values)
                summed_values = step(dve.tensor_reduce(ho[:, :], av[:, :].rearrange("p (n c) -> p c n", n=POINTS),
                                                       AX, ALU.add))
                if r <= CHUNKS:
                    dve.wait_ge(s_dve, raw)
                    largest = step(dve.tensor_reduce(ha[:, 0, :], sc.rearrange("p n h -> p h n"), AX, ALU.max))
                dve.wait_ge(s_dve, summed_values)
                dve.tensor_tensor(dst[:, a * C:(a + 1) * C].rearrange("p (h d) -> p h d", d=DH),
                                  ho[:, :].rearrange("p (h d) -> p h d", d=DH),
                                  bc(ha[:, 2, :], DH), ALU.mult).then_inc(attended, 1)
                if r <= CHUNKS:
                    dve.wait_ge(s_dve, largest)
                    dve.tensor_tensor(sc, sc, ha[:, 0:1, :].broadcast_to([P, POINTS, HEADS]), ALU.subtract
                                      ).then_inc(scored, 1)

            first = lambda name: PRIME + 1
            dve.memset(ones[:, :], 1.0).then_inc(sem("ones_set"), 1)
            step(dve.memset(row_base[:, :], 0.0))
            for name in ("k1t", "dz2t", "dz1t", "u"):
                step(dve.memset(T[name][:, :], 0.0))
            for tile in (b_k, b_v[0], b_v[1], qry, h_all[:, 0, :]):
                step(dve.memset(tile[:, :], 0.0))
            step(dve.memset(prob[:, :, :, :], 1.0))
            step(dve.memset(var[:, :, :], 1.0))
            dve.wait_ge(txt_in, 16)
            sync()
            dve.scalar_tensor_tensor(txt_row[:, :], txt_i[:, 0:TXT_CHUNKS], float(TXT_ROWS),
                                     txt_i[:, TXT_CHUNKS:2 * TXT_CHUNKS], ALU.mult, ALU.add).then_inc(rows_txt, 1)
            dve.wait_ge(params_in, 16)
            for name, n in (("wo1", 2), ("bo1", CHUNKS)):
                w = par(name).rearrange("p (n k) -> p n k", n=n)
                link(dve.tensor_reduce(stat[:, 0, 0:n], w, AX, ALU.add))
                link(dve.tensor_scalar(stat[:, 0, 0:n], stat[:, 0, 0:n], -1.0 / HID, None, ALU.mult))
                link(dve.tensor_tensor(w, w, bc(stat[:, 0, 0:n], HID), ALU.add))
            dve.sem_inc(sem("weights_ready"), 1)
            sync()
            dve.wait_ge(ref_in, 16)
            weigh_reference(first)
            bo2 = par("bo2").rearrange("p (n m a) -> p n m a", n=CHUNKS, a=2)
            refpx = par("refpx").rearrange("p (n a) -> p n a", a=2)
            for n in range(CHUNKS):
                step(dve.scalar_tensor_tensor(refb[:, n, :, :], bo2[:, n, :, :], 4.0,
                                              refpx[:, n:n + 1, :].broadcast_to([P, POINTS, 2]), ALU.mult, ALU.add))
            for r in (2, "gelu_arg", 3, 4):
                points_round(r, first, None)
            sync()
            rows_live(0, None)
            rows_live(1, None)
            dve.wait_ge(rows_b, PRIME + 1)
            link(dve.tensor_scalar(row_base[:, :], row_base[:, :], float(H * W), None, ALU.add))
            step(dve.tensor_copy(wts[:, :, :].rearrange("p n k -> p (n k)"),
                                 wts_next[:, :, :, :].rearrange("p n a b -> p (n a b)")))
            dve.wait_ge(late_in, 16)
            step(dve.tensor_tensor(mvk[:, :], par("mv"), par("mk"), ALU.subtract))
            step(dve.tensor_scalar(txt_cat[:, :, C + TYPE_DIM], par("outc"), par("txts")[:, 0:1], None, ALU.mult))
            step(dve.tensor_scalar(txt_cat[:, :, C + TYPE_DIM + 1], par("dt"), par("txts")[:, 1:2], None, ALU.mult))
            sync()
            dve.memset(txt_cat[:, :, CAT - 1:CAT], 1.0).then_inc(sem("txt_cat_done"), 1)
            nt = TXT_CHUNKS
            tx = T["res"][:, 0:nt * C].rearrange("p (n c) -> p n c", n=nt)
            ty = T["sq"][:, 0:nt * C].rearrange("p (n c) -> p n c", n=nt)
            proj = b_aux[0][:, 0:nt * C].rearrange("p (n c) -> p n c", n=nt)
            dve.wait_ge(made("txt_p"), 1)
            link(dve.tensor_reduce(stat[:, 0, 0:nt], proj, AX, ALU.add))
            link(dve.tensor_scalar(stat[:, 1, 0:nt], stat[:, 0, 0:nt], -1.0 / C, None, ALU.mult))
            dve.tensor_tensor(tx, proj, bc(stat[:, 1, 0:nt], C), ALU.add).then_inc(read("txt_p"), 1)
            dve.wait_ge(read("txt_p"), 1)
            link(dve.tensor_tensor(ty, tx, tx, ALU.mult))
            link(dve.tensor_reduce(var[:, 0, 0:nt], ty, AX, ALU.add))
            link(dve.tensor_scalar(var[:, 0, :], var[:, 0, :], 1.0 / C, LN_EPS, ALU.mult, ALU.add))
            rsqrt()
            link(dve.tensor_tensor(tx, tx, bc(rstd[:, 0, 0:nt], C), ALU.mult))
            link(dve.tensor_tensor(tx, tx, par("txtg").unsqueeze(1).broadcast_to([P, nt, C]), ALU.mult))
            link(dve.tensor_tensor(h_all[:, 0, 0:nt * C].rearrange("p (n c) -> p n c", n=nt), tx,
                                   par("txtb").unsqueeze(1).broadcast_to([P, nt, C]), ALU.add))

            with dve.Fori(0, IMAGES) as i:
                dve.sem_clear(s_dve)
                steps[0] = 0
                ahead = AUX_Q + ["t", "a", "g", "ref"]
                now = lambda name: i + (PRIME + (2 if name in ahead else 1))
                slot = lambda k: h_all[:, bass.ds(k, 1), :].rearrange("p a n -> p (a n)")

                def weigh(c):
                    if c < RING:
                        dve.wait_ge(gathered[c], i * (2 * 16 * POINTS) + 16 * POINTS)
                    else:
                        dve.wait_ge(gathered[c % RING], i * (2 * 16 * POINTS) + 2 * 16 * POINTS)
                    dve.wait_ge(summed, i * CHUNKS + (PRIME + c - 1))
                    dve.tensor_tensor(gathw[:, c % 2, :, :].rearrange("p k (n c) -> p n k c", n=POINTS),
                                      gath[:, c % RING, :, :].rearrange("p n (k c) -> p n k c", k=4),
                                      bc(wts[:, c, :].rearrange("p (n k) -> p n k", k=4), C), ALU.mult
                                      ).then_inc(weighed, 1)

                for r in range(CHUNKS):
                    weigh(r)
                    if r == 3:
                        points_round("gelu_arg", now, None)
                    if r == 1:
                        dve.wait_ge(qry_moved, i + (PRIME + 1))
                    scores_and_attention(r, i * CHUNKS + PRIME, slot(i) if r < 2 else slot(i + 1))
                    if r == 0:
                        dve.wait_ge(ref_in, i * 16 + 32)
                        dve.wait_ge(made("qf"), i + (PRIME + 1))
                        weigh_reference(now)
                    if r == 1:
                        dve.wait_ge(attended, i * CHUNKS + PRIME)
                    if r < 7:
                        mlp_round(r, now, slot(i))
                    points_round(r, now, i + (PRIME + 1))
                    if r == 4:
                        dve.wait_ge(issued_a, i + (PRIME + 1))
                        sync()
                        rows_live(0, now)
                    if r == 7:
                        step(dve.tensor_copy(wts[:, :, :].rearrange("p n k -> p (n k)"),
                                             wts_next[:, :, :, :].rearrange("p n a b -> p (n a b)")))
                        dve.wait_ge(issued_b, i + (PRIME + 1))
                        rows_live(1, now)
                        dve.wait_ge(rows_b, i + (PRIME + 2))
                        step(dve.tensor_scalar(row_base[:, :], row_base[:, :], float(H * W), None, ALU.add))
                        mlp_round(r, now, slot(i))
                sync()
            dve.sem_clear(s_dve)
            steps[0] = 0
            for r in range(CHUNKS, CHUNKS + 2):
                scores_and_attention(r, (IMAGES - 1) * CHUNKS + PRIME, h_all[:, IMAGES, :])
            dve.wait_ge(attended, IMAGES * CHUNKS + PRIME)
            last_now = lambda name: PRIME + IMAGES + 1
            link(dve.tensor_reduce(stat[:, 0, :], chunked(h_all[:, IMAGES, :]), AX, ALU.add))
            link(dve.tensor_scalar(stat[:, 1, :], stat[:, 0, :], -1.0 / C, None, ALU.mult))
            dve.wait_ge(sem("grads_added"), PRIME + IMAGES)
            dve.tensor_tensor(chunked(T["u"][:, :]), chunked(h_all[:, IMAGES, :]), bc(stat[:, 1, :], C), ALU.add
                              ).then_inc(sem("mean_done"), 1)
            dve.wait_ge(sem("var_done"), PRIME + IMAGES + 1)
            link(dve.tensor_reduce(var[:, 0, :], chunked(T["sq"][:, :]), AX, ALU.add))
            link(dve.tensor_scalar(var[:, 0, :], var[:, 0, :], 1.0 / C, LN_EPS, ALU.mult, ALU.add))
            rsqrt()
            dve.tensor_tensor(chunked(T["u"][:, :]), chunked(T["u"][:, :]), bc(rstd[:, 0, :], C), ALU.mult
                              ).then_inc(sem("normed"), 1)
            for r in range(5, 8):
                mlp_round(r, last_now, h_all[:, IMAGES, :])
            phase23_vector(dve, steps, step, sync, link, bc, chunked, rsqrt_of)


def blocks(ms):
    out = np.zeros((sum(m.shape[0] for m in ms), sum(m.shape[1] for m in ms)), np.float32)
    r = c = 0
    for m in ms:
        out[r:r + m.shape[0], c:c + m.shape[1]] = m
        r, c = r + m.shape[0], c + m.shape[1]
    return out


def kernel(**inputs):
    import concourse.bacc as _bacc
    from concourse.bass_utils import run_bass_kernel_spmd as _run

    a = {k: np.asarray(v) for k, v in inputs.items()}
    tok = {k[7:]: v for k, v in a.items() if k.startswith("L0_tok_")}
    txt = {k[7:]: v for k, v in a.items() if k.startswith("L0_txt_")}
    mem = {k[8:]: v for k, v in a.items() if k.startswith("L0_attn_")}
    ffn = {k[7:]: v for k, v in a.items() if k.startswith("L0_ffn_")}

    def rows(v, n=P):
        return np.broadcast_to(v.reshape(1, -1), (n, v.size))

    def pack(entries, parts):
        where, total = columns(entries)
        out = np.zeros((P, total), np.float32)
        for name, m in parts.items():
            at, n = where[name]
            assert m.shape[1] == n, (name, m.shape, n)
            out[:m.shape[0], at:at + n] = m
        return out

    x = a["x"].transpose(0, 2, 3, 1)
    below = np.concatenate([x[:, 1:], np.zeros_like(x[:, :1])], axis=1)
    x_pairs = np.ascontiguousarray(np.stack([x, below], axis=3)).reshape(IMAGES * H * W, 2 * C)

    n = np.arange(P * CHUNKS).reshape(P, CHUNKS)
    grid = (np.linspace(-1.0, 1.0, GRID).astype(np.float32) + np.float32(1)) * np.float32(0.5) * np.float32(W - 1)
    rx, ry = grid[n % GRID], grid[n // GRID]
    x0 = np.clip(np.floor(rx), 0, W - 2).astype(np.int64)
    y0 = np.clip(np.floor(ry), 0, H - 2).astype(np.int64)
    fx, fy = rx - x0, ry - y0
    refw = np.stack([wx * wy for wx in (1 - fx, fx) for wy in (1 - fy, fy)], axis=1)
    corners = np.stack([x[:, y0 + dy, x0 + dx] for dx in (0, 1) for dy in (0, 1)], axis=2)
    x_ref = np.concatenate([corners, np.zeros_like(corners[:1])]).reshape(IMAGES + 1, P, 4 * COLS)

    eye = np.eye(P, dtype=np.float32)
    early = pack(EARLY, {
        "ident": eye, "wq2": blocks([tok["W_q"].T] * 2), "wo1": blocks([tok["W_o1"]] * 2),
        "wo2": blocks([tok["W_o2"]] * CHUNKS), "wk2": blocks([tok["W_k"].T] * 2), "wv2": blocks([tok["W_v"].T] * 2),
        "bo1": rows(np.tile(tok["b_o1"], CHUNKS)), "lng": rows(np.tile(tok["ln_g"], CHUNKS)),
        "lnb": rows(np.tile(tok["ln_b"], CHUNKS)), "bo2": rows(np.tile(tok["b_o2"], CHUNKS)),
        "refw": refw.reshape(P, 32), "refpx": np.stack([rx, ry], axis=2).reshape(P, 16)})

    def per_token(v):
        flat = v.reshape(-1)
        return np.concatenate([flat, np.zeros(P * TXT_CHUNKS - flat.size, flat.dtype)]).reshape(P, TXT_CHUNKS)

    chunk = np.arange(CHUNKS)[None]
    live = (chunk < TXT_CHUNKS) & (np.arange(P)[:, None] * TXT_CHUNKS + chunk < TXT_B * TXT_L)
    live = live.reshape(P, PAIRS, 2).transpose(2, 1, 0).reshape(2, 1, COLS)
    lossw = np.broadcast_to(live, (2, C, COLS)).reshape(P, COLS) * np.float32(MAX_ALR / C)
    half = np.kron(np.eye(2), np.ones((C, C)))
    experts = range(EPAIRS)
    sel = np.zeros((18, EPAIRS * P), np.float32)
    for p in experts:
        for e in range(2):
            sel[[2 * p + e, 6 + 2 * p + e, 12 + 2 * p + e], p * P + e * C:p * P + (e + 1) * C] = 1
    w1, w2, w3 = ffn["expert_w1"], ffn["expert_w2"], ffn["expert_w3"]
    col = lambda v: v.reshape(-1, 1)
    late = pack(LATE, {
        "mk": blocks([mem["Wk"]] * 2), "mv": blocks([mem["Wv"]] * 2), "mq": blocks([mem["Wq"]] * 2),
        "mlr": blocks([np.broadcast_to(mem["Wlr"], (C, C))] * 2),
        "mw1": blocks([mem["Ws"][0]] * 2), "mw2": blocks([mem["Ws"][1]] * 2), "mw2t": blocks([mem["Ws"][1].T] * 2),
        "mkrep": np.tile(mem["Wk"], (1, 2)),
        "par": np.tile(np.concatenate([mem["Ws"][0], mem["Ws"][1], col(mem["bs"][0]), col(mem["bs"][1])], axis=1), (2, 1)),
        "blr": rows(mem["blr"]), "stack": np.tile(np.eye(C, dtype=np.float32), (2, 2)),
        "gmask": np.tile(half.astype(np.float32), (1, 2)), "lossw": lossw,
        "rw1": blocks([ffn["router_w1"]] * 2), "rb1": col(np.tile(ffn["router_b1"], 2)),
        "rw2": blocks([ffn["router_w2"]] * 2), "rb2": rows(np.tile(ffn["router_b2"], CHUNKS)),
        "first": rows(np.tile(np.arange(EXPERTS, 0, -1).astype(np.float32), CHUNKS)),
        "ew1": np.tile(np.concatenate([w1[e] for e in range(EXPERTS)], axis=1), (2, 1)),
        "eb1": ffn["expert_b1"].reshape(EPAIRS, P).T,
        "ew2": np.concatenate([blocks([w2[2 * p], w2[2 * p + 1]]) for p in experts], axis=1),
        "eb2": ffn["expert_b2"].reshape(EPAIRS, P).T,
        "ew3": np.concatenate([w3[2 * p:2 * p + 2].reshape(P, C) for p in experts], axis=1),
        "eb3": blocks([ffn["expert_b3"]] * CHUNKS), "sel": sel,
        "txtw": np.concatenate([txt["W_proj_w"].T, txt["W_proj_b"].reshape(1, C)]),
        "txtg": rows(txt["ln_gamma"]), "txtb": rows(txt["ln_beta"]),
        "txts": rows(np.concatenate([txt["W_o"], txt["W_delta"]])),
        "outc": per_token(a["fside_BS_outcomes"]), "dt": per_token(a["fside_BS_delta_ts"])})
    txt_idx = np.concatenate([per_token(a["x_txt"].astype(np.int32)),
                              per_token(a["itok_BS_0_4999"].astype(np.int32))], axis=1)
    pad = lambda h: np.concatenate([h, np.zeros((TXT_ROWS - h.shape[0], C), np.float32)])
    table = np.concatenate([pad(txt["h_qa"]), pad(txt["h_v"]), pad(txt["h_r"])])

    arrays = {"x_pairs": x_pairs, "x_ref": x_ref, "early": early, "late": late, "txt_idx": txt_idx,
              "txt_table": table, "type_table": np.ascontiguousarray(txt["E_type_w"])}
    nc = _bacc.Bacc("TRN2", target_bir_lowering=False, num_devices=1)
    args = [nc.dram_tensor(k, v.shape, mybir.dt.from_np(v.dtype), kind="ExternalInput").ap() for k, v in arrays.items()]
    args.append(nc.dram_tensor("tokens_out", (SLOTS, P, COLS), F32, kind="ExternalOutput").ap())
    build(nc, *args)
    got = _run(nc, [arrays], core_ids=[0]).results[0]["tokens_out"]
    image = got[1:].reshape(IMAGES, P * CHUNKS, C)
    text = got[0][:, :TXT_CHUNKS * C].reshape(P * TXT_CHUNKS, C)[:TXT_B * TXT_L].reshape(TXT_B, TXT_L, C)
    return np.concatenate([image, text], axis=1)
```
